# Optimizing a Trainium2 kernel written in Bass

```python
import numpy as np
import jax
import jax.numpy as jnp

def _softmax(x, axis=-1):
    return jax.nn.softmax(x, axis=axis)

def _gelu(x):
    return jax.nn.gelu(x, approximate=True)

def _silu(x):
    return jax.nn.silu(x)

def _sigmoid(x):
    return jax.nn.sigmoid(x)

def _layernorm(x, axis=-1, eps=1e-05):
    m = jnp.mean(x, axis=axis, keepdims=True)
    v = jnp.var(x, axis=axis, keepdims=True)
    return (x - m) / jnp.sqrt(v + eps)

def _scatter_add(tgt, idx, src, axis=0):
    return tgt.at[idx].add(src)

def _segment_sum(src, seg, n):
    return jax.ops.segment_sum(src, seg, n)
kernel_name = 'mk_xattn_ffn_d2_seqx_r4_f005d8'

def setup_inputs(seed: int=0):
    np.random.seed(seed)
    _w = jnp.asarray

    def _rec_inputs():
        import jax
        import jax.numpy as jnp
        _rk = jax.random.key(seed)
        x = -0.0003929 + 0.9999 * jax.random.normal(jax.random.fold_in(_rk, 1), (4, 512, 512), jnp.float32)
        _lenS = 512 - jax.random.randint(jax.random.fold_in(_rk, 7), (4,), 0, max(1, 512 // 4) + 1, jnp.int32)
        _lenS2 = 512 - jax.random.randint(jax.random.fold_in(_rk, 8), (4,), 0, max(1, 512 // 4) + 1, jnp.int32)
        _ctx_1024P = jax.random.normal(jax.random.fold_in(_rk, 11), (4, 16, 256), jnp.float32)
        _ctx_1024c = jax.random.dirichlet(jax.random.fold_in(_rk, 511), 0.3 * jnp.ones((16,), jnp.float32), (4, 512))
        _ctx_1024t = jnp.einsum('bsk,bkd->bsd', _ctx_1024c, _ctx_1024P)
        _ctx_1024t = _ctx_1024t * jax.lax.rsqrt(jnp.mean(jnp.square(_ctx_1024t)) + 1e-12) * 0.953939
        ctx_1024 = 0.000227908 + 0.99994 * (_ctx_1024t + 0.3 * jax.random.normal(jax.random.fold_in(_rk, 611), (4, 512, 256), jnp.float32))
        return (x, ctx_1024)
    x, ctx_1024 = _rec_inputs()

    def _L0_xattn_setup():
        import jax, jax.numpy as jnp
        import numpy as np
        EPS = 1e-05

        def rmsnorm(x, g, eps=EPS):
            var = jnp.mean(jnp.square(x), axis=-1, keepdims=True)
            return x * jax.lax.rsqrt(var + eps) * g
        key = jax.random.key(seed)
        ks = jax.random.split(key, 8)
        B, Sq, Skv = (2, 1024, 128)
        dim, cdim, H, D = (512, 256, 16, 128)
        inner = H * D
        s = lambda f: 1.0 / np.sqrt(f)
        return {'hidden_states': jax.random.normal(ks[0], (B, Sq, dim), jnp.float32), 'encoder_hidden_states': jax.random.normal(ks[1], (B, Skv, cdim), jnp.float32), 'Wq': jax.random.normal(ks[2], (dim, inner), jnp.float32) * s(dim), 'Wk': jax.random.normal(ks[3], (cdim, inner), jnp.float32) * s(cdim), 'Wv': jax.random.normal(ks[4], (cdim, inner), jnp.float32) * s(cdim), 'Wo': jax.random.normal(ks[5], (inner, dim), jnp.float32) * s(inner), 'gq': jnp.ones((D,), jnp.float32), 'gk': jnp.ones((D,), jnp.float32)}
    _L0_xattn_all = _L0_xattn_setup()
    _L0_xattn_in = {k: v for k, v in _L0_xattn_all.items() if k in ('Wq', 'Wk', 'Wv', 'Wo', 'gq', 'gk')}
    del _L0_xattn_all

    def _L0_ffn_setup():
        import jax, jax.numpy as jnp
        import numpy as np
        HIDDEN = 512
        INTER = 2048
        SCALE = 64.0

        def fwht(x):
            orig_shape = x.shape
            n = orig_shape[-1]
            x = x.reshape(-1, n)
            h = 1
            while h < n:
                x = x.reshape(-1, n // (2 * h), 2, h)
                a, b = (x[:, :, 0, :], x[:, :, 1, :])
                x = jnp.stack([a + b, a - b], axis=2).reshape(-1, n)
                h *= 2
            return (x / jnp.sqrt(jnp.asarray(n, x.dtype))).reshape(orig_shape)
        key = jax.random.key(seed)
        ks = jax.random.split(key, 8)
        inp = jax.random.normal(ks[0], (4, 512, HIDDEN), dtype=jnp.float32)
        SU_ug = jnp.where(jax.random.bernoulli(ks[1], 0.5, (HIDDEN,)), 1.0, -1.0).astype(jnp.float32)
        SU_dp = jnp.where(jax.random.bernoulli(ks[2], 0.5, (INTER,)), 1.0, -1.0).astype(jnp.float32)
        Wscale_ug = jax.random.uniform(ks[3], (2 * INTER,), jnp.float32, 0.5, 1.5)
        Wscale_dp = jax.random.uniform(ks[4], (HIDDEN,), jnp.float32, 0.5, 1.5)
        W_up = jax.random.normal(ks[5], (INTER, HIDDEN), dtype=jnp.float32) * 0.02
        W_gate = jax.random.normal(ks[6], (INTER, HIDDEN), dtype=jnp.float32) * 0.02
        W_down = jax.random.normal(ks[7], (HIDDEN, INTER), dtype=jnp.float32) * 0.02
        return {'input': inp, 'SU_ug': SU_ug, 'SU_dp': SU_dp, 'Wscale_ug': Wscale_ug, 'Wscale_dp': Wscale_dp, 'W_up': W_up, 'W_gate': W_gate, 'W_down': W_down}
    _L0_ffn_all = _L0_ffn_setup()
    _L0_ffn_in = {k: v for k, v in _L0_ffn_all.items() if k in ('SU_ug', 'SU_dp', 'Wscale_ug', 'Wscale_dp', 'W_up', 'W_gate', 'W_down')}
    del _L0_ffn_all

    def _L1_xattn_setup():
        import jax, jax.numpy as jnp
        import numpy as np
        import math
        B, L, DM = (2, 512, 256)
        DS, DC, EXP = (16, 4, 2)
        DI = EXP * DM
        DR = math.ceil(DM / 16)
        DT_MIN, DT_MAX, DT_FLOOR = (0.001, 0.1, 0.0001)

        def _ssm_forward(hidden_states, z, in_proj_w, conv_w, conv_b, x_proj_w, dt_proj_w, dt_proj_b, A_log, D):
            b = hidden_states.shape[0]
            x = jnp.einsum('ed,bld->bel', in_proj_w, hidden_states)
            xp = jnp.pad(x, ((0, 0), (0, 0), (DC - 1, 0)))
            xc = jax.lax.conv_general_dilated(xp, conv_w[:, None, :], window_strides=(1,), padding='VALID', dimension_numbers=('NCH', 'OIH', 'NCH'), feature_group_count=DI)
            u = jax.nn.silu(xc + conv_b[None, :, None])
            x_dbl = jnp.einsum('ke,bel->bkl', x_proj_w, u)
            dt_lo = x_dbl[:, :DR]
            Bm = x_dbl[:, DR:DR + DS]
            Cm = x_dbl[:, DR + DS:]
            delta = jax.nn.softplus(jnp.einsum('er,brl->bel', dt_proj_w, dt_lo) + dt_proj_b[None, :, None])
            A = -jnp.exp(A_log)

            def step(state, xs):
                d_t, B_t, C_t, u_t = xs
                dA = jnp.exp(d_t[..., None] * A)
                state = state * dA + (d_t * u_t)[..., None] * B_t[:, None, :]
                y_t = jnp.einsum('ben,bn->be', state, C_t)
                return (state, y_t)
            xs = (jnp.moveaxis(delta, -1, 0), jnp.moveaxis(Bm, -1, 0), jnp.moveaxis(Cm, -1, 0), jnp.moveaxis(u, -1, 0))
            state0 = jnp.zeros((b, DI, DS), delta.dtype)
            _, ys = jax.lax.scan(step, state0, xs)
            y = jnp.moveaxis(ys, 0, -1)
            y = y + D[None, :, None] * u
            y = y * jax.nn.silu(z)
            return jnp.swapaxes(y, 1, 2)
        key = jax.random.key(seed)
        ks = jax.random.split(key, 8)
        hidden_states = jax.random.normal(ks[0], (B, L, DM), jnp.float32)
        z = jax.random.normal(ks[1], (B, DI, L), jnp.float32)
        in_proj_w = jax.random.normal(ks[2], (DI, DM), jnp.float32) * DM ** (-0.5)
        conv_w = jax.random.normal(ks[3], (DI, DC), jnp.float32) * DC ** (-0.5)
        conv_b = jnp.zeros((DI,), jnp.float32)
        x_proj_w = jax.random.normal(ks[4], (DR + 2 * DS, DI), jnp.float32) * DI ** (-0.5)
        dt_std = DR ** (-0.5)
        dt_proj_w = jax.random.uniform(ks[5], (DI, DR), jnp.float32, -dt_std, dt_std)
        dt = jnp.exp(jax.random.uniform(ks[6], (DI,), jnp.float32) * (math.log(DT_MAX) - math.log(DT_MIN)) + math.log(DT_MIN))
        dt = jnp.clip(dt, DT_FLOOR)
        dt_proj_b = dt + jnp.log(-jnp.expm1(-dt))
        A_log = jnp.log(jnp.broadcast_to(jnp.arange(1, DS + 1, dtype=jnp.float32), (DI, DS)))
        D = jnp.ones((DI,), jnp.float32)
        return dict(hidden_states=hidden_states, z=z, in_proj_w=in_proj_w, conv_w=conv_w, conv_b=conv_b, x_proj_w=x_proj_w, dt_proj_w=dt_proj_w, dt_proj_b=dt_proj_b, A_log=A_log, D=D)
    _L1_xattn_all = _L1_xattn_setup()
    _L1_xattn_in = {k: v for k, v in _L1_xattn_all.items() if k in ('in_proj_w', 'conv_w', 'conv_b', 'x_proj_w', 'dt_proj_w', 'dt_proj_b', 'A_log', 'D')}
    del _L1_xattn_all

    def _L1_ffn_setup():
        import jax, jax.numpy as jnp
        import numpy as np
        TOPK = 2
        NORM_TOPK = True
        SCALE = 1.0
        EPS = 1e-09
        key = jax.random.key(seed)
        ks = jax.random.split(key, 9)
        h, i, E = (512, 256, 16)
        std = 0.02
        return {'x': jax.random.normal(ks[0], (1, 512, h), jnp.float32), 'Wr': jax.random.normal(ks[1], (E, h), jnp.float32) * std, 'bias': jnp.zeros((E,), jnp.float32), 'Wg': jax.random.normal(ks[2], (E, h, i), jnp.float32) * std, 'Wu': jax.random.normal(ks[3], (E, h, i), jnp.float32) * std, 'Wd': jax.random.normal(ks[4], (E, i, h), jnp.float32) * std, 'sWg': jax.random.normal(ks[5], (h, i), jnp.float32) * std, 'sWu': jax.random.normal(ks[6], (h, i), jnp.float32) * std, 'sWd': jax.random.normal(ks[7], (i, h), jnp.float32) * std}
    _L1_ffn_all = _L1_ffn_setup()
    _L1_ffn_in = {k: v for k, v in _L1_ffn_all.items() if k in ('Wr', 'bias', 'Wg', 'Wu', 'Wd', 'sWg', 'sWu', 'sWd')}
    del _L1_ffn_all
    return {'x': x, 'ctx_1024': ctx_1024, 'L0_xattn_Wq': _L0_xattn_in['Wq'], 'L0_xattn_Wk': _L0_xattn_in['Wk'], 'L0_xattn_Wv': _L0_xattn_in['Wv'], 'L0_xattn_Wo': _L0_xattn_in['Wo'], 'L0_xattn_gq': _L0_xattn_in['gq'], 'L0_xattn_gk': _L0_xattn_in['gk'], 'L0_ffn_SU_ug': _L0_ffn_in['SU_ug'], 'L0_ffn_SU_dp': _L0_ffn_in['SU_dp'], 'L0_ffn_Wscale_ug': _L0_ffn_in['Wscale_ug'], 'L0_ffn_Wscale_dp': _L0_ffn_in['Wscale_dp'], 'L0_ffn_W_up': _L0_ffn_in['W_up'], 'L0_ffn_W_gate': _L0_ffn_in['W_gate'], 'L0_ffn_W_down': _L0_ffn_in['W_down'], 'L1_xattn_in_proj_w': _L1_xattn_in['in_proj_w'], 'L1_xattn_conv_w': _L1_xattn_in['conv_w'], 'L1_xattn_conv_b': _L1_xattn_in['conv_b'], 'L1_xattn_x_proj_w': _L1_xattn_in['x_proj_w'], 'L1_xattn_dt_proj_w': _L1_xattn_in['dt_proj_w'], 'L1_xattn_dt_proj_b': _L1_xattn_in['dt_proj_b'], 'L1_xattn_A_log': _L1_xattn_in['A_log'], 'L1_xattn_D': _L1_xattn_in['D'], 'L1_ffn_Wr': _L1_ffn_in['Wr'], 'L1_ffn_bias': _L1_ffn_in['bias'], 'L1_ffn_Wg': _L1_ffn_in['Wg'], 'L1_ffn_Wu': _L1_ffn_in['Wu'], 'L1_ffn_Wd': _L1_ffn_in['Wd'], 'L1_ffn_sWg': _L1_ffn_in['sWg'], 'L1_ffn_sWu': _L1_ffn_in['sWu'], 'L1_ffn_sWd': _L1_ffn_in['sWd']}

def reference(x, ctx_1024, L0_xattn_Wq, L0_xattn_Wk, L0_xattn_Wv, L0_xattn_Wo, L0_xattn_gq, L0_xattn_gk, L0_ffn_SU_ug, L0_ffn_SU_dp, L0_ffn_Wscale_ug, L0_ffn_Wscale_dp, L0_ffn_W_up, L0_ffn_W_gate, L0_ffn_W_down, L1_xattn_in_proj_w, L1_xattn_conv_w, L1_xattn_conv_b, L1_xattn_x_proj_w, L1_xattn_dt_proj_w, L1_xattn_dt_proj_b, L1_xattn_A_log, L1_xattn_D, L1_ffn_Wr, L1_ffn_bias, L1_ffn_Wg, L1_ffn_Wu, L1_ffn_Wd, L1_ffn_sWg, L1_ffn_sWu, L1_ffn_sWd):
    import jax
    import jax.numpy as jnp

    def _L0_xattn_ref(hidden_states, encoder_hidden_states, Wq, Wk, Wv, Wo, gq, gk):
        import jax, jax.numpy as jnp
        import numpy as np
        EPS = 1e-05

        def rmsnorm(x, g, eps=EPS):
            var = jnp.mean(jnp.square(x), axis=-1, keepdims=True)
            return x * jax.lax.rsqrt(var + eps) * g
        B, Sq, _ = hidden_states.shape
        Skv = encoder_hidden_states.shape[1]
        D = gq.shape[0]
        H = Wq.shape[1] // D
        scale = 1.0 / np.sqrt(D)
        q = (hidden_states @ Wq).reshape(B, Sq, H, D)
        k = (encoder_hidden_states @ Wk).reshape(B, Skv, H, D)
        v = (encoder_hidden_states @ Wv).reshape(B, Skv, H, D)
        q = rmsnorm(q, gq)
        k = rmsnorm(k, gk)
        scores = jnp.einsum('bqhd,bkhd->bhqk', q, k) * scale
        attn = jax.nn.softmax(scores, axis=-1)
        out = jnp.einsum('bhqk,bkhd->bqhd', attn, v)
        out = out.reshape(B, Sq, H * D)
        return out @ Wo

    def _L0_ffn_ref(input, SU_ug, SU_dp, Wscale_ug, Wscale_dp, W_up, W_gate, W_down):
        import jax, jax.numpy as jnp
        import numpy as np
        HIDDEN = 512
        INTER = 2048
        SCALE = 64.0

        def fwht(x):
            orig_shape = x.shape
            n = orig_shape[-1]
            x = x.reshape(-1, n)
            h = 1
            while h < n:
                x = x.reshape(-1, n // (2 * h), 2, h)
                a, b = (x[:, :, 0, :], x[:, :, 1, :])
                x = jnp.stack([a + b, a - b], axis=2).reshape(-1, n)
                h *= 2
            return (x / jnp.sqrt(jnp.asarray(n, x.dtype))).reshape(orig_shape)
        n = SU_ug.shape[0]
        x = input.reshape(-1, n)
        x = fwht(x * SU_ug) / SCALE
        x_up = x @ W_up.T * (Wscale_ug[:INTER] * SCALE)
        x_gate = x @ W_gate.T * (Wscale_ug[INTER:] * SCALE)
        x = jax.nn.silu(x_gate) * x_up
        x = fwht(x * SU_dp) / SCALE
        x = x @ W_down.T * (Wscale_dp * SCALE)
        return x.reshape(input.shape)

    def _L1_xattn_ref(hidden_states, z, in_proj_w, conv_w, conv_b, x_proj_w, dt_proj_w, dt_proj_b, A_log, D):
        import jax, jax.numpy as jnp
        import numpy as np
        import math
        B, L, DM = (2, 512, 256)
        DS, DC, EXP = (16, 4, 2)
        DI = EXP * DM
        DR = math.ceil(DM / 16)
        DT_MIN, DT_MAX, DT_FLOOR = (0.001, 0.1, 0.0001)

        def _ssm_forward(hidden_states, z, in_proj_w, conv_w, conv_b, x_proj_w, dt_proj_w, dt_proj_b, A_log, D):
            b = hidden_states.shape[0]
            x = jnp.einsum('ed,bld->bel', in_proj_w, hidden_states)
            xp = jnp.pad(x, ((0, 0), (0, 0), (DC - 1, 0)))
            xc = jax.lax.conv_general_dilated(xp, conv_w[:, None, :], window_strides=(1,), padding='VALID', dimension_numbers=('NCH', 'OIH', 'NCH'), feature_group_count=DI)
            u = jax.nn.silu(xc + conv_b[None, :, None])
            x_dbl = jnp.einsum('ke,bel->bkl', x_proj_w, u)
            dt_lo = x_dbl[:, :DR]
            Bm = x_dbl[:, DR:DR + DS]
            Cm = x_dbl[:, DR + DS:]
            delta = jax.nn.softplus(jnp.einsum('er,brl->bel', dt_proj_w, dt_lo) + dt_proj_b[None, :, None])
            A = -jnp.exp(A_log)

            def step(state, xs):
                d_t, B_t, C_t, u_t = xs
                dA = jnp.exp(d_t[..., None] * A)
                state = state * dA + (d_t * u_t)[..., None] * B_t[:, None, :]
                y_t = jnp.einsum('ben,bn->be', state, C_t)
                return (state, y_t)
            xs = (jnp.moveaxis(delta, -1, 0), jnp.moveaxis(Bm, -1, 0), jnp.moveaxis(Cm, -1, 0), jnp.moveaxis(u, -1, 0))
            state0 = jnp.zeros((b, DI, DS), delta.dtype)
            _, ys = jax.lax.scan(step, state0, xs)
            y = jnp.moveaxis(ys, 0, -1)
            y = y + D[None, :, None] * u
            y = y * jax.nn.silu(z)
            return jnp.swapaxes(y, 1, 2)
        return _ssm_forward(hidden_states, z, in_proj_w, conv_w, conv_b, x_proj_w, dt_proj_w, dt_proj_b, A_log, D)

    def _L1_ffn_ref(x, Wr, bias, Wg, Wu, Wd, sWg, sWu, sWd):
        import jax, jax.numpy as jnp
        import numpy as np
        TOPK = 2
        NORM_TOPK = True
        SCALE = 1.0
        EPS = 1e-09
        b, s, h = x.shape
        E = Wr.shape[0]
        xt = x.reshape(b * s, h)
        logits = xt @ Wr.T + bias
        probs = jax.nn.softmax(logits, axis=-1)
        topk_val, topk_idx = jax.lax.top_k(probs, TOPK)
        if NORM_TOPK:
            w = topk_val / (jnp.sum(topk_val, axis=-1, keepdims=True) + EPS)
        else:
            w = topk_val
        w = w * SCALE
        g = jnp.einsum('th,ehi->tei', xt, Wg)
        u = jnp.einsum('th,ehi->tei', xt, Wu)
        y = jnp.einsum('tei,eih->teh', jax.nn.silu(g) * u, Wd)
        oh = jax.nn.one_hot(topk_idx, E, dtype=x.dtype)
        routed = jnp.einsum('tke,tk,teh->th', oh, w, y)
        shared = jax.nn.silu(xt @ sWg) * (xt @ sWu) @ sWd
        return (routed + shared).reshape(b, s, h)
    x = x + _L0_xattn_ref(_layernorm(x, axis=-1), ctx_1024, L0_xattn_Wq, L0_xattn_Wk, L0_xattn_Wv, L0_xattn_Wo, L0_xattn_gq, L0_xattn_gk)
    x = x + _L0_ffn_ref(_layernorm(x, axis=-1), L0_ffn_SU_ug, L0_ffn_SU_dp, L0_ffn_Wscale_ug, L0_ffn_Wscale_dp, L0_ffn_W_up, L0_ffn_W_gate, L0_ffn_W_down)
    x = x + _L1_xattn_ref(ctx_1024, _layernorm(x, axis=-1), L1_xattn_in_proj_w, L1_xattn_conv_w, L1_xattn_conv_b, L1_xattn_x_proj_w, L1_xattn_dt_proj_w, L1_xattn_dt_proj_b, L1_xattn_A_log, L1_xattn_D)
    x = x + _L1_ffn_ref(_layernorm(x, axis=-1), L1_ffn_Wr, L1_ffn_bias, L1_ffn_Wg, L1_ffn_Wu, L1_ffn_Wd, L1_ffn_sWg, L1_ffn_sWu, L1_ffn_sWd)
    return x

_drawn_inputs = setup_inputs


def setup_inputs(seed=0):
    import zlib

    import numpy as np

    out = dict(_drawn_inputs(seed))
    spreads = {'L0_xattn_gq': (1.0, 0.2),
     'L0_xattn_gk': (1.0, 0.2),
     'L1_xattn_conv_b': (0.0, 0.1),
     'L1_xattn_D': (1.0, 0.2),
     'L1_ffn_bias': (0.0, 0.8)}
    factors = {'L1_xattn_dt_proj_w': 5.674,
     'L1_ffn_Wr': 2.948,
     'L1_ffn_Wg': 2.763,
     'L1_ffn_Wu': 2.698,
     'L1_ffn_Wd': 2.704}
    for name, (base, spread) in spreads.items():
        noise = np.random.default_rng([zlib.crc32(name.encode()), seed]).standard_normal(out[name].shape)
        drawn = base * np.exp(spread * noise) if base else spread * noise
        out[name] = jnp.asarray(drawn.astype(out[name].dtype))
    for name, factor in factors.items():
        out[name] = (out[name] * factor).astype(out[name].dtype)
    return out
```

```python
from contextlib import ExitStack

import concourse.bass as bass
from concourse import mybir

F32 = mybir.dt.float32
F32R = mybir.dt.float32r
ALU = mybir.AluOpType
ACT = mybir.ActivationFunctionType
AX_X = mybir.AxisListType.X

P = 128
B = 4
S = 512
TB = S // P
DIM = 512
KD = DIM // P
CD = 256
KC = CD // P
HEADS = 16
LN_EPS = 1e-5


class Steps:

    def __init__(self, eng, sem, base=0):
        self.eng, self.sem, self.base, self.n = eng, sem, base, 0

    def mark(self, ins):
        self.n += 1
        ins.then_inc(self.sem, 1)

    def wait(self):
        self.eng.wait_ge(self.sem, self.base + self.n)

    def after(self, ins):
        self.mark(ins)
        self.wait()


class Scope:

    def __init__(self, nc, stage):
        self.nc, self.stage, self.stack, self.sems = nc, stage, ExitStack(), []

    def __enter__(self):
        self.stack.__enter__()
        return self

    def __exit__(self, *a):
        self.nc.clear_and_free_semaphores(self.sems)
        self.nc.all_engine_barrier()
        return self.stack.__exit__(*a)

    def sb(self, name, shape, dt=F32):
        return self.stack.enter_context(self.nc.sbuf_tensor(f"{self.stage}_{name}", shape, dt))

    def ps(self, name, shape, dt=F32):
        return self.stack.enter_context(self.nc.psum_tensor(f"{self.stage}_{name}", shape, dt))

    def sem(self, name):
        self.sems.append(self.nc.alloc_semaphore(f"{self.stage}_{name}"))
        return self.sems[-1]

    def block(self):
        return self.nc.Block()


def wait_apart(eng, sem, value, pace):
    eng.wait_ge(sem, value)
    eng.sem_inc(pace, 1)


def split_product(pe, out, lhs, rhs, start, stop):
    (lh, ll), (rh, rl) = lhs, rhs
    pe.matmul(out, lh, rh, start=start, stop=False)
    pe.matmul(out, lh, rl, start=False, stop=False)
    return pe.matmul(out, ll, rh, start=False, stop=stop)


def newton_rsqrt(dve, own, out, value, guess_bits, work):
    own.after(dve.tensor_scalar(guess_bits.bitcast(mybir.dt.int32), value.bitcast(mybir.dt.int32), 1, None,
                                ALU.logical_shift_right))
    own.after(dve.tensor_scalar(out.bitcast(mybir.dt.int32), guess_bits.bitcast(mybir.dt.int32), -1.0,
                                float(0x5F3759DF), ALU.mult, ALU.add))
    for _ in range(3):
        own.after(dve.tensor_tensor(work, out, out, ALU.mult))
        own.after(dve.tensor_tensor(work, work, value, ALU.mult))
        own.after(dve.tensor_scalar(work, work, -0.5, 1.5, ALU.mult, ALU.add))
        last = dve.tensor_tensor(out, out, work, ALU.mult)
        own.after(last)


RSQRT_STEPS = 2 + 3 * 4


def stage_norm(nc, stage, x, xT, ident, ctx=None, ctxT=None):
    xt = x.rearrange("(b t p) d -> b t p d", b=B, t=TB)
    with Scope(nc, stage) as m:
        ident_sb = m.sb("ident", [P, P])
        rows = [m.sb(f"rows{t}", [P, DIM]) for t in range(TB)]
        normed = [m.sb(f"normed{t}", [P, DIM]) for t in range(TB)]
        stats = m.sb("stats", [P, TB, 6])
        meanvar = m.sb("meanvar", [P, TB, 2])
        var_eps = m.sb("var_eps", [P, TB])
        guess = m.sb("guess", [P, TB])
        work = m.sb("work", [P, TB])
        rstd = m.sb("rstd", [P, TB])
        outT = m.sb("outT", [P, 2, KD, S], F32R)
        banks = [m.ps(f"bank{t}", [P, KD, P]) for t in range(TB)]
        s_ident = m.sem("ident_in")
        s_rows = [m.sem(f"rows_in{t}") for t in range(TB)]
        s_dve = m.sem("dve_steps")
        s_pace = m.sem("pace")
        s_normed = m.sem("normed")
        s_tr = m.sem("transposed")
        s_hi = m.sem("hi")
        s_lo = m.sem("lo")
        s_out = m.sem("stored")
        if ctx is not None:
            crows = [m.sb(f"crows{t}", [P, CD]) for t in range(TB)]
            coutT = m.sb("coutT", [P, 2, KC, S], F32R)
            cbanks = [m.ps(f"cbank{t}", [P, KD, P]) for t in range(TB)]
            s_crows = [m.sem(f"crows_in{t}") for t in range(TB)]
            s_ctr = m.sem("ctx_transposed")
            s_chi = m.sem("ctx_hi")
            s_clo = m.sem("ctx_lo")
            s_cout = m.sem("ctx_stored")

        with m.block() as block:
            @block.sync
            def _(sp):
                sp.sem_inc(s_out, 16)
                if ctx is not None:
                    sp.sem_inc(s_cout, 16)
                sp.dma_start(ident_sb[:, :], ident).then_inc(s_ident, 16)
                with sp.Fori(0, B) as b:
                    for t in range(TB):
                        sp.wait_ge(s_normed, b * TB + t + 1)
                        sp.dma_start(rows[t][:, :], xt[b, t]).then_inc(s_rows[t], 16)
                        if ctx is not None:
                            sp.wait_ge(s_ctr, b * TB + t + 1)
                            sp.dma_start(crows[t][:, :], ctx[b, t * P:(t + 1) * P, :]).then_inc(s_crows[t], 16)
                    sp.wait_ge(s_lo, (b + 2) * TB)
                    sp.dma_start(xT[b], outT[:, :, :, :].bitcast(F32)).then_inc(s_out, 16)
                    if ctx is not None:
                        sp.wait_ge(s_clo, (b + 2) * TB)
                        sp.dma_start(ctxT[b], coutT[:, :, :, :].bitcast(F32)).then_inc(s_cout, 16)
                sp.wait_ge(s_out, 16 * (B + 1))
                if ctx is not None:
                    sp.wait_ge(s_cout, 16 * (B + 1))

            @block.vector
            def _(dve):
                dve.sem_inc(s_normed, TB)
                dve.sem_inc(s_lo, TB)
                if ctx is not None:
                    dve.sem_inc(s_clo, TB)
                per = 2 * TB + 1 + RSQRT_STEPS
                with dve.Fori(0, B) as b:
                    own = Steps(dve, s_dve, b * per)
                    for t in range(TB):
                        dve.wait_ge(s_rows[t], (b + 1) * 16)
                        own.mark(dve.bn_stats(stats[:, t, :], rows[t][:, :]))
                    wait_apart(dve, s_dve, own.base + own.n, s_pace)
                    for t in range(TB):
                        own.mark(dve.bn_aggr(meanvar[:, t, :], stats[:, t, :]))
                    own.wait()
                    own.after(dve.tensor_scalar(var_eps[:, :], meanvar[:, :, 1], LN_EPS, None, ALU.add))
                    newton_rsqrt(dve, own, rstd[:, :], var_eps[:, :], guess[:, :], work[:, :])
                    for t in range(TB):
                        dve.wait_ge(s_tr, b * TB + t + 1)
                        dve.tensor_scalar(normed[t][:, :], rows[t][:, :], meanvar[:, t, 0:1], rstd[:, t:t + 1],
                                          ALU.subtract, ALU.mult).then_inc(s_normed, 1)
                    for t in range(TB):
                        part = slice(t * P, (t + 1) * P)
                        dve.wait_ge(s_hi, b * TB + t + 1)
                        dve.tensor_tensor(outT[:, 1, :, part], banks[t][:, :, :], outT[:, 0, :, part].bitcast(F32),
                                          ALU.subtract).then_inc(s_lo, 1)
                        if ctx is not None:
                            dve.wait_ge(s_chi, b * TB + t + 1)
                            dve.tensor_tensor(coutT[:, 1, :, part], cbanks[t][:, 0:KC, :],
                                              coutT[:, 0, :, part].bitcast(F32), ALU.subtract).then_inc(s_clo, 1)
                    assert own.n == per

            @block.tensor
            def _(pe):
                pe.sem_inc(s_tr, TB)
                if ctx is not None:
                    pe.sem_inc(s_ctr, TB)
                pe.wait_ge(s_ident, 16)
                with pe.Fori(0, B) as b:
                    for t in range(TB):
                        if ctx is not None:
                            pe.wait_ge(s_crows[t], (b + 1) * 16)
                            pe.wait_ge(s_clo, b * TB + t + 1)
                            for k in range(KC):
                                tr = pe.transpose(cbanks[t][:, k, :], crows[t][:, k * P:(k + 1) * P], ident_sb[:, :])
                            tr.then_inc(s_ctr, 1)
                    for t in range(TB):
                        pe.wait_ge(s_normed, (b + 1) * TB + t + 1)
                        pe.wait_ge(s_lo, b * TB + t + 1)
                        for k in range(KD):
                            tr = pe.transpose(banks[t][:, k, :], normed[t][:, k * P:(k + 1) * P], ident_sb[:, :])
                        tr.then_inc(s_tr, 1)

            @block.scalar
            def _(act):
                with act.Fori(0, B) as b:
                    if ctx is not None:
                        act.wait_ge(s_cout, 16 * (b + 1))
                        for t in range(TB):
                            act.wait_ge(s_ctr, (b + 1) * TB + t + 1)
                            act.copy(coutT[:, 0, :, t * P:(t + 1) * P], cbanks[t][:, 0:KC, :]).then_inc(s_chi, 1)
                    act.wait_ge(s_out, 16 * (b + 1))
                    for t in range(TB):
                        act.wait_ge(s_tr, (b + 1) * TB + t + 1)
                        act.copy(outT[:, 0, :, t * P:(t + 1) * P], banks[t][:, :, :]).then_inc(s_hi, 1)


def stage_attention(nc, x, x1, xT, ctxT, Wq, Wk, Wv, Wo, gq, gk, ident):
    D = P
    HP = 2
    PAIRS = HEADS // HP
    W2 = HP * D
    RMS_EPS = 1e-5
    scale = D ** -0.5
    xr = x.rearrange("(n p) d -> p n d", p=P)
    x1r = x1.rearrange("(n p) d -> p n d", p=P)
    wq_d = Wq.rearrange("(k p) n -> p k n", p=P)
    wk_d = Wk.rearrange("(k p) n -> p k n", p=P)
    wv_d = Wv.rearrange("(k p) n -> p k n", p=P)
    wo_d = Wo.rearrange("(h p) n -> p h n", p=P)
    NQ, NKV = KD * W2, KC * W2
    with Scope(nc, "att") as m:
        ident_sb = m.sb("ident", [P, P])
        ones = m.sb("ones", [P, 1])
        gains = m.sb("gains", [P, 2])
        gain = m.sb("gain", [P, 1])
        xs = m.sb("x", [P, B * TB, DIM])
        raw = m.sb("raw_qkv", [P, NQ + 2 * NKV])
        raw_o = m.sb("raw_o", [P, HP, DIM])
        w = m.sb("w_qkv", [P, 2, NQ + 2 * NKV], F32R)
        wo = m.sb("wo", [P, 2, HP, DIM], F32R)
        xn = m.sb("xn", [P, 2, KD, S], F32R)
        cx = m.sb("cx", [P, 2, KC, S], F32R)
        kn = m.sb("kn", [P, TB, HP, D])
        ksq = m.sb("ksq", [P, TB, HP, D])
        qsq = m.sb("qsq", [P, HP, S])
        qT = m.sb("qT", [P, 2, HP, S], F32R)
        kT = m.sb("kT", [P, 2, HP, S], F32R)
        v = m.sb("v", [P, 2, TB, W2], F32R)
        probs = m.sb("probs", [P, HP * TB, S])
        pT = m.sb("pT", [P, 2, TB, S], F32R)
        oT = m.sb("oT", [P, 2, HP, S], F32R)
        kss = m.sb("kss", [P, TB * HP])
        qss = m.sb("qss", [P, TB * HP])
        rk = m.sb("rk", [P, TB * HP])
        rq = m.sb("rq", [P, TB * HP])
        guess = m.sb("guess", [P, TB * HP])
        work = m.sb("work", [P, TB * HP])
        nmax = m.sb("nmax", [P, TB * HP])
        bias = m.sb("bias", [P, TB * HP])
        sums = m.sb("sums", [P, TB * HP])
        recip = m.sb("recip", [P, TB * HP])
        ps_s = [m.ps(f"s{i}", [P, S]) for i in range(2)]
        ps_pt = [m.ps(f"pt{i}", [P, TB, P]) for i in range(2)]
        ps_w = [m.ps(f"w{i}", [P, 512]) for i in range(3)]
        ps_o = m.ps("o", [P, S])

        s_const = m.sem("const_in")
        s_gain = m.sem("gain")
        s_x = m.sem("x_in")
        s_raw, s_rawo = m.sem("raw_in"), m.sem("raw_o_in")
        s_w, s_wo = m.sem("w_split"), m.sem("wo_split")
        s_xn, s_cx = m.sem("xn_in"), m.sem("cx_in")
        s_s = m.sem("scores")
        s_max = m.sem("max")
        s_exp = m.sem("exp")
        s_rec = m.sem("recip")
        s_pn = m.sem("probs_normed")
        s_k, s_kc, s_ksq, s_kn = m.sem("k"), m.sem("k_copied"), m.sem("k_squared"), m.sem("k_normed")
        s_kt, s_kthi, s_ktlo = m.sem("kT"), m.sem("kT_hi"), m.sem("kT_lo")
        s_q, s_qhi, s_qsq, s_qlo = m.sem("q"), m.sem("q_hi"), m.sem("q_squared"), m.sem("q_lo")
        s_ss, s_ssread, s_rq = m.sem("q_sums"), m.sem("q_sums_read"), m.sem("rq")
        s_v, s_vhi, s_vlo = m.sem("v"), m.sem("v_hi"), m.sem("v_lo")
        s_pt, s_pthi = m.sem("pT"), m.sem("pT_hi")
        s_ptlo = m.sem("pT_lo")
        s_pv, s_ohi = m.sem("pv"), m.sem("o_hi")
        s_olo = m.sem("o_lo")
        s_y = m.sem("y")
        s_yadd = m.sem("y_added")
        s_dve = m.sem("dve_steps")
        s_store = m.sem("stored")
        s_pace = m.sem("pace")

        def pairs(eng, iteration):
            with eng.Fori(0, PAIRS - 1) as hp:
                for b in range(B):
                    iteration(hp, b, False)
            for b in range(B):
                iteration(PAIRS - 1, b, b == B - 1)

        def wpart(part, which, k):
            at = {"q": 0, "k": NQ, "v": NQ + NKV}[which] + k * W2
            return w[:, part, at:at + W2]

        with m.block() as block:
            @block.sync
            def _(sp):
                def load_weights(hp):
                    sp.dma_start(raw[:, 0:NQ].rearrange("p (k n) -> p k n", k=KD), wq_d[:, :, bass.ds(hp * W2, W2)]).then_inc(s_raw, 16)
                    for at, src in ((NQ, wk_d), (NQ + NKV, wv_d)):
                        sp.dma_start(raw[:, at:at + NKV].rearrange("p (k n) -> p k n", k=KC),
                                     src[:, :, bass.ds(hp * W2, W2)]).then_inc(s_raw, 16)

                def load_wo(hp):
                    sp.dma_start(raw_o[:, :, :], wo_d[:, bass.ds(hp * HP, HP), :]).then_inc(s_rawo, 16)

                sp.dma_start(ident_sb[:, :], ident).then_inc(s_const, 16)
                sp.dma_start(gains[:, 0:1], gq.rearrange("(p a) -> p a", a=1)).then_inc(s_const, 16)
                sp.dma_start(gains[:, 1:2], gk.rearrange("(p a) -> p a", a=1)).then_inc(s_const, 16)
                load_weights(0)
                sp.dma_start(cx[:, :, :, :].bitcast(F32), ctxT[0]).then_inc(s_cx, 16)
                sp.dma_start(xn[:, :, :, :].bitcast(F32), xT[0]).then_inc(s_xn, 16)
                load_wo(0)
                sp.dma_start(xs[:, :, :], xr).then_inc(s_x, 16)

                def iteration(hp, b, last):
                    i = hp * B + b
                    if b == 0 and not (isinstance(hp, int) and hp == PAIRS - 1):
                        sp.wait_ge(s_w, hp + 1)
                        load_weights(hp + 1)
                        sp.wait_ge(s_wo, hp + 1)
                        load_wo(hp + 1)
                    if not last:
                        sp.wait_ge(s_q, 2 * i + 2)
                        sp.dma_start(xn[:, :, :, :].bitcast(F32), xT[(b + 1) % B]).then_inc(s_xn, 16)
                        sp.wait_ge(s_v, 2 * i + 2)
                        sp.dma_start(cx[:, :, :, :].bitcast(F32), ctxT[(b + 1) % B]).then_inc(s_cx, 16)

                pairs(sp, iteration)
                sp.wait_ge(s_yadd, 4 + 4 * PAIRS * B)
                sp.dma_start(x1r, xs[:, :, :]).then_inc(s_store, 16)
                sp.wait_ge(s_store, 16)

            @block.tensor
            def _(pe):
                def score(i, n):
                    h, t = divmod(n, TB)
                    if n == 0:
                        pe.wait_ge(s_ktlo, 2 * i + 2)
                        pe.wait_ge(s_qlo, 2 * i + 2)
                    pe.wait_ge(s_exp, 8 * i + n + 1)
                    q = slice(t * P, (t + 1) * P)
                    split_product(pe, ps_s[n % 2][:, :], (qT[:, 0, h, q], qT[:, 1, h, q]),
                                  (kT[:, 0, h, :], kT[:, 1, h, :]), True, True).then_inc(s_s, 1)

                def kv(j, which, half, bank, sem):
                    for a in range(2):
                        t = 2 * half + a
                        rows = slice(t * P, (t + 1) * P)
                        for k in range(KC):
                            mm = split_product(pe, ps_w[bank][:, a * W2:(a + 1) * W2],
                                               (cx[:, 0, k, rows], cx[:, 1, k, rows]),
                                               (wpart(0, which, k), wpart(1, which, k)), k == 0, k == KC - 1)
                    mm.then_inc(sem, 1)

                def queries(h, bank):
                    d = slice(h * D, (h + 1) * D)
                    for k in range(KD):
                        mm = split_product(pe, ps_w[bank][:, :], (wpart(0, "q", k)[:, d], wpart(1, "q", k)[:, d]),
                                           (xn[:, 0, k, :], xn[:, 1, k, :]), k == 0, k == KD - 1)
                    mm.then_inc(s_q, 1)

                def turn_k(h, bank):
                    for t in range(TB):
                        tr = pe.transpose(ps_w[bank][:, t * P:(t + 1) * P], kn[:, t, h, :], ident_sb[:, :])
                    tr.then_inc(s_kt, 1)

                def sums_q():
                    for n in range(HP * TB):
                        h, t = divmod(n, TB)
                        mm = pe.matmul(ps_o[:, n:n + 1], qsq[:, h, t * P:(t + 1) * P], ones[:, :], start=True, stop=True)
                    mm.then_inc(s_ss, 1)

                def turn_p(i, h, k):
                    n = 8 * i + 4 * h + k
                    if k == 0:
                        pe.wait_ge(s_pn, 8 * i + 4 * h + 4)
                    pe.wait_ge(s_ptlo, n + 1)
                    for t in range(TB):
                        tr = pe.transpose(ps_pt[k % 2][:, t, :], probs[:, h * TB + t, k * P:(k + 1) * P], ident_sb[:, :])
                    tr.then_inc(s_pt, 1)

                def pv(i, h):
                    pe.wait_ge(s_ptlo, 8 * i + 4 * h + 4 + 2)
                    d = slice(h * D, (h + 1) * D)
                    for k in range(TB):
                        mm = split_product(pe, ps_o[:, :], (v[:, 0, k, d], v[:, 1, k, d]),
                                           (pT[:, 0, k, :], pT[:, 1, k, :]), k == 0, k == TB - 1)
                    mm.then_inc(s_pv, 1)

                def project(t, bank):
                    rows = slice(t * P, (t + 1) * P)
                    for h in range(HP):
                        mm = split_product(pe, ps_w[bank][:, :], (oT[:, 0, h, rows], oT[:, 1, h, rows]),
                                           (wo[:, 0, h, :], wo[:, 1, h, :]), h == 0, h == HP - 1)
                    mm.then_inc(s_y, 1)

                pe.wait_ge(s_const, 48)
                pe.wait_ge(s_gain, 1)
                pe.wait_ge(s_w, 1)
                pe.wait_ge(s_cx, 16)
                kv(0, "k", 0, 0, s_k)
                kv(0, "k", 1, 1, s_k)
                pe.wait_ge(s_xn, 16)
                queries(0, 2)
                pe.wait_ge(s_kc, 1)
                queries(1, 0)
                pe.wait_ge(s_kn, 1)
                turn_k(0, 1)
                pe.wait_ge(s_qlo, 1)
                turn_k(1, 2)
                pe.wait_ge(s_qsq, 2)
                sums_q()
                pe.wait_ge(s_qlo, 2)
                kv(0, "v", 0, 0, s_v)
                pe.wait_ge(s_ktlo, 1)
                kv(0, "v", 1, 1, s_v)

                def iteration(hp, b, last):
                    i = hp * B + b
                    j = i + 1
                    score(i, 0)
                    score(i, 1)
                    if not last:
                        pe.wait_ge(s_w, (hp + 2) if b == B - 1 else (hp + 1))
                        pe.wait_ge(s_cx, 16 * j + 16)
                        pe.wait_ge(s_yadd, 4 * i + 2)
                        kv(j, "k", 0, 0, s_k)
                    score(i, 2)
                    score(i, 3)
                    if not last:
                        pe.wait_ge(s_yadd, 4 * i + 3)
                        kv(j, "k", 1, 1, s_k)
                    score(i, 4)
                    for k in range(TB):
                        turn_p(i, 0, k)
                        if k < 3:
                            score(i, 5 + k)
                    if not last:
                        pe.wait_ge(s_xn, 16 * j + 16)
                        pe.wait_ge(s_yadd, 4 * i + 4)
                        queries(0, 2)
                    pe.wait_ge(s_vlo, 2 * i + 2)
                    pe.wait_ge(s_olo, 2 * i + 2)
                    pv(i, 0)
                    if not last:
                        pe.wait_ge(s_kc, 2 * j + 1)
                        queries(1, 0)
                        pe.wait_ge(s_kn, j + 1)
                        turn_k(0, 1)
                        pe.wait_ge(s_qlo, 2 * j + 1)
                        turn_k(1, 2)
                    for k in range(TB):
                        turn_p(i, 1, k)
                    pe.wait_ge(s_olo, 2 * i + 3)
                    if not last:
                        pe.wait_ge(s_qsq, 2 * j + 2)
                        sums_q()
                        pe.wait_ge(s_ssread, j + 1)
                    pv(i, 1)
                    if not last:
                        pe.wait_ge(s_qlo, 2 * j + 2)
                        kv(j, "v", 0, 0, s_v)
                        pe.wait_ge(s_ktlo, 2 * j + 1)
                        kv(j, "v", 1, 1, s_v)
                    pe.wait_ge(s_olo, 2 * i + 4)
                    pe.wait_ge(s_wo, hp + 1)
                    if not last:
                        pe.wait_ge(s_ktlo, 2 * j + 2)
                    project(0, 2)
                    if not last:
                        pe.wait_ge(s_vlo, 2 * j + 1)
                    project(1, 0)
                    if not last:
                        pe.wait_ge(s_vlo, 2 * j + 2)
                    project(2, 1)
                    pe.wait_ge(s_yadd, 4 + 4 * i + 1)
                    project(3, 2)

                pairs(pe, iteration)

            @block.scalar
            def _(act):
                def copy_k(j, half):
                    act.wait_ge(s_k, 2 * j + half + 1)
                    act.copy(kn[:, 2 * half:2 * half + 2, :, :], ps_w[half][:, :]).then_inc(s_kc, 1)

                def q_parts(j, h):
                    bank = ps_w[(2, 0)[h]]
                    act.wait_ge(s_q, 2 * j + h + 1)
                    act.copy(qT[:, 0, h, :], bank[:, :]).then_inc(s_qhi, 1)
                    act.activation(qsq[:, h, :], bank[:, :], ACT.Square).then_inc(s_qsq, 1)

                def kt_hi(j, h):
                    act.wait_ge(s_kt, 2 * j + h + 1)
                    act.activation(kT[:, 0, h, :], ps_w[1 + h][:, :], ACT.Copy, scale=gain[:, 0:1]).then_inc(s_kthi, 1)

                def v_hi(j, half):
                    act.wait_ge(s_v, 2 * j + half + 1)
                    act.copy(v[:, 0, 2 * half:2 * half + 2, :], ps_w[half][:, :]).then_inc(s_vhi, 1)

                def exp(i, n):
                    act.wait_ge(s_max, 8 * i + n + 1)
                    act.activation(probs[:, n, :], ps_s[n % 2][:, :], ACT.Exp, bias=bias[:, n:n + 1],
                                   scale=rq[:, n:n + 1], accum_out=sums[:, n:n + 1]).then_inc(s_exp, 1)

                def pt_hi(i, h, k):
                    act.wait_ge(s_pt, 8 * i + 4 * h + k + 1)
                    act.copy(pT[:, 0, k, :], ps_pt[k % 2][:, :, :]).then_inc(s_pthi, 1)

                def o_hi(i, h):
                    act.wait_ge(s_pv, 2 * i + h + 1)
                    act.copy(oT[:, 0, h, :], ps_o[:, :]).then_inc(s_ohi, 1)

                act.sem_inc(s_exp, 2)
                act.wait_ge(s_gain, 1)
                copy_k(0, 0)
                copy_k(0, 1)
                q_parts(0, 0)
                q_parts(0, 1)
                kt_hi(0, 0)
                kt_hi(0, 1)
                v_hi(0, 0)
                v_hi(0, 1)
                act.wait_ge(s_rq, 1)

                def iteration(hp, b, last):
                    i = hp * B + b
                    j = i + 1
                    act.wait_ge(s_rq, i + 1)
                    exp(i, 0)
                    exp(i, 1)
                    if not last:
                        copy_k(j, 0)
                    exp(i, 2)
                    exp(i, 3)
                    if not last:
                        copy_k(j, 1)
                    exp(i, 4)
                    for k in range(TB):
                        pt_hi(i, 0, k)
                        if k < 3:
                            exp(i, 5 + k)
                    if not last:
                        q_parts(j, 0)
                    o_hi(i, 0)
                    if not last:
                        q_parts(j, 1)
                        kt_hi(j, 0)
                        kt_hi(j, 1)
                    for k in range(TB):
                        pt_hi(i, 1, k)
                    o_hi(i, 1)
                    if not last:
                        v_hi(j, 0)
                        v_hi(j, 1)

                pairs(act, iteration)

            @block.gpsimd
            def _(pool):
                def square_k(j):
                    pool.wait_ge(s_kc, 2 * j + 2)
                    pool.tensor_tensor(ksq[:, :, :, :], kn[:, :, :, :], kn[:, :, :, :], ALU.mult).then_inc(s_ksq, 1)

                def norm_p(i, n):
                    wait_apart(pool, s_rec, 8 * i + n + 1, s_pace)
                    pool.tensor_scalar(probs[:, n, :], probs[:, n, :], recip[:, n:n + 1], 1.0, ALU.mult,
                                       ALU.mult).then_inc(s_pn, 1)

                square_k(0)

                def iteration(hp, b, last):
                    i = hp * B + b
                    for n in range(4):
                        norm_p(i, n)
                    if not last:
                        square_k(i + 1)
                    for n in range(4, 8):
                        norm_p(i, n)

                pairs(pool, iteration)

            @block.vector
            def _(dve):
                def split_w(own, hp):
                    dve.wait_ge(s_raw, 48 * (hp + 1))
                    own.after(dve.tensor_copy(w[:, 0, :], raw[:, :]))
                    dve.tensor_tensor(w[:, 1, :], raw[:, :], w[:, 0, :].bitcast(F32), ALU.subtract).then_inc(s_w, 1)

                def split_wo(own, hp):
                    dve.wait_ge(s_rawo, 16 * (hp + 1))
                    own.after(dve.tensor_copy(wo[:, 0, :, :], raw_o[:, :, :]))
                    dve.tensor_tensor(wo[:, 1, :, :], raw_o[:, :, :], wo[:, 0, :, :].bitcast(F32),
                                      ALU.subtract).then_inc(s_wo, 1)

                def row_max(own, i, n):
                    dve.wait_ge(s_s, 8 * i + n + 1)
                    own.after(dve.tensor_reduce(nmax[:, n:n + 1], ps_s[n % 2][:, :], AX_X, ALU.max, negate=True))
                    dve.tensor_tensor(bias[:, n:n + 1], nmax[:, n:n + 1], rq[:, n:n + 1], ALU.mult).then_inc(s_max, 1)

                def row_recip(i, n):
                    dve.wait_ge(s_exp, 8 * i + n + 1 + 2)
                    dve.reciprocal(recip[:, n:n + 1], sums[:, n:n + 1]).then_inc(s_rec, 1)

                def norm_k(own, j):
                    dve.wait_ge(s_ksq, j + 1)
                    own.after(dve.tensor_reduce(kss[:, :], ksq[:, :, :, :], AX_X, ALU.add))
                    own.after(dve.tensor_scalar(kss[:, :], kss[:, :], 1.0 / D, RMS_EPS, ALU.mult, ALU.add))
                    newton_rsqrt(dve, own, rk[:, :], kss[:, :], guess[:, :], work[:, :])
                    for n in range(TB * HP):
                        t, h = divmod(n, HP)
                        ins = dve.tensor_scalar(kn[:, t, h, :], kn[:, t, h, :], rk[:, n:n + 1], None, ALU.mult)
                    ins.then_inc(s_kn, 1)

                def q_lo(j, h):
                    dve.wait_ge(s_qsq, 2 * j + h + 1)
                    dve.tensor_tensor(qT[:, 1, h, :], ps_w[(2, 0)[h]][:, :], qT[:, 0, h, :].bitcast(F32),
                                      ALU.subtract).then_inc(s_qlo, 1)

                def kt_lo(j, h):
                    dve.wait_ge(s_kthi, 2 * j + h + 1)
                    dve.scalar_tensor_tensor(kT[:, 1, h, :], ps_w[1 + h][:, :], gain[:, 0:1],
                                             kT[:, 0, h, :].bitcast(F32), ALU.mult, ALU.subtract).then_inc(s_ktlo, 1)

                def v_lo(j, half):
                    dve.wait_ge(s_vhi, 2 * j + half + 1)
                    rows = slice(2 * half, 2 * half + 2)
                    dve.tensor_tensor(v[:, 1, rows, :], ps_w[half][:, :].rearrange("p (a n) -> p a n", a=2),
                                      v[:, 0, rows, :].bitcast(F32), ALU.subtract).then_inc(s_vlo, 1)

                def rms_q(own, j):
                    dve.wait_ge(s_ss, j + 1)
                    ins = dve.tensor_scalar(qss[:, :], ps_o[:, 0:TB * HP], 1.0 / D, RMS_EPS, ALU.mult, ALU.add)
                    ins.then_inc(s_ssread, 1)
                    dve.wait_ge(s_ssread, j + 1)
                    newton_rsqrt(dve, own, rq[:, :], qss[:, :], guess[:, :], work[:, :])
                    dve.sem_inc(s_rq, 1)

                def pt_lo(i, h, k):
                    dve.wait_ge(s_pthi, 8 * i + 4 * h + k + 1)
                    dve.tensor_tensor(pT[:, 1, k, :], ps_pt[k % 2][:, :, :].rearrange("p t n -> p (t n)"),
                                      pT[:, 0, k, :].bitcast(F32), ALU.subtract).then_inc(s_ptlo, 1)

                def o_lo(i, h):
                    dve.wait_ge(s_ohi, 2 * i + h + 1)
                    dve.tensor_tensor(oT[:, 1, h, :], ps_o[:, :], oT[:, 0, h, :].bitcast(F32),
                                      ALU.subtract).then_inc(s_olo, 1)

                def add_y(i, b, t):
                    dve.wait_ge(s_y, 4 * i + t + 1)
                    row = xs[:, b * TB + t, :]
                    dve.tensor_tensor(row, ps_w[(2, 0, 1, 2)[t]][:, :], row, ALU.add).then_inc(s_yadd, 1)

                dve.sem_inc(s_ptlo, 2)
                dve.sem_inc(s_olo, 2)
                dve.sem_inc(s_yadd, 4)
                own = Steps(dve, s_dve)
                own.mark(dve.memset(ones[:, :], 1.0))
                own.wait()
                dve.wait_ge(s_const, 48)
                dve.scalar_tensor_tensor(gain[:, :], gains[:, 0:1], scale, gains[:, 1:2], ALU.mult,
                                         ALU.mult).then_inc(s_gain, 1)
                dve.wait_ge(s_gain, 1)
                split_w(own, 0)
                norm_k(own, 0)
                q_lo(0, 0)
                q_lo(0, 1)
                kt_lo(0, 0)
                kt_lo(0, 1)
                rms_q(own, 0)
                v_lo(0, 0)
                v_lo(0, 1)
                split_wo(own, 0)
                dve.wait_ge(s_x, 16)
                base = own.n
                per_pair = B * (8 + 2 + 2 * RSQRT_STEPS) + 2

                def iteration(own, hp, b, last):
                    i = hp * B + b
                    j = i + 1
                    if b == B - 1 and not last:
                        split_w(own, hp + 1)
                    row_max(own, i, 0)
                    row_max(own, i, 1)
                    row_max(own, i, 2)
                    row_recip(i, 0)
                    row_max(own, i, 3)
                    row_recip(i, 1)
                    row_max(own, i, 4)
                    row_recip(i, 2)
                    row_recip(i, 3)
                    for k in range(TB):
                        pt_lo(i, 0, k)
                        if k < 3:
                            row_max(own, i, 5 + k)
                            row_recip(i, 4 + k)
                    row_recip(i, 7)
                    if not last:
                        norm_k(own, j)
                        q_lo(j, 0)
                    o_lo(i, 0)
                    if not last:
                        q_lo(j, 1)
                        kt_lo(j, 0)
                        kt_lo(j, 1)
                    for k in range(TB):
                        pt_lo(i, 1, k)
                    if not last:
                        rms_q(own, j)
                    o_lo(i, 1)
                    if not last:
                        v_lo(j, 0)
                        v_lo(j, 1)
                    for t in range(TB):
                        add_y(i, b, t)
                    if b == B - 1 and not last:
                        split_wo(own, hp + 1)

                with dve.Fori(0, PAIRS - 1) as hp:
                    own = Steps(dve, s_dve, hp * per_pair + base)
                    for b in range(B):
                        iteration(own, hp, b, False)
                    assert own.n == per_pair, own.n
                own = Steps(dve, s_dve, (PAIRS - 1) * per_pair + base)
                for b in range(B):
                    iteration(own, PAIRS - 1, b, b == B - 1)


def stage_mlp(nc, stage, x, out, xT, units, inner, weights, split, resident, shares=None):
    IC = inner // P
    N_IN = KD * inner
    N_ALL = 2 * N_IN + IC * DIM
    xr = x.rearrange("(n p) d -> p n d", p=P)
    outr = out.rearrange("(n p) d -> p n d", p=P)
    pairs, odd = divmod(units, 2)
    with Scope(nc, stage) as m:
        xs = m.sb("x", [P, B * TB, DIM])
        w = [m.sb(f"w{i}", [P, 2, N_ALL], F32R) for i in range(2)]
        raw = m.sb("raw", [P, N_ALL]) if split else None
        nx = B if resident else 2
        xin = [m.sb(f"xT{i}", [P, 2, KD, S], F32R) for i in range(nx)]
        gated = [m.sb(f"gated{i}", [P, S]) for i in range(2)]
        hid = [m.sb(f"hid{i}", [P, S]) for i in range(2)]
        hT = [m.sb(f"hT{i}", [P, 2, IC, S], F32R) for i in range(2)]
        share_sb = m.sb("shares", [P, B * TB, units]) if shares is not None else None
        ps_u = [m.ps(f"up{i}", [P, S]) for i in range(2)]
        ps_g = [m.ps(f"gate{i}", [P, S]) for i in range(2)]
        ps_y = [m.ps(f"y{i}", [P, DIM]) for i in range(TB)]

        s_x = m.sem("x_in")
        s_w = m.sem("w_in")
        s_wraw = m.sem("w_raw_in")
        s_whi, s_wsplit = m.sem("w_hi"), m.sem("w_split")
        s_xT = [m.sem(f"xT_in{i}") for i in range(nx)]
        s_ug = m.sem("up_gate")
        s_silu = m.sem("silu")
        s_h = m.sem("hidden")
        s_hhi = m.sem("hidden_hi")
        s_hlo = m.sem("hidden_lo")
        s_y = m.sem("y")
        s_yadd = m.sem("y_added")
        s_store = m.sem("stored")

        def every(eng, unit):
            tail = 3 if odd else 2
            n = (units - tail) // 2
            with eng.Fori(0, n) as pair:
                unit(pair * 2, 0, False)
                unit(pair * 2 + 1, 1, False)
            for u in range(units - tail, units):
                unit(u, u % 2, u == units - 1)

        def part(par, which, hl, k):
            at = {"gate": 0, "up": N_IN, "down": 2 * N_IN}[which] + k * (inner if which != "down" else DIM)
            return w[par][:, hl, at:at + (inner if which != "down" else DIM)]

        with m.block() as block:
            @block.sync
            def _(sp):
                def load_w(u, par):
                    if split:
                        weights(sp, u, raw, s_wraw)
                    else:
                        weights(sp, u, w[par], s_w)

                load_w(0, 0)
                if resident:
                    for b in range(B):
                        sp.dma_start(xin[b][:, :, :, :].bitcast(F32), xT[b]).then_inc(s_xT[b], 16)
                else:
                    for j in range(2):
                        sp.dma_start(xin[j][:, :, :, :].bitcast(F32), xT[j]).then_inc(s_xT[j], 16)
                sp.dma_start(xs[:, :, :], xr).then_inc(s_x, 16)
                if shares is not None:
                    sp.dma_start(share_sb[:, :, :], shares.rearrange("(n p) e -> p n e", p=P)).then_inc(s_x, 16)

                def unit(u, par, last):
                    if not last:
                        if split:
                            sp.wait_ge(s_wsplit, u + 1)
                        else:
                            sp.wait_ge(s_yadd, TB + TB * B * u)
                        if isinstance(u, int) and split and u + 1 == units - 1:
                            load_w("last", 1 - par)
                        else:
                            load_w(u + 1, 1 - par)
                    if not resident:
                        for b in range(B):
                            j = u * B + b + 2
                            if not (last and b >= B - 2):
                                sp.wait_ge(s_ug, IC * (j - 1))
                                sp.dma_start(xin[b % 2][:, :, :, :].bitcast(F32), xT[(b + 2) % B]).then_inc(s_xT[b % 2], 16)

                every(sp, unit)
                sp.wait_ge(s_yadd, TB + TB * B * units)
                sp.dma_start(outr, xs[:, :, :]).then_inc(s_store, 16)
                sp.wait_ge(s_store, 16)

            @block.tensor
            def _(pe):
                def up_gate(u, par, b):
                    j = u * B + b
                    if b == 0:
                        pe.wait_ge(s_wsplit if split else s_w, (u + 1) * (1 if split else 16))
                    if resident:
                        pe.wait_ge(s_xT[b], 16)
                        xi = xin[b]
                    else:
                        pe.wait_ge(s_xT[b % 2], u * 32 + (b // 2) * 16 + 16)
                        xi = xin[b % 2]
                    for ic in range(IC):
                        pe.wait_ge(s_h, IC * j + ic + 1)
                        cols = slice(ic * P, (ic + 1) * P)
                        for which, bank in (("gate", ps_g), ("up", ps_u)):
                            for k in range(KD):
                                mm = split_product(pe, bank[ic % 2][:, :],
                                                   (part(par, which, 0, k)[:, cols], part(par, which, 1, k)[:, cols]),
                                                   (xi[:, 0, k, :], xi[:, 1, k, :]), k == 0, k == KD - 1)
                        mm.then_inc(s_ug, 1)

                def down(u, par, b):
                    i = u * B + b
                    pe.wait_ge(s_hlo, 2 + IC * (i + 1))
                    ht = hT[b % 2]
                    for t in range(TB):
                        pe.wait_ge(s_yadd, TB * i + t + 1)
                        rows = slice(t * P, (t + 1) * P)
                        for ic in range(IC):
                            mm = split_product(pe, ps_y[t][:, :], (ht[:, 0, ic, rows], ht[:, 1, ic, rows]),
                                               (part(par, "down", 0, ic), part(par, "down", 1, ic)),
                                               ic == 0, ic == IC - 1)
                        mm.then_inc(s_y, 1)

                up_gate(0, 0, 0)

                def unit(u, par, last):
                    for b in range(B):
                        if b < B - 1:
                            up_gate(u, par, b + 1)
                        elif not last:
                            up_gate(u + 1, 1 - par, 0)
                        down(u, par, b)

                every(pe, unit)

            @block.scalar
            def _(act):
                def unit(u, par, last):
                    for b in range(B):
                        i = u * B + b
                        for ic in range(IC + 1):
                            if ic < IC:
                                act.wait_ge(s_ug, IC * i + ic + 1)
                                act.wait_ge(s_h, IC * i + ic + 1)
                                act.activation(gated[ic % 2][:, :], ps_g[ic % 2][:, :], ACT.Silu).then_inc(s_silu, 1)
                            if ic > 0:
                                act.wait_ge(s_h, 2 + IC * i + ic)
                                act.copy(hT[b % 2][:, 0, ic - 1, :], hid[(ic - 1) % 2][:, :]).then_inc(s_hhi, 1)

                every(act, unit)

            @block.gpsimd
            def _(pool):
                def unit(u, par, last):
                    for b in range(B):
                        i = u * B + b
                        for ic in range(IC):
                            pool.wait_ge(s_hhi, IC * i + ic + 1)
                            pool.tensor_tensor(hT[b % 2][:, 1, ic, :], hid[ic % 2][:, :],
                                               hT[b % 2][:, 0, ic, :].bitcast(F32), ALU.subtract).then_inc(s_hlo, 1)

                pool.sem_inc(s_hlo, 2)
                every(pool, unit)

            @block.vector
            def _(dve):
                def split_w(u, par):
                    dve.wait_ge(s_wraw, 48 * (u + 1))
                    dve.tensor_copy(w[par][:, 0, :], raw[:, :]).then_inc(s_whi, 1)
                    dve.wait_ge(s_whi, u + 1)
                    dve.tensor_tensor(w[par][:, 1, :], raw[:, :], w[par][:, 0, :].bitcast(F32),
                                      ALU.subtract).then_inc(s_wsplit, 1)

                def hidden(u, b):
                    i = u * B + b
                    for ic in range(IC):
                        dve.wait_ge(s_silu, IC * i + ic + 1)
                        dve.wait_ge(s_hlo, IC * i + ic + 1)
                        dve.tensor_tensor(hid[ic % 2][:, :], ps_u[ic % 2][:, :], gated[ic % 2][:, :],
                                          ALU.mult).then_inc(s_h, 1)

                dve.sem_inc(s_h, 2)
                dve.sem_inc(s_yadd, TB)
                if split:
                    split_w(0, 0)
                hidden(0, 0)
                dve.wait_ge(s_x, 16 + 16 * (shares is not None))

                def unit(u, par, last):
                    for b in range(B):
                        i = u * B + b
                        if b < B - 1:
                            hidden(u, b + 1)
                        elif not last:
                            hidden(u + 1, 0)
                        for t in range(TB):
                            dve.wait_ge(s_y, TB * i + t + 1)
                            row = xs[:, b * TB + t, :]
                            if shares is None:
                                ins = dve.tensor_tensor(row, ps_y[t][:, :], row, ALU.add)
                            else:
                                ins = dve.scalar_tensor_tensor(row, ps_y[t][:, :], share_sb[:, b * TB + t, bass.ds(u, 1)],
                                                               row, ALU.mult, ALU.add)
                            ins.then_inc(s_yadd, 1)
                        if split and b == 0 and not last:
                            split_w(u + 1, 1 - par)

                every(dve, unit)


def hadamard_sign(i, j):
    return -1 if bin(i & j).count("1") % 2 else 1


def stage_ffn_weights(nc, wT, W_gate, W_up, W_down, Wscale_ug, Wscale_dp, SU_dp, ident, had):
    INTER = W_gate.shape[0]
    CH, NB = 512, INTER // P
    CHUNKS = INTER // CH
    PART = KD * CH
    srcs = [(W_gate, INTER), (W_up, 0)]
    with Scope(nc, "ffw") as m:
        ident_sb = m.sb("ident", [P, P])
        had_f = m.sb("had_f", [P, P])
        had_r = m.sb("had", [P, P], F32R)
        scales = m.sb("scales", [P, 2 * NB])
        dscale = m.sb("dscale", [P, KD])
        su = m.sb("su", [P, NB])
        raw = [m.sb(f"raw{t}", [P, DIM]) for t in range(TB)]
        scaled = [m.sb(f"scaled{t}", [P, DIM]) for t in range(TB)]
        outT = m.sb("outT", [P, 2, KD, CH], F32R)
        dn = [m.sb(f"down{i}", [P, KD, INTER]) for i in range(2)]
        dT = [m.sb(f"downT{i}", [P, 2, DIM], F32R) for i in range(2)]
        dout = [m.sb(f"dout{i}", [P, 2, 4, DIM], F32R) for i in range(2)]
        banks = [m.ps(f"bank{t}", [P, KD, P]) for t in range(TB)]
        tb = [m.ps(f"turn{i}", [P, DIM]) for i in range(2)]
        hb = [m.ps(f"rot{i}", [P, DIM]) for i in range(2)]

        s_const = m.sem("const_in")
        s_raw = [m.sem(f"raw_in{t}") for t in range(TB)]
        s_scaled = m.sem("scaled")
        s_tr = m.sem("transposed")
        s_hi = m.sem("hi")
        s_lo = m.sem("lo")
        s_out = m.sem("stored")
        s_dn, s_bf = m.sem("down_in"), m.sem("butterflies")
        s_had = m.sem("had_rounded")
        s_dt, s_dthi, s_dtlo = m.sem("downT"), m.sem("downT_hi"), m.sem("downT_lo")
        s_dr, s_drhi, s_drlo = m.sem("rotated"), m.sem("rotated_hi"), m.sem("rotated_lo")
        s_dout = [m.sem(f"down_stored{i}") for i in range(2)]

        with m.block() as block:
            @block.sync
            def _(sp):
                sp.sem_inc(s_out, 16)
                sp.dma_start(dn[0][:, :, :], W_down.rearrange("(k p) n -> p k n", p=P)).then_inc(s_dn, 16)
                sp.dma_start(dscale[:, :], Wscale_dp.rearrange("(k p) -> p k", p=P), allow_slow_non_contiguous=True).then_inc(s_dn, 16)
                sp.dma_start(ident_sb[:, :], ident).then_inc(s_const, 16)
                sp.dma_start(had_f[:, :], had).then_inc(s_const, 16)
                sp.dma_start(scales[:, :], Wscale_ug.rearrange("(n p) -> p n", p=P), allow_slow_non_contiguous=True).then_inc(s_const, 16)
                sp.dma_start(su[:, :], SU_dp.rearrange("(n p) -> p n", p=P), allow_slow_non_contiguous=True).then_inc(s_const, 16)
                for n, (src, _) in enumerate(srcs):
                    rows = src.rearrange("(c t p) d -> c t p d", c=CHUNKS, t=TB)
                    with sp.Fori(0, CHUNKS) as c:
                        i = c + n * CHUNKS
                        for t in range(TB):
                            sp.wait_ge(s_scaled, i * TB + t + 1)
                            sp.dma_start(raw[t][:, :], rows[c, t]).then_inc(s_raw[t], 16)
                        sp.wait_ge(s_lo, (i + 2) * TB)
                        sp.dma_start(wT[c, :, :, n * PART:(n + 1) * PART],
                                     outT[:, :, :, :].bitcast(F32).rearrange("p s k n -> p s (k n)")).then_inc(s_out, 16)
                for c in range(CHUNKS):
                    sp.wait_ge(s_drlo, 4 * (c + 1))
                    sp.dma_start(wT[c, :, :, 2 * PART:3 * PART],
                                 dout[c % 2][:, :, :, :].bitcast(F32).rearrange("p s k n -> p s (k n)")).then_inc(s_dout[c % 2], 16)
                sp.wait_ge(s_out, 16 * (2 * CHUNKS + 1))
                for i in range(2):
                    sp.wait_ge(s_dout[i], 16 * CHUNKS // 2)

            @block.gpsimd
            def _(pool):
                pool.wait_ge(s_dn, 32)
                for k in range(KD):
                    pool.tensor_scalar(dn[0][:, k, :], dn[0][:, k, :], dscale[:, k:k + 1], INTER ** -0.5,
                                       ALU.mult, ALU.mult).then_inc(s_bf, 1)
                done = KD
                for stage in range(NB.bit_length() - 1):
                    src, dst = dn[stage % 2], dn[1 - stage % 2]
                    width = P << stage
                    s_v, d_v = (x[:, :, :].rearrange("p k (g two w) -> p (k g) two w", two=2, w=width) for x in (src, dst))
                    pool.wait_ge(s_bf, done)
                    for two, op in ((0, ALU.add), (1, ALU.subtract)):
                        pool.tensor_tensor(d_v[:, :, two, :], s_v[:, :, 0, :], s_v[:, :, 1, :], op).then_inc(s_bf, 1)
                    done += 2

            @block.vector
            def _(dve):
                dve.sem_inc(s_scaled, TB)
                dve.sem_inc(s_lo, TB)
                dve.wait_ge(s_const, 64)
                dve.tensor_copy(had_r[:, :], had_f[:, :]).then_inc(s_had, 1)
                for n, (_, at) in enumerate(srcs):
                    with dve.Fori(0, CHUNKS) as c:
                        i = c + n * CHUNKS
                        for t in range(TB):
                            dve.wait_ge(s_raw[t], (i + 1) * 16)
                            dve.wait_ge(s_tr, i * TB + t + 1)
                            dve.tensor_scalar(scaled[t][:, :], raw[t][:, :], scales[:, bass.ds(c * TB + (at // P + t), 1)],
                                              None, ALU.mult).then_inc(s_scaled, 1)
                        for t in range(TB):
                            cols = slice(t * P, (t + 1) * P)
                            dve.wait_ge(s_hi, i * TB + t + 1)
                            dve.tensor_tensor(outT[:, 1, :, cols], banks[t][:, :, :], outT[:, 0, :, cols].bitcast(F32),
                                              ALU.subtract).then_inc(s_lo, 1)

                def turned_lo(a):
                    dve.wait_ge(s_dthi, a + 1)
                    dve.tensor_tensor(dT[a % 2][:, 1, :], tb[a % 2][:, :], dT[a % 2][:, 0, :].bitcast(F32),
                                      ALU.subtract).then_inc(s_dtlo, 1)

                def rotated_lo(a):
                    dve.wait_ge(s_drhi, a + 1)
                    o = dout[a // 4 % 2]
                    dve.scalar_tensor_tensor(o[:, 1, a % 4, :], hb[a % 2][:, :], su[:, a:a + 1],
                                             o[:, 0, a % 4, :].bitcast(F32), ALU.mult, ALU.subtract).then_inc(s_drlo, 1)

                turned_lo(0)
                for a in range(NB):
                    if a + 1 < NB:
                        turned_lo(a + 1)
                    rotated_lo(a)

            @block.tensor
            def _(pe):
                pe.sem_inc(s_tr, TB)
                pe.wait_ge(s_const, 64)
                for n in range(2):
                    with pe.Fori(0, CHUNKS) as c:
                        i = c + n * CHUNKS
                        for t in range(TB):
                            pe.wait_ge(s_scaled, (i + 1) * TB + t + 1)
                            pe.wait_ge(s_lo, i * TB + t + 1)
                            for k in range(KD):
                                tr = pe.transpose(banks[t][:, k, :], scaled[t][:, k * P:(k + 1) * P], ident_sb[:, :])
                            tr.then_inc(s_tr, 1)
                dsrc = dn[(NB.bit_length() - 1) % 2]
                pe.wait_ge(s_bf, KD + 2 * (NB.bit_length() - 1))
                pe.wait_ge(s_had, 1)

                def turn(a):
                    if a >= 2:
                        pe.wait_ge(s_dtlo, a - 1)
                    for k in range(KD):
                        tr = pe.transpose(tb[a % 2][:, k * P:(k + 1) * P], dsrc[:, k, a * P:(a + 1) * P], ident_sb[:, :])
                    tr.then_inc(s_dt, 1)

                turn(0)
                for a in range(NB):
                    if a + 1 < NB:
                        turn(a + 1)
                    pe.wait_ge(s_dtlo, a + 1)
                    if a >= 2:
                        pe.wait_ge(s_drlo, a - 1)
                    pe.matmul(hb[a % 2][:, :], had_r[:, :], dT[a % 2][:, 0, :], start=True, stop=False)
                    pe.matmul(hb[a % 2][:, :], had_r[:, :], dT[a % 2][:, 1, :], start=False, stop=True).then_inc(s_dr, 1)

            @block.scalar
            def _(act):
                for n in range(2):
                    with act.Fori(0, CHUNKS) as c:
                        i = c + n * CHUNKS
                        act.wait_ge(s_out, 16 * (i + 1))
                        for t in range(TB):
                            act.wait_ge(s_tr, (i + 1) * TB + t + 1)
                            act.copy(outT[:, 0, :, t * P:(t + 1) * P], banks[t][:, :, :]).then_inc(s_hi, 1)

                def turned_hi(a):
                    act.wait_ge(s_dt, a + 1)
                    if a >= 2:
                        act.wait_ge(s_dr, a - 1)
                    act.copy(dT[a % 2][:, 0, :], tb[a % 2][:, :]).then_inc(s_dthi, 1)

                def rotated_hi(a):
                    act.wait_ge(s_dr, a + 1)
                    if a >= 8 and a % 4 == 0:
                        act.wait_ge(s_dout[a // 4 % 2], 16 * (a // 8))
                    act.activation(dout[a // 4 % 2][:, 0, a % 4, :], hb[a % 2][:, :], ACT.Copy,
                                   scale=su[:, a:a + 1]).then_inc(s_drhi, 1)

                turned_hi(0)
                for a in range(NB):
                    if a + 1 < NB:
                        turned_hi(a + 1)
                    rotated_hi(a)


def stage_rotate(nc, xT, uT, SU, had):
    with Scope(nc, "rot") as m:
        had_f = m.sb("had_f", [P, P])
        su = m.sb("su", [P, KD])
        hs_f = m.sb("hs_f", [P, 2, KD, P])
        hs = m.sb("hs", [P, 2, 2, KD, P], F32R)
        xin = [m.sb(f"x{i}", [P, 2, KD, S], F32R) for i in range(2)]
        out = [m.sb(f"out{i}", [P, 2, KD, S], F32R) for i in range(2)]
        banks = [m.ps(f"bank{k}", [P, S]) for k in range(KD)]
        s_const, s_x = m.sem("const_in"), [m.sem(f"x_in{i}") for i in range(2)]
        s_dve = m.sem("dve_steps")
        s_r, s_hi, s_lo = m.sem("rotated"), m.sem("hi"), m.sem("lo")
        s_out = [m.sem(f"stored{i}") for i in range(2)]
        SC = DIM ** -0.5
        with m.block() as block:
            @block.sync
            def _(sp):
                sp.dma_start(had_f[:, :], had).then_inc(s_const, 16)
                sp.dma_start(su[:, :], SU.rearrange("(k p) -> p k", p=P), allow_slow_non_contiguous=True).then_inc(s_const, 16)
                for b in range(2):
                    sp.dma_start(xin[b][:, :, :, :].bitcast(F32), xT[b]).then_inc(s_x[b], 16)
                for b in range(B):
                    if b + 2 < B:
                        sp.wait_ge(s_r, KD * (b + 1))
                        sp.dma_start(xin[b % 2][:, :, :, :].bitcast(F32), xT[b + 2]).then_inc(s_x[b % 2], 16)
                    sp.wait_ge(s_lo, KD * (b + 1))
                    sp.dma_start(uT[b], out[b % 2][:, :, :, :].bitcast(F32)).then_inc(s_out[b % 2], 16)
                for i in range(2):
                    sp.wait_ge(s_out[i], 16 * B // 2)

            @block.vector
            def _(dve):
                own = Steps(dve, s_dve)
                dve.wait_ge(s_const, 32)
                for k in range(KD):
                    own.mark(dve.tensor_scalar(hs_f[:, 0, k, :], had_f[:, :], su[:, k:k + 1], None, ALU.mult))
                    own.mark(dve.tensor_scalar(hs_f[:, 1, k, :], had_f[:, :], su[:, k:k + 1], -1.0, ALU.mult, ALU.mult))
                own.wait()
                own.after(dve.tensor_copy(hs[:, 0, :, :, :], hs_f[:, :, :, :]))
                own.after(dve.tensor_tensor(hs[:, 1, :, :, :], hs_f[:, :, :, :], hs[:, 0, :, :, :].bitcast(F32), ALU.subtract))
                for b in range(B):
                    for k in range(KD):
                        dve.wait_ge(s_hi, KD * b + k + 1)
                        dve.scalar_tensor_tensor(out[b % 2][:, 1, k, :], banks[k][:, :], SC,
                                                 out[b % 2][:, 0, k, :].bitcast(F32), ALU.mult, ALU.subtract).then_inc(s_lo, 1)

            @block.tensor
            def _(pe):
                pe.wait_ge(s_dve, 2 * KD + 2)
                for b in range(B):
                    pe.wait_ge(s_x[b % 2], 16 * (b // 2 + 1))
                    for ko in range(KD):
                        if b > 0:
                            pe.wait_ge(s_lo, KD * (b - 1) + ko + 1)
                        for k in range(KD):
                            g = 0 if hadamard_sign(k, ko) > 0 else 1
                            mm = split_product(pe, banks[ko][:, :], (hs[:, 0, g, k, :], hs[:, 1, g, k, :]),
                                               (xin[b % 2][:, 0, k, :], xin[b % 2][:, 1, k, :]), k == 0, k == KD - 1)
                        mm.then_inc(s_r, 1)

            @block.scalar
            def _(act):
                for b in range(B):
                    if b >= 2:
                        act.wait_ge(s_out[b % 2], 16 * (b // 2))
                    for k in range(KD):
                        act.wait_ge(s_r, KD * b + k + 1)
                        act.activation(out[b % 2][:, 0, k, :], banks[k][:, :], ACT.Copy, scale=SC).then_inc(s_hi, 1)


STATES = 16
RANK = 16
ET = DIM // P


def stage_ssm_inputs(nc, ctxT, in_proj, conv_w, conv_b, x_proj, dt_proj, dt_bias, u_d, delta_d, du_d, bc_d, ident):
    NX = RANK + 2 * STATES
    TAPS = conv_w.shape[1]
    PAD = TAPS - 1
    with Scope(nc, "ssi") as m:
        ident_sb = m.sb("ident", [P, P])
        in_raw = m.sb("in_raw", [P, ET, CD])
        x_raw = m.sb("x_raw", [NX, DIM])
        dt_raw = m.sb("dt_raw", [P, ET, RANK])
        inT = m.sb("inT", [P, 2, KC, DIM], F32R)
        xT = m.sb("xT", [P, ET, NX])
        dtT = m.sb("dtT", [RANK, DIM])
        taps = m.sb("taps", [P, ET, TAPS])
        cb = m.sb("conv_b", [P, ET])
        db = m.sb("dt_b", [P, ET])
        cx = m.sb("cx", [P, 2, KC, S], F32R)
        xp = [m.sb(f"xp{i}", [P, PAD + S]) for i in range(2)]
        conv = [m.sb(f"conv{i}", [P, S]) for i in range(2)]
        u = m.sb("u", [P, ET, S])
        dbl = m.sb("dbl", [NX, S])
        mag = m.sb("mag", [P, ET, S])
        ex = m.sb("ex", [P, ET, S])
        soft = m.sb("soft", [P, ET, S])
        relu = m.sb("relu", [P, ET, S])
        delta = m.sb("delta", [P, ET, S])
        du = m.sb("du", [P, ET, S])
        ps_t = m.ps("turn", [P, 512])
        ps_x = [m.ps(f"x{i}", [P, S]) for i in range(2)]
        ps_d = m.ps("dbl_ps", [P, S])
        ps_z = [m.ps(f"z{i}", [P, S]) for i in range(ET)]

        s_in = m.sem("weights_in")
        s_t = m.sem("turned")
        s_te = m.sem("turned_out")
        s_tl = m.sem("turned_lo")
        s_cx = m.sem("cx_in")
        s_x, s_xp = m.sem("x"), m.sem("x_padded")
        s_conv, s_u = m.sem("conv"), m.sem("u")
        s_dve = m.sem("dve_steps")
        s_d, s_dbl = m.sem("dbl_made"), m.sem("dbl_copied")
        s_z, s_mag, s_ex, s_soft = m.sem("z"), m.sem("mag_done"), m.sem("exp_done"), m.sem("ln_done")
        s_relu, s_delta, s_du = m.sem("relu_done"), m.sem("delta_done"), m.sem("du_done")
        s_st = [m.sem(f"stored{i}") for i in range(4)]
        with m.block() as block:
            @block.sync
            def _(sp):
                sp.dma_start(ident_sb[:, :], ident).then_inc(s_in, 16)
                sp.dma_start(in_raw[:, :, :], in_proj.rearrange("(t p) d -> p t d", p=P)).then_inc(s_in, 16)
                sp.dma_start(x_raw[:, :], x_proj).then_inc(s_in, 16)
                sp.dma_start(dt_raw[:, :, :], dt_proj.rearrange("(t p) r -> p t r", p=P)).then_inc(s_in, 16)
                sp.dma_start(taps[:, :, :], conv_w.rearrange("(t p) r -> p t r", p=P)).then_inc(s_in, 16)
                sp.dma_start(cb[:, :], conv_b.rearrange("(t p) -> p t", p=P), allow_slow_non_contiguous=True).then_inc(s_in, 16)
                sp.dma_start(db[:, :], dt_bias.rearrange("(t p) -> p t", p=P), allow_slow_non_contiguous=True).then_inc(s_in, 16)
                sp.dma_start(cx[:, :, :, :].bitcast(F32), ctxT[0]).then_inc(s_cx, 16)
                for b in range(B):
                    if b + 1 < B:
                        sp.wait_ge(s_x, ET * (b + 1))
                        sp.dma_start(cx[:, :, :, :].bitcast(F32), ctxT[b + 1]).then_inc(s_cx, 16)
                    sp.wait_ge(s_dbl, b + 1)
                    sp.dma_start(bc_d[b], dbl[RANK:NX, :]).then_inc(s_st[0], 16)
                    sp.wait_ge(s_u, ET * (b + 1))
                    sp.dma_start(u_d[b], u[:, :, :]).then_inc(s_st[1], 16)
                    sp.wait_ge(s_delta, b + 1)
                    sp.dma_start(delta_d[b], delta[:, :, :]).then_inc(s_st[2], 16)
                    sp.wait_ge(s_du, b + 1)
                    sp.dma_start(du_d[b], du[:, :, :]).then_inc(s_st[3], 16)
                for q in s_st:
                    sp.wait_ge(q, 16 * B)

            @block.tensor
            def _(pe):
                pe.wait_ge(s_in, 16 * 7)
                for k in range(KC):
                    if k:
                        pe.wait_ge(s_tl, k)
                    for t in range(ET):
                        tr = pe.transpose(ps_t[:, t * P:(t + 1) * P], in_raw[:, t, k * P:(k + 1) * P], ident_sb[:, :])
                    tr.then_inc(s_t, 1)
                pe.wait_ge(s_tl, KC)
                for t in range(ET):
                    tr = pe.transpose(ps_t[:, t * NX:(t + 1) * NX], x_raw[:, t * P:(t + 1) * P], ident_sb[0:NX, 0:NX])
                tr.then_inc(s_t, 1)
                pe.wait_ge(s_te, KC + 1)
                for t in range(ET):
                    tr = pe.transpose(ps_t[0:RANK, t * P:(t + 1) * P], dt_raw[:, t, :], ident_sb[:, :])
                tr.then_inc(s_t, 1)
                pe.wait_ge(s_te, KC + 2)
                for b in range(B):
                    pe.wait_ge(s_cx, 16 * (b + 1))
                    for t in range(ET):
                        n = b * ET + t
                        if n >= 2:
                            pe.wait_ge(s_xp, n - 1)
                        cols = slice(t * P, (t + 1) * P)
                        for k in range(KC):
                            mm = split_product(pe, ps_x[n % 2][:, :], (inT[:, 0, k, cols], inT[:, 1, k, cols]),
                                               (cx[:, 0, k, :], cx[:, 1, k, :]), k == 0, k == KC - 1)
                        mm.then_inc(s_x, 1)
                    if b:
                        pe.wait_ge(s_dbl, b)
                    for t in range(ET):
                        pe.wait_ge(s_u, b * ET + t + 1)
                        mm = pe.matmul(ps_d[0:NX, :], xT[:, t, :], u[:, t, :], start=(t == 0), stop=(t == ET - 1))
                    mm.then_inc(s_d, 1)
                    pe.wait_ge(s_dbl, b + 1)
                    for t in range(ET):
                        if b:
                            pe.wait_ge(s_relu, b)
                            pe.wait_ge(s_mag, ET * b)
                        pe.matmul(ps_z[t][:, :], dtT[:, t * P:(t + 1) * P], dbl[0:RANK, :], start=True,
                                  stop=True).then_inc(s_z, 1)

            @block.scalar
            def _(act):
                for k in range(KC):
                    act.wait_ge(s_t, k + 1)
                    act.copy(inT[:, 0, k, :], ps_t[:, :]).then_inc(s_te, 1)
                act.wait_ge(s_t, KC + 1)
                act.copy(xT[:, :, :], ps_t[:, 0:ET * NX].rearrange("p (t n) -> p t n", t=ET)).then_inc(s_te, 1)
                act.wait_ge(s_t, KC + 2)
                act.copy(dtT[:, :], ps_t[0:RANK, :]).then_inc(s_te, 1)
                act.wait_ge(s_dve, 2)
                for b in range(B):
                    for t in range(ET + 1):
                        n = b * ET + t
                        if t < ET:
                            act.wait_ge(s_x, n + 1)
                            if n >= 2:
                                act.wait_ge(s_conv, n - 1)
                            act.copy(xp[n % 2][:, PAD:], ps_x[n % 2][:, :]).then_inc(s_xp, 1)
                        if t > 0:
                            act.wait_ge(s_conv, n)
                            if b:
                                act.wait_ge(s_st[1], 16 * b)
                                act.wait_ge(s_du, b)
                            act.activation(u[:, t - 1, :], conv[(n - 1) % 2][:, :], ACT.Silu,
                                           bias=cb[:, t - 1:t]).then_inc(s_u, 1)
                    act.wait_ge(s_d, b + 1)
                    if b:
                        act.wait_ge(s_st[0], 16 * b)
                        act.wait_ge(s_z, ET * b)
                    act.copy(dbl[:, :], ps_d[0:NX, :]).then_inc(s_dbl, 1)
                    for t in range(ET):
                        act.wait_ge(s_z, ET * b + t + 1)
                        act.activation(mag[:, t, :], ps_z[t][:, :], ACT.Abs, bias=db[:, t:t + 1]).then_inc(s_mag, 1)
                    act.wait_ge(s_mag, ET * (b + 1))
                    act.activation(ex[:, :, :], mag[:, :, :], ACT.Exp, scale=-1.0).then_inc(s_ex, 1)
                    act.wait_ge(s_ex, b + 1)
                    if b:
                        act.wait_ge(s_delta, b)
                    act.activation(soft[:, :, :], ex[:, :, :], ACT.Ln, bias=1.0).then_inc(s_soft, 1)

            @block.vector
            def _(dve):
                own = Steps(dve, s_dve)
                for i in range(2):
                    own.mark(dve.memset(xp[i][:, 0:PAD], 0.0))
                for k in range(KC):
                    dve.wait_ge(s_te, k + 1)
                    dve.tensor_tensor(inT[:, 1, k, :], ps_t[:, :], inT[:, 0, k, :].bitcast(F32), ALU.subtract).then_inc(s_tl, 1)
                for b in range(B):
                    for t in range(ET):
                        n = b * ET + t
                        dve.wait_ge(s_xp, n + 1)
                        if n >= 2:
                            dve.wait_ge(s_u, n - 1)
                        c, x = conv[n % 2], xp[n % 2]
                        own.after(dve.tensor_scalar(c[:, :], x[:, 0:S], taps[:, t, 0:1], None, ALU.mult))
                        for j in range(1, TAPS):
                            ins = dve.scalar_tensor_tensor(c[:, :], x[:, j:j + S], taps[:, t, j:j + 1], c[:, :],
                                                           ALU.mult, ALU.add)
                            if j < TAPS - 1:
                                own.after(ins)
                        ins.then_inc(s_conv, 1)
                    dve.wait_ge(s_mag, ET * (b + 1))
                    if b:
                        dve.wait_ge(s_delta, b)
                    for t in range(ET):
                        ins = dve.tensor_scalar(relu[:, t, :], ps_z[t][:, :], db[:, t:t + 1], 0.0, ALU.add, ALU.max)
                    ins.then_inc(s_relu, 1)
                    dve.wait_ge(s_relu, b + 1)
                    dve.wait_ge(s_soft, b + 1)
                    if b:
                        dve.wait_ge(s_st[2], 16 * b)
                        dve.wait_ge(s_st[3], 16 * b)
                    dve.tensor_tensor(delta[:, :, :], relu[:, :, :], soft[:, :, :], ALU.add).then_inc(s_delta, 1)
                    dve.wait_ge(s_delta, b + 1)
                    dve.tensor_tensor(du[:, :, :], delta[:, :, :], u[:, :, :], ALU.mult).then_inc(s_du, 1)


def stage_ssm_scan(nc, A_log, delta_d, du_d, bc_d, y_d, ident):
    A_v = A_log.rearrange("(t p) n -> p t n", p=P)
    GROUP = 4
    RING = 4
    UNITS = B * ET
    with Scope(nc, "scan") as m:
        ident_sb = m.sb("ident", [P, P])
        a_log = m.sb("a_log", [P, ET, STATES])
        a_exp = m.sb("a_exp", [P, ET, STATES])
        a = m.sb("a", [P, ET * STATES])
        delta = m.sb("delta", [P, 2, ET, S])
        du = m.sb("du", [P, 2, ET, S])
        rows = m.sb("rows", [P, 2, STATES, S])
        decay = [m.sb(f"decay{i}", [P, S]) for i in range(RING)]
        drive = [m.sb(f"drive{i}", [P, S]) for i in range(RING)]
        state = [m.sb(f"state{i}", [P, S]) for i in range(2)]
        term = [m.sb(f"term{i}", [P, S]) for i in range(RING)]
        y = m.sb("y", [P, 2, ET, S])
        ps_y = m.ps("y_ps", [P, 2, S])
        s_in, s_aexp, s_a, s_id = m.sem("in"), m.sem("a_exp_done"), m.sem("a_done"), m.sem("ident_in")
        s_ld = m.sem("batch_in")
        s_rows = [m.sem(f"rows_in{i}") for i in range(STATES // GROUP)]
        s_decay, s_drive, s_state = m.sem("decay_done"), m.sem("drive_done"), m.sem("state_done")
        s_term, s_sum, s_y, s_st = m.sem("term_done"), m.sem("summed"), m.sem("y_out"), m.sem("stored")
        s_pace = m.sem("pace")
        N = STATES * ET
        with m.block() as block:
            @block.sync
            def _(sp):
                sp.sem_inc(s_st, 32)
                sp.dma_start(a_log[:, :, :], A_v).then_inc(s_in, 16)
                sp.dma_start(ident_sb[:, :], ident).then_inc(s_id, 16)

                def batch(b, first):
                    if not first:
                        wait_apart(sp, s_ld, 32 * b, s_pace)
                        wait_apart(sp, s_state, RING + N * (b - 1), s_pace)
                    sp.dma_start(delta[:, b % 2], delta_d[b]).then_inc(s_ld, 16)
                    sp.dma_start(du[:, b % 2], du_d[b]).then_inc(s_ld, 16)
                    for g in range(STATES // GROUP):
                        if not first:
                            last = N * b - STATES + (g + 1) * GROUP
                            wait_apart(sp, s_drive, last, s_pace)
                            wait_apart(sp, s_term, 2 + last, s_pace)
                        for j in range(2):
                            at = j * STATES + g * GROUP
                            src = bc_d[b, at:at + GROUP, :].rearrange("(a n) s -> a n s", a=1)
                            sp.dma_start(rows[:, j, g * GROUP:(g + 1) * GROUP, :],
                                         src.to_broadcast([P, GROUP, S])).then_inc(s_rows[g], 16)
                    if not first:
                        wait_apart(sp, s_y, 2 + ET * b, s_pace)
                        wait_apart(sp, s_st, 16 * (b + 1), s_pace)
                        sp.dma_start(y_d[b - 1], y[:, (b + 1) % 2]).then_inc(s_st, 16)

                batch(0, True)
                with sp.Fori(1, B) as b:
                    batch(b, False)
                sp.wait_ge(s_y, 2 + ET * B)
                sp.wait_ge(s_st, 16 * (B + 1))
                sp.dma_start(y_d[B - 1], y[:, (B - 1) % 2]).then_inc(s_st, 16)
                sp.wait_ge(s_st, 16 * (B + 2))

            @block.scalar
            def _(act):
                act.sem_inc(s_y, 2)
                act.wait_ge(s_in, 16)
                act.activation(a_exp[:, :, :], a_log[:, :, :], ACT.Exp).then_inc(s_aexp, 1)
                act.wait_ge(s_aexp, 1)
                act.mul(a[:, :], a_exp[:, :, :].rearrange("p t n -> p (t n)"), -1.0).then_inc(s_a, 1)
                act.wait_ge(s_a, 1)

                def unit(i, first):
                    b, t = i // ET, i % ET
                    act.wait_ge(s_ld, 32 * (b + 1))
                    for n in range(STATES):
                        wait_apart(act, s_state, i * STATES + n + 1, s_pace)
                        act.activation(decay[n % RING][:, :], delta[:, b % 2, t, :], ACT.Exp,
                                       scale=a[:, bass.ds(t * STATES + n, 1)]).then_inc(s_decay, 1)
                        if n == 1 and not first:
                            flush(i - 1)

                def flush(i):
                    b, t = i // ET, i % ET
                    act.wait_ge(s_st, 16 * (b + 1))
                    wait_apart(act, s_sum, RING + (i + 1) * STATES, s_pace)
                    act.copy(y[:, b % 2, t, :], ps_y[:, i % 2, :]).then_inc(s_y, 1)

                unit(0, True)
                with act.Fori(1, UNITS) as i:
                    unit(i, False)
                flush(UNITS - 1)

            @block.gpsimd
            def _(pool):
                with pool.Fori(0, UNITS) as i:
                    b, t = i // ET, i % ET
                    pool.wait_ge(s_ld, 32 * (b + 1))
                    for n in range(STATES):
                        if n % GROUP == 0:
                            pool.wait_ge(s_rows[n // GROUP], 32 * (b + 1))
                        wait_apart(pool, s_state, i * STATES + n + 1, s_pace)
                        pool.tensor_tensor(drive[n % RING][:, :], du[:, b % 2, t, :], rows[:, 0, n, :],
                                           ALU.mult).then_inc(s_drive, 1)

            @block.vector
            def _(dve):
                dve.sem_inc(s_state, RING)
                dve.sem_inc(s_term, 2)

                def product(q, n):
                    dve.wait_ge(s_state, RING + q + 1)
                    dve.wait_ge(s_sum, q + 1)
                    dve.tensor_tensor(term[n % RING][:, :], state[n % 2][:, :], rows[:, 1, n, :],
                                      ALU.mult).then_inc(s_term, 1)

                def unit(i, first):
                    for n in range(STATES):
                        q = i * STATES + n
                        dve.wait_ge(s_decay, q + 1)
                        dve.wait_ge(s_drive, q + 1)
                        dve.wait_ge(s_term, q + 1)
                        dve.tensor_tensor_scan(state[n % 2][:, :], decay[n % RING][:, :], drive[n % RING][:, :], 0.0,
                                               ALU.mult, ALU.add).then_inc(s_state, 1)
                        if n or not first:
                            product(q - 1, (n - 1) % STATES)

                unit(0, True)
                with dve.Fori(1, UNITS) as i:
                    unit(i, False)
                product(UNITS * STATES - 1, STATES - 1)

            @block.tensor
            def _(pe):
                pe.sem_inc(s_sum, RING)
                pe.wait_ge(s_id, 16)
                with pe.Fori(0, UNITS) as i:
                    pe.wait_ge(s_y, i + 1)
                    for n in range(STATES):
                        pe.wait_ge(s_term, 2 + i * STATES + n + 1)
                        pe.matmul(ps_y[:, i % 2, :], ident_sb[:, :], term[n % RING][:, :], start=(n == 0),
                                  stop=(n == STATES - 1)).then_inc(s_sum, 1)


def stage_ssm_gate(nc, x, out, u_d, y_d, skip, ident):
    xr = x.rearrange("(b t p) d -> b p t d", b=B, t=TB)
    outr = out.rearrange("(b t p) d -> b p t d", b=B, t=TB)
    with Scope(nc, "gate") as m:
        ident_sb = m.sb("ident", [P, P])
        d = m.sb("skip", [P, ET])
        rows = [m.sb(f"rows{i}", [P, TB, DIM]) for i in range(2)]
        u = [m.sb(f"u{i}", [P, ET, S]) for i in range(2)]
        y = [m.sb(f"y{i}", [P, ET, S]) for i in range(2)]
        silu = m.sb("silu", [P, TB, DIM])
        gated = m.sb("gated", [P, ET, S])
        res = m.sb("res", [P, TB, DIM])
        stats = m.sb("stats", [P, TB, 6])
        meanvar = m.sb("meanvar", [P, TB, 2])
        var_eps = m.sb("var_eps", [P, TB])
        rstd = m.sb("rstd", [P, TB])
        shift = m.sb("shift", [P, TB])
        guess = m.sb("guess", [P, TB])
        work = m.sb("work", [P, TB])
        banks = [m.ps(f"bank{t}", [P, ET, P]) for t in range(TB)]
        s_in = m.sem("in")
        s_ld = [m.sem(f"batch_in{i}") for i in range(2)]
        s_dve, s_shift, s_silu = m.sem("dve_steps"), m.sem("shift_done"), m.sem("silu_done")
        s_g, s_t, s_res, s_st = m.sem("gated_done"), m.sem("turned"), m.sem("res_done"), m.sem("stored")
        with m.block() as block:
            @block.sync
            def _(sp):
                sp.dma_start(ident_sb[:, :], ident).then_inc(s_in, 16)
                sp.dma_start(d[:, :], skip.rearrange("(t p) -> p t", p=P), allow_slow_non_contiguous=True).then_inc(s_in, 16)
                for b in range(B):
                    if b >= 2:
                        sp.wait_ge(s_res, TB * (b - 1))
                    sp.dma_start(rows[b % 2][:, :, :], xr[b]).then_inc(s_ld[b % 2], 16)
                    sp.dma_start(u[b % 2][:, :, :], u_d[b]).then_inc(s_ld[b % 2], 16)
                    sp.dma_start(y[b % 2][:, :, :], y_d[b]).then_inc(s_ld[b % 2], 16)
                    if b:
                        sp.wait_ge(s_res, TB * b)
                        sp.dma_start(outr[b - 1], res[:, :, :]).then_inc(s_st, 16)
                sp.wait_ge(s_res, TB * B)
                sp.dma_start(outr[B - 1], res[:, :, :]).then_inc(s_st, 16)
                sp.wait_ge(s_st, 16 * B)

            @block.vector
            def _(dve):
                own = Steps(dve, s_dve)
                dve.wait_ge(s_in, 32)
                for b in range(B):
                    dve.wait_ge(s_ld[b % 2], 48 * (b // 2 + 1))
                    for t in range(TB):
                        own.mark(dve.bn_stats(stats[:, t, :], rows[b % 2][:, t, :]))
                    own.wait()
                    for t in range(TB):
                        own.mark(dve.bn_aggr(meanvar[:, t, :], stats[:, t, :]))
                    own.wait()
                    own.after(dve.tensor_scalar(var_eps[:, :], meanvar[:, :, 1], LN_EPS, None, ALU.add))
                    newton_rsqrt(dve, own, rstd[:, :], var_eps[:, :], guess[:, :], work[:, :])
                    dve.scalar_tensor_tensor(shift[:, :], meanvar[:, :, 0], -1.0, rstd[:, :], ALU.mult,
                                             ALU.mult).then_inc(s_shift, 1)
                    for t in range(ET):
                        own.mark(dve.scalar_tensor_tensor(y[b % 2][:, t, :], u[b % 2][:, t, :], d[:, t:t + 1],
                                                          y[b % 2][:, t, :], ALU.mult, ALU.add))
                    own.wait()
                    if b:
                        dve.wait_ge(s_t, TB * b)
                    for t in range(ET):
                        dve.wait_ge(s_silu, TB * b + t + 1)
                        dve.tensor_tensor(gated[:, t, :], y[b % 2][:, t, :], silu[:, t, :], ALU.mult).then_inc(s_g, 1)
                    if b:
                        dve.wait_ge(s_st, 16 * b)
                    for t in range(TB):
                        dve.wait_ge(s_t, TB * b + t + 1)
                        dve.tensor_tensor(res[:, t, :], banks[t][:, :, :].rearrange("p e n -> p (e n)"),
                                          rows[b % 2][:, t, :], ALU.add).then_inc(s_res, 1)

            @block.scalar
            def _(act):
                for b in range(B):
                    act.wait_ge(s_ld[b % 2], 48 * (b // 2 + 1))
                    act.wait_ge(s_shift, b + 1)
                    if b:
                        act.wait_ge(s_g, ET * b)
                    for t in range(TB):
                        act.activation(silu[:, t, :], rows[b % 2][:, t, :], ACT.Silu, bias=shift[:, t:t + 1],
                                       scale=rstd[:, t:t + 1]).then_inc(s_silu, 1)

            @block.tensor
            def _(pe):
                pe.wait_ge(s_in, 32)
                for b in range(B):
                    pe.wait_ge(s_g, ET * (b + 1))
                    for t in range(TB):
                        if b:
                            pe.wait_ge(s_res, TB * (b - 1) + t + 1)
                        for e in range(ET):
                            tr = pe.transpose(banks[t][:, e, :], gated[:, e, t * P:(t + 1) * P], ident_sb[:, :])
                        tr.then_inc(s_t, 1)


EXPERTS = 16


def stage_router(nc, xT, Wr, bias, shares, ident, iota):
    N = B * TB
    with Scope(nc, "rou") as m:
        ident_sb = m.sb("ident", [P, P])
        iota_sb = m.sb("iota", [P, EXPERTS])
        bias_sb = m.sb("bias", [P, EXPERTS])
        wr = m.sb("wr", [EXPERTS, DIM])
        wrT = m.sb("wrT", [P, 2, KD, EXPERTS], F32R)
        xin = [m.sb(f"x{b}", [P, 2, KD, S], F32R) for b in range(B)]
        logits = m.sb("logits", [P, N, EXPERTS])
        top = m.sb("top", [P, N])
        ex = m.sb("ex", [P, N, EXPERTS])
        total = m.sb("total", [P, N])
        best = m.sb("best", [P, N, 8])
        where = m.sb("where", [P, N, 8], mybir.dt.uint32)
        wheref = m.sb("wheref", [P, N, 2])
        pick = m.sb("pick", [P, N])
        weight = m.sb("weight", [P, N, 2])
        hot = [m.sb(f"hot{i}", [P, N, EXPERTS]) for i in range(2)]
        share = m.sb("share", [P, N, EXPERTS + 1])
        ps_t = m.ps("turn", [P, KD, EXPERTS])
        ps_l = m.ps("logits_ps", [P, N, EXPERTS])
        s_in, s_x = m.sem("in"), [m.sem(f"x_in{b}") for b in range(B)]
        s_t, s_whi, s_wlo, s_l = m.sem("turned"), m.sem("w_hi"), m.sem("w_lo"), m.sem("logits_done")
        s_sub, s_ex, s_dve, s_st = m.sem("shifted"), m.sem("exp_done"), m.sem("dve_steps"), m.sem("stored")

        def spread(a):
            return a.rearrange("p (n a) -> p n a", a=1).to_broadcast([P, N, EXPERTS])

        with m.block() as block:
            @block.sync
            def _(sp):
                sp.dma_start(ident_sb[:, :], ident).then_inc(s_in, 16)
                sp.dma_start(iota_sb[:, :], iota).then_inc(s_in, 16)
                sp.dma_start(wr[:, :], Wr).then_inc(s_in, 16)
                sp.dma_start(bias_sb[:, :], bias.rearrange("(a n) -> a n", a=1).to_broadcast([P, EXPERTS])).then_inc(s_in, 16)
                for b in range(B):
                    sp.dma_start(xin[b][:, :, :, :].bitcast(F32), xT[b]).then_inc(s_x[b], 16)
                sp.wait_ge(s_st, 1)
                sp.dma_start(shares.rearrange("(n p) e -> p n e", p=P), share[:, :, :]).then_inc(s_in, 16)
                sp.wait_ge(s_in, 16 * 5)

            @block.tensor
            def _(pe):
                pe.wait_ge(s_in, 16 * 4)
                for k in range(KD):
                    tr = pe.transpose(ps_t[:, k, :], wr[:, k * P:(k + 1) * P], ident_sb[0:EXPERTS, 0:EXPERTS])
                tr.then_inc(s_t, 1)
                pe.wait_ge(s_wlo, 1)
                for b in range(B):
                    pe.wait_ge(s_x[b], 16)
                    for t in range(TB):
                        rows = slice(t * P, (t + 1) * P)
                        for k in range(KD):
                            mm = split_product(pe, ps_l[:, b * TB + t, :], (xin[b][:, 0, k, rows], xin[b][:, 1, k, rows]),
                                               (wrT[:, 0, k, :], wrT[:, 1, k, :]), k == 0, k == KD - 1)
                mm.then_inc(s_l, 1)

            @block.scalar
            def _(act):
                act.wait_ge(s_t, 1)
                act.copy(wrT[:, 0, :, :], ps_t[:, :, :]).then_inc(s_whi, 1)
                act.wait_ge(s_sub, 1)
                act.activation(ex[:, :, :], logits[:, :, :], ACT.Exp).then_inc(s_ex, 1)

            @block.vector
            def _(dve):
                own = Steps(dve, s_dve)
                dve.wait_ge(s_whi, 1)
                dve.tensor_tensor(wrT[:, 1, :, :], ps_t[:, :, :], wrT[:, 0, :, :].bitcast(F32), ALU.subtract).then_inc(s_wlo, 1)
                dve.wait_ge(s_l, 1)
                b_all = bias_sb[:, :].rearrange("p (a n) -> p a n", a=1).to_broadcast([P, N, EXPERTS])
                i_all = iota_sb[:, :].rearrange("p (a n) -> p a n", a=1).to_broadcast([P, N, EXPERTS])
                own.after(dve.tensor_tensor(logits[:, :, :], ps_l[:, :, :], b_all, ALU.add))
                own.after(dve.tensor_reduce(top[:, :], logits[:, :, :], AX_X, ALU.max))
                dve.tensor_tensor(logits[:, :, :], logits[:, :, :], spread(top[:, :]), ALU.subtract).then_inc(s_sub, 1)
                dve.wait_ge(s_ex, 1)
                own.after(dve.tensor_reduce(total[:, :], ex[:, :, :], AX_X, ALU.add))
                own.after(dve.reciprocal(total[:, :], total[:, :]))
                own.after(dve.tensor_tensor(ex[:, :, :], ex[:, :, :], spread(total[:, :]), ALU.mult))
                for n in range(N):
                    own.mark(dve.max(best[:, n, :], ex[:, n, :]))
                own.wait()
                for n in range(N):
                    own.mark(dve.max_index(where[:, n, :], best[:, n, :], ex[:, n, :]))
                own.wait()
                own.after(dve.tensor_copy(wheref[:, :, :], where[:, :, 0:2]))
                own.after(dve.tensor_tensor(pick[:, :], best[:, :, 0], best[:, :, 1], ALU.add))
                own.after(dve.tensor_scalar(pick[:, :], pick[:, :], 1e-9, None, ALU.add))
                own.after(dve.reciprocal(pick[:, :], pick[:, :]))
                for j in range(2):
                    own.mark(dve.tensor_tensor(weight[:, :, j], best[:, :, j], pick[:, :], ALU.mult))
                    own.mark(dve.tensor_tensor(hot[j][:, :, :], i_all, spread(wheref[:, :, j]), ALU.is_equal))
                own.wait()
                for j in range(2):
                    own.mark(dve.tensor_tensor(hot[j][:, :, :], hot[j][:, :, :], spread(weight[:, :, j]), ALU.mult))
                own.mark(dve.memset(share[:, :, EXPERTS:EXPERTS + 1], 1.0))
                own.wait()
                dve.tensor_tensor(share[:, :, 0:EXPERTS], hot[0][:, :, :], hot[1][:, :, :], ALU.add).then_inc(s_st, 1)


def build(nc, x, ctx_1024, L0_xattn_Wq, L0_xattn_Wk, L0_xattn_Wv, L0_xattn_Wo, L0_xattn_gq, L0_xattn_gk,
          L0_ffn_SU_ug, L0_ffn_SU_dp, L0_ffn_Wscale_ug, L0_ffn_Wscale_dp, L0_ffn_W_up, L0_ffn_W_gate, L0_ffn_W_down,
          L1_xattn_in_proj_w, L1_xattn_conv_w, L1_xattn_conv_b, L1_xattn_x_proj_w, L1_xattn_dt_proj_w,
          L1_xattn_dt_proj_b, L1_xattn_A_log, L1_xattn_D, L1_ffn_Wr, L1_ffn_bias, L1_ffn_Wg, L1_ffn_Wu, L1_ffn_Wd,
          L1_ffn_sWg, L1_ffn_sWu, L1_ffn_sWd, ident, had, iota, out):
    def scratch(name, shape):
        return nc.dram_tensor(name, shape, F32).ap()

    x0 = x.rearrange("b s d -> (b s) d")
    result = out.rearrange("b s d -> (b s) d")
    x1, x2, x3 = (scratch(f"x{i}", (B * S, DIM)) for i in (1, 2, 3))
    normT = scratch("normT", (B, P, 2, KD, S))
    rotT = scratch("rotT", (B, P, 2, KD, S))
    ctxT = scratch("ctxT", (B, P, 2, KC, S))
    ffnT = scratch("ffnT", (4, P, 2, 3 * KD * 512))
    u_d, delta_d, du_d, y_d = (scratch(n, (B, P, ET, S)) for n in ("u_d", "delta_d", "du_d", "y_d"))
    bc_d = scratch("bc_d", (B, 2 * STATES, S))
    shares = scratch("shares", (B * S, EXPERTS + 1))

    stage_norm(nc, "nrm0", x0, normT, ident, ctx_1024, ctxT)
    stage_attention(nc, x0, x1, normT, ctxT, L0_xattn_Wq, L0_xattn_Wk, L0_xattn_Wv, L0_xattn_Wo, L0_xattn_gq,
                    L0_xattn_gk, ident)

    stage_ffn_weights(nc, ffnT, L0_ffn_W_gate, L0_ffn_W_up, L0_ffn_W_down, L0_ffn_Wscale_ug, L0_ffn_Wscale_dp,
                      L0_ffn_SU_dp, ident, had)
    stage_norm(nc, "nrm1", x1, normT, ident)
    stage_rotate(nc, normT, rotT, L0_ffn_SU_ug, had)

    def ffn_weights(sp, c, dst, sem):
        sp.dma_start(dst[:, :, :].bitcast(F32), ffnT[c]).then_inc(sem, 16)

    stage_mlp(nc, "ffn", x1, x2, rotT, 4, 512, ffn_weights, False, False)

    stage_ssm_inputs(nc, ctxT, L1_xattn_in_proj_w, L1_xattn_conv_w, L1_xattn_conv_b, L1_xattn_x_proj_w,
                     L1_xattn_dt_proj_w, L1_xattn_dt_proj_b, u_d, delta_d, du_d, bc_d, ident)
    stage_ssm_scan(nc, L1_xattn_A_log, delta_d, du_d, bc_d, y_d, ident)
    stage_ssm_gate(nc, x2, x3, u_d, y_d, L1_xattn_D, ident)

    stage_norm(nc, "nrm2", x3, normT, ident)
    stage_router(nc, normT, L1_ffn_Wr, L1_ffn_bias, shares, ident, iota)
    INNER = 256

    def expert_weights(sp, e, dst, sem):
        shared = isinstance(e, str)
        parts = (L1_ffn_sWg, L1_ffn_sWu, L1_ffn_sWd) if shared else (L1_ffn_Wg[e], L1_ffn_Wu[e], L1_ffn_Wd[e])
        at = 0
        for src in parts:
            n = src.shape[0] // P * src.shape[1]
            sp.dma_start(dst[:, at:at + n].rearrange("p (k n) -> p k n", k=src.shape[0] // P),
                         src.rearrange("(k p) n -> p k n", p=P)).then_inc(sem, 16)
            at += n

    stage_mlp(nc, "moe", x3, result, normT, EXPERTS + 1, INNER, expert_weights, True, True, shares)


def kernel(**inputs):
    import numpy as _np
    import concourse.bacc as _bacc
    from concourse import mybir as _mybir
    from concourse.bass_utils import run_bass_kernel_spmd as _run

    nc = _bacc.Bacc("TRN2", target_bir_lowering=False, num_devices=1)
    sylvester = _np.ones((1, 1), _np.float32)
    while len(sylvester) < P:
        sylvester = _np.block([[sylvester, sylvester], [sylvester, -sylvester]])
    constants = {
        "ident": _np.eye(P, dtype=_np.float32),
        "had": sylvester,
        "iota": _np.tile(_np.arange(EXPERTS, dtype=_np.float32), (P, 1)),
    }
    arrays, args = {}, {}
    for name, a in {**inputs, **constants}.items():
        a = _np.ascontiguousarray(a)
        arrays[f"in_{name}"] = a
        args[name] = nc.dram_tensor(f"in_{name}", a.shape, _mybir.dt.from_np(a.dtype), kind="ExternalInput").ap()
    args["out"] = nc.dram_tensor("out_0", (B, S, DIM), F32, kind="ExternalOutput").ap()
    build(nc, **args)
    r = _run(nc, [arrays], core_ids=[0])
    return r.results[0]["out_0"]
```

```python
from contextlib import ExitStack

import concourse.bass as bass
from concourse import mybir

F32 = mybir.dt.float32
F32R = mybir.dt.float32r
ALU = mybir.AluOpType
ACT = mybir.ActivationFunctionType
AX_X = mybir.AxisListType.X

P = 128
B = 4
S = 512
TB = S // P
DIM = 512
KD = DIM // P
CD = 256
KC = CD // P
HEADS = 16
LN_EPS = 1e-5


class Steps:

    def __init__(self, eng, sem, base=0):
        self.eng, self.sem, self.base, self.n = eng, sem, base, 0

    def mark(self, ins):
        self.n += 1
        ins.then_inc(self.sem, 1)

    def wait(self):
        self.eng.wait_ge(self.sem, self.base + self.n)

    def wait_apart(self, pace):
        wait_apart(self.eng, self.sem, self.base + self.n, pace)

    def after(self, ins):
        self.mark(ins)
        self.wait()


class Memory:

    def __init__(self, nc, stage):
        self.nc, self.stage, self.stack, self.sems = nc, stage, ExitStack(), []

    def __enter__(self):
        self.stack.__enter__()
        return self

    def __exit__(self, *a):
        return self.stack.__exit__(*a)

    def sb(self, name, shape, dt=F32):
        return self.stack.enter_context(self.nc.sbuf_tensor(f"{self.stage}_{name}", shape, dt))


class Scope(Memory):

    def __exit__(self, *a):
        self.nc.clear_and_free_semaphores(self.sems)
        self.nc.all_engine_barrier()
        return self.stack.__exit__(*a)

    def ps(self, name, shape, dt=F32):
        return self.stack.enter_context(self.nc.psum_tensor(f"{self.stage}_{name}", shape, dt))

    def sem(self, name):
        self.sems.append(self.nc.alloc_semaphore(f"{self.stage}_{name}"))
        return self.sems[-1]

    def block(self):
        return self.nc.Block()


def wait_apart(eng, sem, value, pace):
    eng.wait_ge(sem, value)
    eng.sem_inc(pace, 1)


def split_product(pe, out, lhs, rhs, start, stop):
    (lh, ll), (rh, rl) = lhs, rhs
    pe.matmul(out, lh, rh, start=start, stop=False)
    pe.matmul(out, lh, rl, start=False, stop=False)
    return pe.matmul(out, ll, rh, start=False, stop=stop)


def newton_rsqrt(dve, own, out, value, guess_bits, work):
    own.after(dve.tensor_scalar(guess_bits.bitcast(mybir.dt.int32), value.bitcast(mybir.dt.int32), 1, None,
                                ALU.logical_shift_right))
    own.after(dve.tensor_scalar(out.bitcast(mybir.dt.int32), guess_bits.bitcast(mybir.dt.int32), -1.0,
                                float(0x5F3759DF), ALU.mult, ALU.add))
    for _ in range(3):
        own.after(dve.tensor_tensor(work, out, out, ALU.mult))
        own.after(dve.tensor_tensor(work, work, value, ALU.mult))
        own.after(dve.tensor_scalar(work, work, -0.5, 1.5, ALU.mult, ALU.add))
        last = dve.tensor_tensor(out, out, work, ALU.mult)
        own.after(last)


RSQRT_STEPS = 2 + 3 * 4


def stage_norm(nc, stage, xs, xT, ident, x=None, ctx=None, ctxT=None, rowsout=None):
    with Scope(nc, stage) as m:
        ident_sb = m.sb("ident", [P, P])
        normed = [m.sb(f"normed{i}", [P, TB, DIM]) for i in range(2)]
        stats = m.sb("stats", [P, TB, 6])
        meanvar = m.sb("meanvar", [P, TB, 2])
        var_eps = m.sb("var_eps", [P, TB])
        guess = m.sb("guess", [P, TB])
        work = m.sb("work", [P, TB])
        rstd = m.sb("rstd", [P, TB])
        outT = [m.sb(f"outT{i}", [P, 2, KD, S], F32R) for i in range(2)]
        banks = [m.ps(f"bank{t}", [P, KD, P]) for t in range(TB)]
        s_ident = m.sem("ident_in")
        s_x = [m.sem(f"x_in{b}") for b in range(B)]
        s_dve = m.sem("dve_steps")
        s_normed, s_tr, s_hi, s_lo = m.sem("normed"), m.sem("transposed"), m.sem("hi"), m.sem("lo")
        s_out = [m.sem(f"stored{i}") for i in range(2)]
        s_rowsout = [m.sem(f"rows_stored{i}") for i in range(2)]
        if ctx is not None:
            crows = m.sb("crows", [P, B, TB, CD])
            coutT = [m.sb(f"coutT{i}", [P, 2, KC, S], F32R) for i in range(2)]
            cbanks = [m.ps(f"cbank{t}", [P, KD, P]) for t in range(TB)]
            s_crows = [m.sem(f"crows_in{b}") for b in range(B)]
            s_ctr, s_chi, s_clo = m.sem("ctx_transposed"), m.sem("ctx_hi"), m.sem("ctx_lo")
            s_cout = [m.sem(f"ctx_stored{i}") for i in range(2)]

        with m.block() as block:
            @block.sync
            def _(sp):
                sp.dma_start(ident_sb[:, :], ident).then_inc(s_ident, 16)
                for b in range(B):
                    if ctx is not None:
                        sp.dma_start(crows[:, b], ctx[b].rearrange("(t p) d -> p t d", p=P)).then_inc(s_crows[b], 16)
                    if x is not None:
                        rows = x[b * S:(b + 1) * S, :].rearrange("(t p) d -> p t d", p=P)
                        sp.dma_start(xs[:, b * TB:(b + 1) * TB, :], rows).then_inc(s_x[b], 16)
                for b in range(B):
                    if rowsout is not None:
                        sp.wait_ge(s_normed, (b + 1) * TB)
                        rows = rowsout[b * S:(b + 1) * S, :].rearrange("(t p) d -> p t d", p=P)
                        sp.dma_start(rows, normed[b % 2][:, :, :]).then_inc(s_rowsout[b % 2], 16)
                    if ctx is not None:
                        sp.wait_ge(s_clo, (b + 1) * TB)
                        sp.dma_start(ctxT[b], coutT[b % 2][:, :, :, :].bitcast(F32)).then_inc(s_cout[b % 2], 16)
                    sp.wait_ge(s_lo, (b + 1) * TB)
                    sp.dma_start(xT[b], outT[b % 2][:, :, :, :].bitcast(F32)).then_inc(s_out[b % 2], 16)
                for i in range(2):
                    sp.wait_ge(s_out[i], 16 * B // 2)
                    if rowsout is not None:
                        sp.wait_ge(s_rowsout[i], 16 * B // 2)
                    if ctx is not None:
                        sp.wait_ge(s_cout[i], 16 * B // 2)

            @block.vector
            def _(dve):
                own = Steps(dve, s_dve)

                def normalize(b):
                    if x is not None:
                        dve.wait_ge(s_x[b], 16)
                    for t in range(TB):
                        own.mark(dve.bn_stats(stats[:, t, :], xs[:, b * TB + t, :]))
                    own.wait()
                    for t in range(TB):
                        own.mark(dve.bn_aggr(meanvar[:, t, :], stats[:, t, :]))
                    own.wait()
                    own.after(dve.tensor_scalar(var_eps[:, :], meanvar[:, :, 1], LN_EPS, None, ALU.add))
                    newton_rsqrt(dve, own, rstd[:, :], var_eps[:, :], guess[:, :], work[:, :])
                    if b >= 2:
                        dve.wait_ge(s_tr, (b - 1) * TB)
                        if rowsout is not None:
                            dve.wait_ge(s_rowsout[b % 2], 16)
                    for t in range(TB):
                        dve.tensor_scalar(normed[b % 2][:, t, :], xs[:, b * TB + t, :], meanvar[:, t, 0:1],
                                          rstd[:, t:t + 1], ALU.subtract, ALU.mult).then_inc(s_normed, 1)

                normalize(0)
                for b in range(B):
                    if b + 1 < B:
                        normalize(b + 1)
                    for t in range(TB):
                        part = slice(t * P, (t + 1) * P)
                        if ctx is not None:
                            dve.wait_ge(s_chi, b * TB + t + 1)
                            dve.tensor_tensor(coutT[b % 2][:, 1, :, part], cbanks[t][:, 0:KC, :],
                                              coutT[b % 2][:, 0, :, part].bitcast(F32), ALU.subtract).then_inc(s_clo, 1)
                        dve.wait_ge(s_hi, b * TB + t + 1)
                        dve.tensor_tensor(outT[b % 2][:, 1, :, part], banks[t][:, :, :],
                                          outT[b % 2][:, 0, :, part].bitcast(F32), ALU.subtract).then_inc(s_lo, 1)

            @block.tensor
            def _(pe):
                pe.wait_ge(s_ident, 16)
                for b in range(B):
                    for t in range(TB):
                        if ctx is not None:
                            pe.wait_ge(s_crows[b], 16)
                            if b:
                                pe.wait_ge(s_clo, (b - 1) * TB + t + 1)
                            for k in range(KC):
                                tr = pe.transpose(cbanks[t][:, k, :], crows[:, b, t, k * P:(k + 1) * P], ident_sb[:, :])
                            tr.then_inc(s_ctr, 1)
                    for t in range(TB):
                        pe.wait_ge(s_normed, b * TB + t + 1)
                        if b:
                            pe.wait_ge(s_lo, (b - 1) * TB + t + 1)
                        for k in range(KD):
                            tr = pe.transpose(banks[t][:, k, :], normed[b % 2][:, t, k * P:(k + 1) * P], ident_sb[:, :])
                        tr.then_inc(s_tr, 1)

            @block.scalar
            def _(act):
                for b in range(B):
                    if b >= 2:
                        act.wait_ge(s_out[b % 2], 16)
                        if ctx is not None:
                            act.wait_ge(s_cout[b % 2], 16)
                    for t in range(TB):
                        part = slice(t * P, (t + 1) * P)
                        if ctx is not None:
                            act.wait_ge(s_ctr, b * TB + t + 1)
                            act.copy(coutT[b % 2][:, 0, :, part], cbanks[t][:, 0:KC, :]).then_inc(s_chi, 1)
                        act.wait_ge(s_tr, b * TB + t + 1)
                        act.copy(outT[b % 2][:, 0, :, part], banks[t][:, :, :]).then_inc(s_hi, 1)


def stage_attention(nc, xs, xT, ctxT, Wq, Wk, Wv, Wo, gq, gk, ident):
    D = P
    HP = 2
    PAIRS = HEADS // HP
    W2 = HP * D
    RMS_EPS = 1e-5
    NEWTON = 3
    scale = D ** -0.5
    wq_d = Wq.rearrange("(k p) n -> p k n", p=P)
    wk_d = Wk.rearrange("(k p) n -> p k n", p=P)
    wv_d = Wv.rearrange("(k p) n -> p k n", p=P)
    wo_d = Wo.rearrange("(h p) n -> p h n", p=P)
    NQ, NKV = KD * W2, KC * W2
    with Scope(nc, "att") as m:
        ident_sb = m.sb("ident", [P, P])
        ones = m.sb("ones", [P, 1])
        gains = m.sb("gains", [P, 2])
        gain = m.sb("gain", [P, 1])
        raw = m.sb("raw_qkv", [P, NQ + 2 * NKV])
        raw_o = m.sb("raw_o", [P, HP, DIM])
        w = m.sb("w_qkv", [P, 2, NQ + 2 * NKV], F32R)
        wo = m.sb("wo", [P, 2, 2, HP, DIM], F32R)
        xn = m.sb("xn", [P, 2, KD, S], F32R)
        cxs = [m.sb(f"cx{b}", [P, 2, KC, S], F32R) for b in range(B)]
        kn = m.sb("kn", [P, TB, HP, D])
        ksq = m.sb("ksq", [P, TB, HP, D])
        qsq = m.sb("qsq", [P, HP, S])
        qT = m.sb("qT", [P, 2, HP, S], F32R)
        kT = m.sb("kT", [P, 2, HP, S], F32R)
        v = m.sb("v", [P, 2, TB, W2], F32R)
        probs = m.sb("probs", [P, HP * TB, S])
        pT = m.sb("pT", [P, 2, TB, S], F32R)
        oT = m.sb("oT", [P, 2, HP, S], F32R)
        kss = m.sb("kss", [P, TB * HP])
        qss = m.sb("qss", [P, TB * HP])
        rk = m.sb("rk", [P, TB * HP])
        rq = m.sb("rq", [P, TB * HP])
        kguess = m.sb("kguess", [P, TB * HP])
        qguess = m.sb("qguess", [P, TB * HP])
        work = m.sb("work", [P, TB * HP])
        nmax = m.sb("nmax", [P, TB * HP])
        bias = m.sb("bias", [P, TB * HP])
        sums = m.sb("sums", [P, TB * HP])
        recip = m.sb("recip", [P, TB * HP])
        ps_s = [m.ps(f"s{i}", [P, S]) for i in range(2)]
        ps_pt = [m.ps(f"pt{i}", [P, TB, P]) for i in range(2)]
        ps_w = [m.ps(f"w{i}", [P, 512]) for i in range(3)]
        ps_o = m.ps("o", [P, S])

        s_const = m.sem("const_in")
        s_gain = m.sem("gain")
        s_raw, s_rawo = m.sem("raw_in"), m.sem("raw_o_in")
        s_w, s_wo = m.sem("w_split"), m.sem("wo_split")
        s_xn, s_cx = m.sem("xn_in"), [m.sem(f"cx_in{b}") for b in range(B)]
        s_s = m.sem("scores")
        s_max = m.sem("max")
        s_exp = m.sem("exp")
        s_rec = m.sem("recip")
        s_pn = m.sem("probs_normed")
        s_k, s_kc, s_ksq, s_kn = m.sem("k"), m.sem("k_copied"), m.sem("k_squared"), m.sem("k_normed")
        s_kt, s_kthi, s_ktlo = m.sem("kT"), m.sem("kT_hi"), m.sem("kT_lo")
        s_q, s_qhi, s_qsq, s_qlo = m.sem("q"), m.sem("q_hi"), m.sem("q_squared"), m.sem("q_lo")
        s_kss, s_rk, s_qss, s_pool = m.sem("k_sums"), m.sem("rk"), m.sem("q_squares"), m.sem("pool_steps")
        s_ss, s_ssread, s_rq = m.sem("q_sums"), m.sem("q_sums_read"), m.sem("rq")
        s_v, s_vhi, s_vlo = m.sem("v"), m.sem("v_hi"), m.sem("v_lo")
        s_pt, s_pthi = m.sem("pT"), m.sem("pT_hi")
        s_ptlo = m.sem("pT_lo")
        s_pv, s_ohi = m.sem("pv"), m.sem("o_hi")
        s_olo = m.sem("o_lo")
        s_y = m.sem("y")
        s_yadd = m.sem("y_added")
        s_dve = m.sem("dve_steps")
        s_pace = m.sem("pace")

        def pairs(eng, iteration):
            with eng.Fori(0, PAIRS - 1) as hp:
                for b in range(B):
                    iteration(hp, b, False)
            for b in range(B):
                iteration(PAIRS - 1, b, b == B - 1)

        def wpart(part, which, k):
            at = {"q": 0, "k": NQ, "v": NQ + NKV}[which] + k * W2
            return w[:, part, at:at + W2]

        with m.block() as block:
            @block.sync
            def _(sp):
                def load_weights(hp):
                    sp.dma_start(raw[:, 0:NQ].rearrange("p (k n) -> p k n", k=KD), wq_d[:, :, bass.ds(hp * W2, W2)]).then_inc(s_raw, 16)
                    for at, src in ((NQ, wk_d), (NQ + NKV, wv_d)):
                        sp.dma_start(raw[:, at:at + NKV].rearrange("p (k n) -> p k n", k=KC),
                                     src[:, :, bass.ds(hp * W2, W2)]).then_inc(s_raw, 16)

                def load_wo(hp):
                    sp.dma_start(raw_o[:, :, :], wo_d[:, bass.ds(hp * HP, HP), :]).then_inc(s_rawo, 16)

                sp.dma_start(ident_sb[:, :], ident).then_inc(s_const, 16)
                sp.dma_start(gains[:, 0:1], gq.rearrange("(p a) -> p a", a=1)).then_inc(s_const, 16)
                sp.dma_start(gains[:, 1:2], gk.rearrange("(p a) -> p a", a=1)).then_inc(s_const, 16)
                load_weights(0)
                sp.dma_start(cxs[0][:, :, :, :].bitcast(F32), ctxT[0]).then_inc(s_cx[0], 16)
                sp.dma_start(xn[:, :, :, :].bitcast(F32), xT[0]).then_inc(s_xn, 16)
                load_wo(0)
                for b in range(1, B):
                    sp.dma_start(cxs[b][:, :, :, :].bitcast(F32), ctxT[b]).then_inc(s_cx[b], 16)

                def iteration(hp, b, last):
                    i = hp * B + b
                    if not last:
                        sp.wait_ge(s_q, 2 * i + 2)
                        sp.dma_start(xn[:, :, :, :].bitcast(F32), xT[(b + 1) % B]).then_inc(s_xn, 16)
                    if b == 0 and not (isinstance(hp, int) and hp == PAIRS - 1):
                        sp.wait_ge(s_w, 2 * hp + 2)
                        load_weights(hp + 1)
                        sp.wait_ge(s_wo, hp + 1)
                        load_wo(hp + 1)

                pairs(sp, iteration)

            @block.tensor
            def _(pe):
                def score(i, n):
                    h, t = divmod(n, TB)
                    if n == 0:
                        pe.wait_ge(s_ktlo, 2 * i + 2)
                        pe.wait_ge(s_qlo, 2 * i + 2)
                    pe.wait_ge(s_exp, 8 * i + n + 1)
                    q = slice(t * P, (t + 1) * P)
                    split_product(pe, ps_s[n % 2][:, :], (qT[:, 0, h, q], qT[:, 1, h, q]),
                                  (kT[:, 0, h, :], kT[:, 1, h, :]), True, True).then_inc(s_s, 1)

                def kv(cx, which, half, bank, sem):
                    for a in range(2):
                        t = 2 * half + a
                        rows = slice(t * P, (t + 1) * P)
                        for k in range(KC):
                            mm = split_product(pe, ps_w[bank][:, a * W2:(a + 1) * W2],
                                               (cx[:, 0, k, rows], cx[:, 1, k, rows]),
                                               (wpart(0, which, k), wpart(1, which, k)), k == 0, k == KC - 1)
                    mm.then_inc(sem, 1)

                def queries(h, bank):
                    d = slice(h * D, (h + 1) * D)
                    for k in range(KD):
                        mm = split_product(pe, ps_w[bank][:, :], (wpart(0, "q", k)[:, d], wpart(1, "q", k)[:, d]),
                                           (xn[:, 0, k, :], xn[:, 1, k, :]), k == 0, k == KD - 1)
                    mm.then_inc(s_q, 1)

                def turn_k(h, bank):
                    for t in range(TB):
                        tr = pe.transpose(ps_w[bank][:, t * P:(t + 1) * P], kn[:, t, h, :], ident_sb[:, :])
                    tr.then_inc(s_kt, 1)

                def sums_q():
                    for n in range(HP * TB):
                        h, t = divmod(n, TB)
                        mm = pe.matmul(ps_o[:, n:n + 1], qsq[:, h, t * P:(t + 1) * P], ones[:, :], start=True, stop=True)
                    mm.then_inc(s_ss, 1)

                def turn_p(i, h, k):
                    n = 8 * i + 4 * h + k
                    if k == 0:
                        pe.wait_ge(s_pn, 8 * i + 4 * h + 4)
                    pe.wait_ge(s_ptlo, n + 1)
                    for t in range(TB):
                        tr = pe.transpose(ps_pt[k % 2][:, t, :], probs[:, h * TB + t, k * P:(k + 1) * P], ident_sb[:, :])
                    tr.then_inc(s_pt, 1)

                def pv(i, h):
                    pe.wait_ge(s_ptlo, 8 * i + 4 * h + 4 + 2)
                    d = slice(h * D, (h + 1) * D)
                    for k in range(TB):
                        mm = split_product(pe, ps_o[:, :], (v[:, 0, k, d], v[:, 1, k, d]),
                                           (pT[:, 0, k, :], pT[:, 1, k, :]), k == 0, k == TB - 1)
                    mm.then_inc(s_pv, 1)

                def project(hp, t, bank):
                    rows = slice(t * P, (t + 1) * P)
                    for h in range(HP):
                        mm = split_product(pe, ps_w[bank][:, :], (oT[:, 0, h, rows], oT[:, 1, h, rows]),
                                           (wo[:, hp % 2, 0, h, :], wo[:, hp % 2, 1, h, :]), h == 0, h == HP - 1)
                    mm.then_inc(s_y, 1)

                pe.wait_ge(s_const, 48)
                pe.wait_ge(s_gain, 1)
                pe.wait_ge(s_w, 2)
                pe.wait_ge(s_cx[0], 16)
                kv(cxs[0], "k", 0, 0, s_k)
                kv(cxs[0], "k", 1, 1, s_k)
                pe.wait_ge(s_xn, 16)
                queries(0, 2)
                pe.wait_ge(s_kc, 1)
                queries(1, 0)
                pe.wait_ge(s_kn, 1)
                turn_k(0, 1)
                pe.wait_ge(s_qlo, 1)
                turn_k(1, 2)
                pe.wait_ge(s_qsq, 2)
                sums_q()
                pe.wait_ge(s_qlo, 2)
                kv(cxs[0], "v", 0, 0, s_v)
                pe.wait_ge(s_ktlo, 1)
                kv(cxs[0], "v", 1, 1, s_v)
                score(0, 0)
                score(0, 1)

                def iteration(hp, b, last):
                    i = hp * B + b
                    j = i + 1
                    cx = cxs[(b + 1) % B]
                    score(i, 2)
                    score(i, 3)
                    if not last:
                        pe.wait_ge(s_w, (2 * hp + 3) if b == B - 1 else (2 * hp + 2))
                        pe.wait_ge(s_cx[(b + 1) % B], 16)
                        pe.wait_ge(s_yadd, 4 * i + 2)
                        kv(cx, "k", 0, 0, s_k)
                    score(i, 4)
                    if not last:
                        pe.wait_ge(s_yadd, 4 * i + 3)
                        kv(cx, "k", 1, 1, s_k)
                    score(i, 5)
                    if not last:
                        pe.wait_ge(s_xn, 16 * j + 16)
                        if b == B - 1:
                            pe.wait_ge(s_w, 2 * hp + 4)
                        pe.wait_ge(s_yadd, 4 * i + 4)
                        queries(0, 2)
                    turn_p(i, 0, 0)
                    turn_p(i, 0, 1)
                    score(i, 6)
                    score(i, 7)
                    turn_p(i, 0, 2)
                    turn_p(i, 0, 3)
                    if not last:
                        pe.wait_ge(s_kc, 2 * j + 1)
                        queries(1, 0)
                    pe.wait_ge(s_vlo, 2 * i + 2)
                    pe.wait_ge(s_olo, 2 * i + 2)
                    pv(i, 0)
                    if not last:
                        pe.wait_ge(s_kn, j + 1)
                        turn_k(0, 1)
                        pe.wait_ge(s_qlo, 2 * j + 1)
                        turn_k(1, 2)
                    turn_p(i, 1, 0)
                    turn_p(i, 1, 1)
                    if not last:
                        pe.wait_ge(s_qlo, 2 * j + 2)
                        kv(cx, "v", 0, 0, s_v)
                    turn_p(i, 1, 2)
                    pe.wait_ge(s_olo, 2 * i + 3)
                    if not last:
                        pe.wait_ge(s_qsq, 2 * j + 2)
                        sums_q()
                    turn_p(i, 1, 3)
                    if not last:
                        pe.wait_ge(s_ktlo, 2 * j + 1)
                        kv(cx, "v", 1, 1, s_v)
                        pe.wait_ge(s_ssread, j + 1)
                    pv(i, 1)
                    if not last:
                        score(j, 0)
                        score(j, 1)
                    pe.wait_ge(s_olo, 2 * i + 4)
                    pe.wait_ge(s_wo, hp + 1)
                    project(hp, 0, 2)
                    if not last:
                        pe.wait_ge(s_vlo, 2 * j + 1)
                    project(hp, 1, 0)
                    if not last:
                        pe.wait_ge(s_vlo, 2 * j + 2)
                    project(hp, 2, 1)
                    pe.wait_ge(s_yadd, 4 + 4 * i + 1)
                    project(hp, 3, 2)

                pairs(pe, iteration)

            @block.scalar
            def _(act):
                def copy_k(j, half):
                    act.wait_ge(s_k, 2 * j + half + 1)
                    act.copy(kn[:, 2 * half:2 * half + 2, :, :], ps_w[half][:, :]).then_inc(s_kc, 1)

                def q_parts(j, h):
                    bank = ps_w[(2, 0)[h]]
                    act.wait_ge(s_q, 2 * j + h + 1)
                    act.copy(qT[:, 0, h, :], bank[:, :]).then_inc(s_qhi, 1)
                    act.activation(qsq[:, h, :], bank[:, :], ACT.Square).then_inc(s_qsq, 1)

                def kt_hi(j, h):
                    act.wait_ge(s_kt, 2 * j + h + 1)
                    act.activation(kT[:, 0, h, :], ps_w[1 + h][:, :], ACT.Copy, scale=gain[:, 0:1]).then_inc(s_kthi, 1)

                def v_hi(j, half):
                    act.wait_ge(s_v, 2 * j + half + 1)
                    act.copy(v[:, 0, 2 * half:2 * half + 2, :], ps_w[half][:, :]).then_inc(s_vhi, 1)

                def exp(i, n):
                    act.wait_ge(s_max, 8 * i + n + 1)
                    act.activation(probs[:, n, :], ps_s[n % 2][:, :], ACT.Exp, bias=bias[:, n:n + 1],
                                   scale=rq[:, n:n + 1], accum_out=sums[:, n:n + 1]).then_inc(s_exp, 1)

                def pt_hi(i, h, k):
                    act.wait_ge(s_pt, 8 * i + 4 * h + k + 1)
                    act.copy(pT[:, 0, k, :], ps_pt[k % 2][:, :, :]).then_inc(s_pthi, 1)

                def o_hi(i, h):
                    act.wait_ge(s_pv, 2 * i + h + 1)
                    act.copy(oT[:, 0, h, :], ps_o[:, :]).then_inc(s_ohi, 1)

                act.sem_inc(s_exp, 2)
                act.wait_ge(s_gain, 1)
                copy_k(0, 0)
                copy_k(0, 1)
                q_parts(0, 0)
                q_parts(0, 1)
                kt_hi(0, 0)
                kt_hi(0, 1)
                v_hi(0, 0)
                v_hi(0, 1)
                act.wait_ge(s_rq, 1)
                exp(0, 0)
                exp(0, 1)

                def iteration(hp, b, last):
                    i = hp * B + b
                    j = i + 1
                    exp(i, 2)
                    exp(i, 3)
                    if not last:
                        copy_k(j, 0)
                    exp(i, 4)
                    if not last:
                        copy_k(j, 1)
                    exp(i, 5)
                    pt_hi(i, 0, 0)
                    pt_hi(i, 0, 1)
                    pt_hi(i, 0, 2)
                    exp(i, 6)
                    pt_hi(i, 0, 3)
                    if not last:
                        q_parts(j, 0)
                    exp(i, 7)
                    if not last:
                        q_parts(j, 1)
                    o_hi(i, 0)
                    if not last:
                        kt_hi(j, 0)
                        kt_hi(j, 1)
                    for k in range(TB):
                        pt_hi(i, 1, k)
                    o_hi(i, 1)
                    if not last:
                        v_hi(j, 0)
                        v_hi(j, 1)
                        act.wait_ge(s_rq, j + 1)
                        exp(j, 0)
                        exp(j, 1)

                pairs(act, iteration)

            @block.gpsimd
            def _(pool):
                def square_k(j):
                    pool.wait_ge(s_kc, 2 * j + 2)
                    pool.tensor_tensor(ksq[:, :, :, :], kn[:, :, :, :], kn[:, :, :, :], ALU.mult).then_inc(s_ksq, 1)

                def norm_p(i, n):
                    wait_apart(pool, s_rec, 8 * i + n + 1, s_pace)
                    pool.tensor_scalar(probs[:, n, :], probs[:, n, :], recip[:, n:n + 1], 1.0, ALU.mult,
                                       ALU.mult).then_inc(s_pn, 1)

                def newton(own, out, value, guess, work):
                    cur = guess
                    for _ in range(NEWTON):
                        own.mark(pool.tensor_tensor(work, cur, cur, ALU.mult))
                        own.wait_apart(s_pace)
                        own.mark(pool.tensor_tensor(work, work, value, ALU.mult))
                        own.wait_apart(s_pace)
                        own.mark(pool.tensor_scalar(work, work, -0.5, 1.5, ALU.mult, ALU.add))
                        own.wait_apart(s_pace)
                        own.mark(pool.tensor_tensor(out, cur, work, ALU.mult))
                        own.wait_apart(s_pace)
                        cur = out

                def norm_k(own, j):
                    wait_apart(pool, s_kss, j + 1, s_pace)
                    newton(own, rk[:, :], kss[:, :], kguess[:, :], work[:, :])
                    pool.sem_inc(s_rk, 1)

                def norm_q(own, j):
                    wait_apart(pool, s_qss, j + 1, s_pace)
                    newton(own, rq[:, :], qss[:, :], qguess[:, :], work[:, :])
                    pool.sem_inc(s_rq, 1)

                own = Steps(pool, s_pool)
                square_k(0)
                norm_k(own, 0)
                norm_q(own, 0)
                base = own.n
                per_pair = B * base

                def iteration(own, hp, b, last):
                    i = hp * B + b
                    j = i + 1
                    for n in range(4):
                        norm_p(i, n)
                    if not last:
                        square_k(j)
                    norm_p(i, 4)
                    norm_p(i, 5)
                    if not last:
                        norm_k(own, j)
                    norm_p(i, 6)
                    norm_p(i, 7)
                    if not last:
                        norm_q(own, j)

                with pool.Fori(0, PAIRS - 1) as hp:
                    own = Steps(pool, s_pool, hp * per_pair + base)
                    for b in range(B):
                        iteration(own, hp, b, False)
                own = Steps(pool, s_pool, (PAIRS - 1) * per_pair + base)
                for b in range(B):
                    iteration(own, PAIRS - 1, b, b == B - 1)

            @block.vector
            def _(dve):
                def split_w(own, hp, cols):
                    dve.wait_ge(s_raw, 48 * (hp + 1))
                    own.after(dve.tensor_copy(w[:, 0, cols], raw[:, cols]))
                    dve.tensor_tensor(w[:, 1, cols], raw[:, cols], w[:, 0, cols].bitcast(F32),
                                      ALU.subtract).then_inc(s_w, 1)

                KV, Q = slice(NQ, NQ + 2 * NKV), slice(0, NQ)

                def split_wo(own, hp):
                    dve.wait_ge(s_rawo, 16 * (hp + 1))
                    own.after(dve.tensor_copy(wo[:, hp % 2, 0, :, :], raw_o[:, :, :]))
                    dve.tensor_tensor(wo[:, hp % 2, 1, :, :], raw_o[:, :, :], wo[:, hp % 2, 0, :, :].bitcast(F32),
                                      ALU.subtract).then_inc(s_wo, 1)

                def row_max(own, i, n):
                    dve.wait_ge(s_s, 8 * i + n + 1)
                    own.after(dve.tensor_reduce(nmax[:, n:n + 1], ps_s[n % 2][:, :], AX_X, ALU.max, negate=True))
                    dve.tensor_tensor(bias[:, n:n + 1], nmax[:, n:n + 1], rq[:, n:n + 1], ALU.mult).then_inc(s_max, 1)

                def row_recip(i, n):
                    dve.wait_ge(s_exp, 8 * i + n + 1 + 2)
                    dve.reciprocal(recip[:, n:n + 1], sums[:, n:n + 1]).then_inc(s_rec, 1)

                def guess(own, out, value):
                    I32 = mybir.dt.int32
                    own.after(dve.tensor_scalar(out.bitcast(I32), value.bitcast(I32), 1, None, ALU.logical_shift_right))
                    return dve.tensor_scalar(out.bitcast(I32), out.bitcast(I32), -1.0, float(0x5F3759DF), ALU.mult, ALU.add)

                def sum_k(own, j):
                    dve.wait_ge(s_ksq, j + 1)
                    own.after(dve.tensor_reduce(kss[:, :], ksq[:, :, :, :], AX_X, ALU.add))
                    own.after(dve.tensor_scalar(kss[:, :], kss[:, :], 1.0 / D, RMS_EPS, ALU.mult, ALU.add))
                    guess(own, kguess[:, :], kss[:, :]).then_inc(s_kss, 1)

                def scale_k(j):
                    dve.wait_ge(s_rk, j + 1)
                    for n in range(TB * HP):
                        t, h = divmod(n, HP)
                        ins = dve.tensor_scalar(kn[:, t, h, :], kn[:, t, h, :], rk[:, n:n + 1], None, ALU.mult)
                    ins.then_inc(s_kn, 1)

                def q_lo(j, h):
                    dve.wait_ge(s_qsq, 2 * j + h + 1)
                    dve.tensor_tensor(qT[:, 1, h, :], ps_w[(2, 0)[h]][:, :], qT[:, 0, h, :].bitcast(F32),
                                      ALU.subtract).then_inc(s_qlo, 1)

                def kt_lo(j, h):
                    dve.wait_ge(s_kthi, 2 * j + h + 1)
                    dve.scalar_tensor_tensor(kT[:, 1, h, :], ps_w[1 + h][:, :], gain[:, 0:1],
                                             kT[:, 0, h, :].bitcast(F32), ALU.mult, ALU.subtract).then_inc(s_ktlo, 1)

                def v_lo(j, half):
                    dve.wait_ge(s_vhi, 2 * j + half + 1)
                    rows = slice(2 * half, 2 * half + 2)
                    dve.tensor_tensor(v[:, 1, rows, :], ps_w[half][:, :].rearrange("p (a n) -> p a n", a=2),
                                      v[:, 0, rows, :].bitcast(F32), ALU.subtract).then_inc(s_vlo, 1)

                def sum_q(own, j):
                    dve.wait_ge(s_ss, j + 1)
                    ins = dve.tensor_scalar(qss[:, :], ps_o[:, 0:TB * HP], 1.0 / D, RMS_EPS, ALU.mult, ALU.add)
                    ins.then_inc(s_ssread, 1)
                    dve.wait_ge(s_ssread, j + 1)
                    guess(own, qguess[:, :], qss[:, :]).then_inc(s_qss, 1)

                def pt_lo(i, h, k):
                    dve.wait_ge(s_pthi, 8 * i + 4 * h + k + 1)
                    dve.tensor_tensor(pT[:, 1, k, :], ps_pt[k % 2][:, :, :].rearrange("p t n -> p (t n)"),
                                      pT[:, 0, k, :].bitcast(F32), ALU.subtract).then_inc(s_ptlo, 1)

                def o_lo(i, h):
                    dve.wait_ge(s_ohi, 2 * i + h + 1)
                    dve.tensor_tensor(oT[:, 1, h, :], ps_o[:, :], oT[:, 0, h, :].bitcast(F32),
                                      ALU.subtract).then_inc(s_olo, 1)

                def add_y(i, b, t):
                    dve.wait_ge(s_y, 4 * i + t + 1)
                    row = xs[:, b * TB + t, :]
                    dve.tensor_tensor(row, ps_w[(2, 0, 1, 2)[t]][:, :], row, ALU.add).then_inc(s_yadd, 1)

                dve.sem_inc(s_ptlo, 2)
                dve.sem_inc(s_olo, 2)
                dve.sem_inc(s_yadd, 4)
                own = Steps(dve, s_dve)
                own.mark(dve.memset(ones[:, :], 1.0))
                own.wait()
                dve.wait_ge(s_const, 48)
                dve.scalar_tensor_tensor(gain[:, :], gains[:, 0:1], scale, gains[:, 1:2], ALU.mult,
                                         ALU.mult).then_inc(s_gain, 1)
                dve.wait_ge(s_gain, 1)
                split_w(own, 0, KV)
                split_w(own, 0, Q)
                sum_k(own, 0)
                scale_k(0)
                q_lo(0, 0)
                q_lo(0, 1)
                kt_lo(0, 0)
                kt_lo(0, 1)
                sum_q(own, 0)
                v_lo(0, 0)
                v_lo(0, 1)
                split_wo(own, 0)
                dve.wait_ge(s_rq, 1)
                row_max(own, 0, 0)
                row_max(own, 0, 1)
                base = own.n
                per_pair = B * (8 + 3 + 1) + 3

                def iteration(own, hp, b, last):
                    i = hp * B + b
                    j = i + 1
                    more = not isinstance(hp, int)
                    row_recip(i, 0)
                    row_recip(i, 1)
                    row_max(own, i, 2)
                    row_max(own, i, 3)
                    row_recip(i, 2)
                    row_max(own, i, 4)
                    row_recip(i, 3)
                    row_max(own, i, 5)
                    row_recip(i, 4)
                    if not last:
                        sum_k(own, j)
                    row_recip(i, 5)
                    pt_lo(i, 0, 0)
                    pt_lo(i, 0, 1)
                    row_max(own, i, 6)
                    pt_lo(i, 0, 2)
                    row_max(own, i, 7)
                    row_recip(i, 6)
                    pt_lo(i, 0, 3)
                    if not last:
                        q_lo(j, 0)
                    row_recip(i, 7)
                    if not last:
                        scale_k(j)
                        q_lo(j, 1)
                    o_lo(i, 0)
                    if not last:
                        kt_lo(j, 0)
                        kt_lo(j, 1)
                    pt_lo(i, 1, 0)
                    pt_lo(i, 1, 1)
                    pt_lo(i, 1, 2)
                    if not last:
                        sum_q(own, j)
                    pt_lo(i, 1, 3)
                    if b == B - 3 and more:
                        split_wo(own, hp + 1)
                    if b == B - 2 and more:
                        dve.wait_ge(s_v, 2 * j + 2)
                        split_w(own, hp + 1, KV)
                        split_w(own, hp + 1, Q)
                    o_lo(i, 1)
                    if not last:
                        v_lo(j, 0)
                        v_lo(j, 1)
                        dve.wait_ge(s_rq, j + 1)
                        row_max(own, j, 0)
                        row_max(own, j, 1)
                    for t in range(TB):
                        add_y(i, b, t)

                with dve.Fori(0, PAIRS - 1) as hp:
                    own = Steps(dve, s_dve, hp * per_pair + base)
                    for b in range(B):
                        iteration(own, hp, b, False)
                    assert own.n == per_pair, own.n
                own = Steps(dve, s_dve, (PAIRS - 1) * per_pair + base)
                for b in range(B):
                    iteration(own, PAIRS - 1, b, b == B - 1)


def stage_mlp(nc, stage, xs, xT, units, inner, weights, split, resident):
    IC = inner // P
    N_IN = KD * inner
    N_ALL = 2 * N_IN + IC * DIM
    pairs, odd = divmod(units, 2)
    with Scope(nc, stage) as m:
        w = [m.sb(f"w{i}", [P, 2, N_ALL], F32R) for i in range(2)]
        raw = m.sb("raw", [P, N_ALL]) if split else None
        nx = B if resident else 2
        xin = [m.sb(f"xT{i}", [P, 2, KD, S], F32R) for i in range(nx)]
        gated = [m.sb(f"gated{i}", [P, S]) for i in range(2)]
        hid = [m.sb(f"hid{i}", [P, S]) for i in range(2)]
        hT = [m.sb(f"hT{i}", [P, 2, IC, S], F32R) for i in range(2)]
        ps_u = [m.ps(f"up{i}", [P, S]) for i in range(2)]
        ps_g = [m.ps(f"gate{i}", [P, S]) for i in range(2)]
        ps_y = [m.ps(f"y{i}", [P, DIM]) for i in range(TB)]

        s_w = m.sem("w_in")
        s_wraw = m.sem("w_raw_in")
        s_whi, s_wsplit = m.sem("w_hi"), m.sem("w_split")
        s_xT = [m.sem(f"xT_in{i}") for i in range(nx)]
        s_ug = m.sem("up_gate")
        s_silu = m.sem("silu")
        s_h = m.sem("hidden")
        s_hhi = m.sem("hidden_hi")
        s_hlo = m.sem("hidden_lo")
        s_y = m.sem("y")
        s_yadd = m.sem("y_added")

        def every(eng, unit):
            tail = 1 if units == 1 else 3 if odd else 2
            n = (units - tail) // 2
            if n == 0:
                return [unit(u, u % 2, u == units - 1) for u in range(units)]
            with eng.Fori(0, n) as pair:
                unit(pair * 2, 0, False)
                unit(pair * 2 + 1, 1, False)
            for u in range(units - tail, units):
                unit(u, u % 2, u == units - 1)

        def part(par, which, hl, k):
            at = {"gate": 0, "up": N_IN, "down": 2 * N_IN}[which] + k * (inner if which != "down" else DIM)
            return w[par][:, hl, at:at + (inner if which != "down" else DIM)]

        with m.block() as block:
            @block.sync
            def _(sp):
                def load_w(u, par):
                    if split:
                        weights(sp, u, raw, s_wraw)
                    else:
                        weights(sp, u, w[par], s_w)

                load_w(0, 0)
                if resident:
                    for b in range(B):
                        sp.dma_start(xin[b][:, :, :, :].bitcast(F32), xT[b]).then_inc(s_xT[b], 16)
                else:
                    for j in range(2):
                        sp.dma_start(xin[j][:, :, :, :].bitcast(F32), xT[j]).then_inc(s_xT[j], 16)

                def unit(u, par, last):
                    if not last:
                        if split:
                            sp.wait_ge(s_wsplit, u + 1)
                        else:
                            sp.wait_ge(s_yadd, TB + TB * B * u)
                        if isinstance(u, int) and split and u + 1 == units - 1:
                            load_w("last", 1 - par)
                        else:
                            load_w(u + 1, 1 - par)
                    if not resident:
                        for b in range(B):
                            j = u * B + b + 2
                            if not (last and b >= B - 2):
                                sp.wait_ge(s_ug, IC * (j - 1))
                                sp.dma_start(xin[b % 2][:, :, :, :].bitcast(F32), xT[(b + 2) % B]).then_inc(s_xT[b % 2], 16)

                every(sp, unit)

            @block.tensor
            def _(pe):
                def up_gate(u, par, b):
                    j = u * B + b
                    if b == 0:
                        pe.wait_ge(s_wsplit if split else s_w, (u + 1) * (1 if split else 16))
                    if resident:
                        pe.wait_ge(s_xT[b], 16)
                        xi = xin[b]
                    else:
                        pe.wait_ge(s_xT[b % 2], u * 32 + (b // 2) * 16 + 16)
                        xi = xin[b % 2]
                    for ic in range(IC):
                        pe.wait_ge(s_h, IC * j + ic + 1)
                        cols = slice(ic * P, (ic + 1) * P)
                        for which, bank in (("gate", ps_g), ("up", ps_u)):
                            for k in range(KD):
                                mm = split_product(pe, bank[ic % 2][:, :],
                                                   (part(par, which, 0, k)[:, cols], part(par, which, 1, k)[:, cols]),
                                                   (xi[:, 0, k, :], xi[:, 1, k, :]), k == 0, k == KD - 1)
                        mm.then_inc(s_ug, 1)

                def down(u, par, b):
                    i = u * B + b
                    pe.wait_ge(s_hlo, 2 + IC * (i + 1))
                    ht = hT[b % 2]
                    for t in range(TB):
                        pe.wait_ge(s_yadd, TB * i + t + 1)
                        rows = slice(t * P, (t + 1) * P)
                        for ic in range(IC):
                            mm = split_product(pe, ps_y[t][:, :], (ht[:, 0, ic, rows], ht[:, 1, ic, rows]),
                                               (part(par, "down", 0, ic), part(par, "down", 1, ic)),
                                               ic == 0, ic == IC - 1)
                        mm.then_inc(s_y, 1)

                up_gate(0, 0, 0)

                def unit(u, par, last):
                    for b in range(B):
                        if b < B - 1:
                            up_gate(u, par, b + 1)
                        elif not last:
                            up_gate(u + 1, 1 - par, 0)
                        down(u, par, b)

                every(pe, unit)

            @block.scalar
            def _(act):
                def unit(u, par, last):
                    for b in range(B):
                        i = u * B + b
                        for ic in range(IC + 1):
                            if ic < IC:
                                act.wait_ge(s_ug, IC * i + ic + 1)
                                act.wait_ge(s_h, IC * i + ic + 1)
                                act.activation(gated[ic % 2][:, :], ps_g[ic % 2][:, :], ACT.Silu).then_inc(s_silu, 1)
                            if ic > 0:
                                act.wait_ge(s_h, 2 + IC * i + ic)
                                act.copy(hT[b % 2][:, 0, ic - 1, :], hid[(ic - 1) % 2][:, :]).then_inc(s_hhi, 1)

                every(act, unit)

            @block.gpsimd
            def _(pool):
                def unit(u, par, last):
                    for b in range(B):
                        i = u * B + b
                        for ic in range(IC):
                            pool.wait_ge(s_hhi, IC * i + ic + 1)
                            pool.tensor_tensor(hT[b % 2][:, 1, ic, :], hid[ic % 2][:, :],
                                               hT[b % 2][:, 0, ic, :].bitcast(F32), ALU.subtract).then_inc(s_hlo, 1)

                pool.sem_inc(s_hlo, 2)
                every(pool, unit)

            @block.vector
            def _(dve):
                def split_w(u, par):
                    dve.wait_ge(s_wraw, 48 * (u + 1))
                    dve.tensor_copy(w[par][:, 0, :], raw[:, :]).then_inc(s_whi, 1)
                    dve.wait_ge(s_whi, u + 1)
                    dve.tensor_tensor(w[par][:, 1, :], raw[:, :], w[par][:, 0, :].bitcast(F32),
                                      ALU.subtract).then_inc(s_wsplit, 1)

                def hidden(u, b):
                    i = u * B + b
                    for ic in range(IC):
                        dve.wait_ge(s_silu, IC * i + ic + 1)
                        dve.wait_ge(s_hlo, IC * i + ic + 1)
                        dve.tensor_tensor(hid[ic % 2][:, :], ps_u[ic % 2][:, :], gated[ic % 2][:, :],
                                          ALU.mult).then_inc(s_h, 1)

                dve.sem_inc(s_h, 2)
                dve.sem_inc(s_yadd, TB)
                if split:
                    split_w(0, 0)
                hidden(0, 0)

                def unit(u, par, last):
                    for b in range(B):
                        i = u * B + b
                        if b < B - 1:
                            hidden(u, b + 1)
                        elif not last:
                            hidden(u + 1, 0)
                        for t in range(TB):
                            dve.wait_ge(s_y, TB * i + t + 1)
                            row = xs[:, b * TB + t, :]
                            dve.tensor_tensor(row, ps_y[t][:, :], row, ALU.add).then_inc(s_yadd, 1)
                        if split and b == 0 and not last:
                            split_w(u + 1, 1 - par)

                every(dve, unit)


def hadamard_sign(i, j):
    return -1 if bin(i & j).count("1") % 2 else 1


def stage_ffn_weights(nc, wT, W_gate, W_up, W_down, Wscale_ug, Wscale_dp, SU_dp, ident, had):
    INTER = W_gate.shape[0]
    CH, NB = 512, INTER // P
    CHUNKS = INTER // CH
    PART = KD * CH
    srcs = [(W_gate, INTER), (W_up, 0)]
    with Scope(nc, "ffw") as m:
        ident_sb = m.sb("ident", [P, P])
        had_f = m.sb("had_f", [P, P])
        had_r = m.sb("had", [P, P], F32R)
        scales = m.sb("scales", [P, 2 * NB])
        dscale = m.sb("dscale", [P, KD])
        su = m.sb("su", [P, NB])
        raw = [m.sb(f"raw{t}", [P, DIM]) for t in range(TB)]
        scaled = [m.sb(f"scaled{t}", [P, DIM]) for t in range(TB)]
        outT = m.sb("outT", [P, 2, KD, CH], F32R)
        dn = [m.sb(f"down{i}", [P, KD, INTER]) for i in range(2)]
        dT = [m.sb(f"downT{i}", [P, 2, DIM], F32R) for i in range(2)]
        dout = [m.sb(f"dout{i}", [P, 2, 4, DIM], F32R) for i in range(2)]
        banks = [m.ps(f"bank{t}", [P, KD, P]) for t in range(TB)]
        tb = [m.ps(f"turn{i}", [P, DIM]) for i in range(2)]
        hb = [m.ps(f"rot{i}", [P, DIM]) for i in range(2)]

        s_const = m.sem("const_in")
        s_raw = [m.sem(f"raw_in{t}") for t in range(TB)]
        s_scaled = m.sem("scaled")
        s_tr = m.sem("transposed")
        s_hi = m.sem("hi")
        s_lo = m.sem("lo")
        s_out = m.sem("stored")
        s_dn, s_bf = m.sem("down_in"), m.sem("butterflies")
        s_had = m.sem("had_rounded")
        s_dt, s_dthi, s_dtlo = m.sem("downT"), m.sem("downT_hi"), m.sem("downT_lo")
        s_dr, s_drhi, s_drlo = m.sem("rotated"), m.sem("rotated_hi"), m.sem("rotated_lo")
        s_dout = [m.sem(f"down_stored{i}") for i in range(2)]

        with m.block() as block:
            @block.sync
            def _(sp):
                sp.sem_inc(s_out, 16)
                sp.dma_start(dn[0][:, :, :], W_down.rearrange("(k p) n -> p k n", p=P)).then_inc(s_dn, 16)
                sp.dma_start(dscale[:, :], Wscale_dp.rearrange("(k p) -> p k", p=P), allow_slow_non_contiguous=True).then_inc(s_dn, 16)
                sp.dma_start(ident_sb[:, :], ident).then_inc(s_const, 16)
                sp.dma_start(had_f[:, :], had).then_inc(s_const, 16)
                sp.dma_start(scales[:, :], Wscale_ug.rearrange("(n p) -> p n", p=P), allow_slow_non_contiguous=True).then_inc(s_const, 16)
                sp.dma_start(su[:, :], SU_dp.rearrange("(n p) -> p n", p=P), allow_slow_non_contiguous=True).then_inc(s_const, 16)
                for n, (src, _) in enumerate(srcs):
                    rows = src.rearrange("(c t p) d -> c t p d", c=CHUNKS, t=TB)
                    with sp.Fori(0, CHUNKS) as c:
                        i = c + n * CHUNKS
                        for t in range(TB):
                            sp.wait_ge(s_scaled, i * TB + t + 1)
                            sp.dma_start(raw[t][:, :], rows[c, t]).then_inc(s_raw[t], 16)
                        sp.wait_ge(s_lo, (i + 2) * TB)
                        sp.dma_start(wT[c, :, :, n * PART:(n + 1) * PART],
                                     outT[:, :, :, :].bitcast(F32).rearrange("p s k n -> p s (k n)")).then_inc(s_out, 16)
                for c in range(CHUNKS):
                    sp.wait_ge(s_drlo, 4 * (c + 1))
                    sp.dma_start(wT[c, :, :, 2 * PART:3 * PART],
                                 dout[c % 2][:, :, :, :].bitcast(F32).rearrange("p s k n -> p s (k n)")).then_inc(s_dout[c % 2], 16)
                sp.wait_ge(s_out, 16 * (2 * CHUNKS + 1))
                for i in range(2):
                    sp.wait_ge(s_dout[i], 16 * CHUNKS // 2)

            @block.gpsimd
            def _(pool):
                pool.wait_ge(s_dn, 32)
                for k in range(KD):
                    pool.tensor_scalar(dn[0][:, k, :], dn[0][:, k, :], dscale[:, k:k + 1], INTER ** -0.5,
                                       ALU.mult, ALU.mult).then_inc(s_bf, 1)
                done = KD
                for stage in range(NB.bit_length() - 1):
                    src, dst = dn[stage % 2], dn[1 - stage % 2]
                    width = P << stage
                    s_v, d_v = (x[:, :, :].rearrange("p k (g two w) -> p (k g) two w", two=2, w=width) for x in (src, dst))
                    pool.wait_ge(s_bf, done)
                    for two, op in ((0, ALU.add), (1, ALU.subtract)):
                        pool.tensor_tensor(d_v[:, :, two, :], s_v[:, :, 0, :], s_v[:, :, 1, :], op).then_inc(s_bf, 1)
                    done += 2

            @block.vector
            def _(dve):
                dve.sem_inc(s_scaled, TB)
                dve.sem_inc(s_lo, TB)
                dve.wait_ge(s_const, 64)
                dve.tensor_copy(had_r[:, :], had_f[:, :]).then_inc(s_had, 1)
                for n, (_, at) in enumerate(srcs):
                    with dve.Fori(0, CHUNKS) as c:
                        i = c + n * CHUNKS
                        for t in range(TB):
                            dve.wait_ge(s_raw[t], (i + 1) * 16)
                            dve.wait_ge(s_tr, i * TB + t + 1)
                            dve.tensor_scalar(scaled[t][:, :], raw[t][:, :], scales[:, bass.ds(c * TB + (at // P + t), 1)],
                                              None, ALU.mult).then_inc(s_scaled, 1)
                        for t in range(TB):
                            cols = slice(t * P, (t + 1) * P)
                            dve.wait_ge(s_hi, i * TB + t + 1)
                            dve.tensor_tensor(outT[:, 1, :, cols], banks[t][:, :, :], outT[:, 0, :, cols].bitcast(F32),
                                              ALU.subtract).then_inc(s_lo, 1)

                def turned_lo(a):
                    dve.wait_ge(s_dthi, a + 1)
                    dve.tensor_tensor(dT[a % 2][:, 1, :], tb[a % 2][:, :], dT[a % 2][:, 0, :].bitcast(F32),
                                      ALU.subtract).then_inc(s_dtlo, 1)

                def rotated_lo(a):
                    dve.wait_ge(s_drhi, a + 1)
                    o = dout[a // 4 % 2]
                    dve.scalar_tensor_tensor(o[:, 1, a % 4, :], hb[a % 2][:, :], su[:, a:a + 1],
                                             o[:, 0, a % 4, :].bitcast(F32), ALU.mult, ALU.subtract).then_inc(s_drlo, 1)

                turned_lo(0)
                for a in range(NB):
                    if a + 1 < NB:
                        turned_lo(a + 1)
                    rotated_lo(a)

            @block.tensor
            def _(pe):
                pe.sem_inc(s_tr, TB)
                pe.wait_ge(s_const, 64)
                for n in range(2):
                    with pe.Fori(0, CHUNKS) as c:
                        i = c + n * CHUNKS
                        for t in range(TB):
                            pe.wait_ge(s_scaled, (i + 1) * TB + t + 1)
                            pe.wait_ge(s_lo, i * TB + t + 1)
                            for k in range(KD):
                                tr = pe.transpose(banks[t][:, k, :], scaled[t][:, k * P:(k + 1) * P], ident_sb[:, :])
                            tr.then_inc(s_tr, 1)
                dsrc = dn[(NB.bit_length() - 1) % 2]
                pe.wait_ge(s_bf, KD + 2 * (NB.bit_length() - 1))
                pe.wait_ge(s_had, 1)

                def turn(a):
                    if a >= 2:
                        pe.wait_ge(s_dtlo, a - 1)
                    for k in range(KD):
                        tr = pe.transpose(tb[a % 2][:, k * P:(k + 1) * P], dsrc[:, k, a * P:(a + 1) * P], ident_sb[:, :])
                    tr.then_inc(s_dt, 1)

                turn(0)
                for a in range(NB):
                    if a + 1 < NB:
                        turn(a + 1)
                    pe.wait_ge(s_dtlo, a + 1)
                    if a >= 2:
                        pe.wait_ge(s_drlo, a - 1)
                    pe.matmul(hb[a % 2][:, :], had_r[:, :], dT[a % 2][:, 0, :], start=True, stop=False)
                    pe.matmul(hb[a % 2][:, :], had_r[:, :], dT[a % 2][:, 1, :], start=False, stop=True).then_inc(s_dr, 1)

            @block.scalar
            def _(act):
                for n in range(2):
                    with act.Fori(0, CHUNKS) as c:
                        i = c + n * CHUNKS
                        act.wait_ge(s_out, 16 * (i + 1))
                        for t in range(TB):
                            act.wait_ge(s_tr, (i + 1) * TB + t + 1)
                            act.copy(outT[:, 0, :, t * P:(t + 1) * P], banks[t][:, :, :]).then_inc(s_hi, 1)

                def turned_hi(a):
                    act.wait_ge(s_dt, a + 1)
                    if a >= 2:
                        act.wait_ge(s_dr, a - 1)
                    act.copy(dT[a % 2][:, 0, :], tb[a % 2][:, :]).then_inc(s_dthi, 1)

                def rotated_hi(a):
                    act.wait_ge(s_dr, a + 1)
                    if a >= 8 and a % 4 == 0:
                        act.wait_ge(s_dout[a // 4 % 2], 16 * (a // 8))
                    act.activation(dout[a // 4 % 2][:, 0, a % 4, :], hb[a % 2][:, :], ACT.Copy,
                                   scale=su[:, a:a + 1]).then_inc(s_drhi, 1)

                turned_hi(0)
                for a in range(NB):
                    if a + 1 < NB:
                        turned_hi(a + 1)
                    rotated_hi(a)


def stage_rotate(nc, xT, uT, SU, had):
    with Scope(nc, "rot") as m:
        had_f = m.sb("had_f", [P, P])
        su = m.sb("su", [P, KD])
        hs_f = m.sb("hs_f", [P, 2, KD, P])
        hs = m.sb("hs", [P, 2, 2, KD, P], F32R)
        xin = [m.sb(f"x{i}", [P, 2, KD, S], F32R) for i in range(2)]
        out = [m.sb(f"out{i}", [P, 2, KD, S], F32R) for i in range(2)]
        banks = [m.ps(f"bank{k}", [P, S]) for k in range(KD)]
        s_const, s_x = m.sem("const_in"), [m.sem(f"x_in{i}") for i in range(2)]
        s_dve = m.sem("dve_steps")
        s_r, s_hi, s_lo = m.sem("rotated"), m.sem("hi"), m.sem("lo")
        s_out = [m.sem(f"stored{i}") for i in range(2)]
        SC = DIM ** -0.5
        with m.block() as block:
            @block.sync
            def _(sp):
                sp.dma_start(had_f[:, :], had).then_inc(s_const, 16)
                sp.dma_start(su[:, :], SU.rearrange("(k p) -> p k", p=P), allow_slow_non_contiguous=True).then_inc(s_const, 16)
                for b in range(2):
                    sp.dma_start(xin[b][:, :, :, :].bitcast(F32), xT[b]).then_inc(s_x[b], 16)
                for b in range(B):
                    if b + 2 < B:
                        sp.wait_ge(s_r, KD * (b + 1))
                        sp.dma_start(xin[b % 2][:, :, :, :].bitcast(F32), xT[b + 2]).then_inc(s_x[b % 2], 16)
                    sp.wait_ge(s_lo, KD * (b + 1))
                    sp.dma_start(uT[b], out[b % 2][:, :, :, :].bitcast(F32)).then_inc(s_out[b % 2], 16)
                for i in range(2):
                    sp.wait_ge(s_out[i], 16 * B // 2)

            @block.vector
            def _(dve):
                own = Steps(dve, s_dve)
                dve.wait_ge(s_const, 32)
                for k in range(KD):
                    own.mark(dve.tensor_scalar(hs_f[:, 0, k, :], had_f[:, :], su[:, k:k + 1], None, ALU.mult))
                    own.mark(dve.tensor_scalar(hs_f[:, 1, k, :], had_f[:, :], su[:, k:k + 1], -1.0, ALU.mult, ALU.mult))
                own.wait()
                own.after(dve.tensor_copy(hs[:, 0, :, :, :], hs_f[:, :, :, :]))
                own.after(dve.tensor_tensor(hs[:, 1, :, :, :], hs_f[:, :, :, :], hs[:, 0, :, :, :].bitcast(F32), ALU.subtract))
                for b in range(B):
                    for k in range(KD):
                        dve.wait_ge(s_hi, KD * b + k + 1)
                        dve.scalar_tensor_tensor(out[b % 2][:, 1, k, :], banks[k][:, :], SC,
                                                 out[b % 2][:, 0, k, :].bitcast(F32), ALU.mult, ALU.subtract).then_inc(s_lo, 1)

            @block.tensor
            def _(pe):
                pe.wait_ge(s_dve, 2 * KD + 2)
                for b in range(B):
                    pe.wait_ge(s_x[b % 2], 16 * (b // 2 + 1))
                    for ko in range(KD):
                        if b > 0:
                            pe.wait_ge(s_lo, KD * (b - 1) + ko + 1)
                        for k in range(KD):
                            g = 0 if hadamard_sign(k, ko) > 0 else 1
                            mm = split_product(pe, banks[ko][:, :], (hs[:, 0, g, k, :], hs[:, 1, g, k, :]),
                                               (xin[b % 2][:, 0, k, :], xin[b % 2][:, 1, k, :]), k == 0, k == KD - 1)
                        mm.then_inc(s_r, 1)

            @block.scalar
            def _(act):
                for b in range(B):
                    if b >= 2:
                        act.wait_ge(s_out[b % 2], 16 * (b // 2))
                    for k in range(KD):
                        act.wait_ge(s_r, KD * b + k + 1)
                        act.activation(out[b % 2][:, 0, k, :], banks[k][:, :], ACT.Copy, scale=SC).then_inc(s_hi, 1)


STATES = 16
RANK = 16
ET = DIM // P


def stage_ssm_inputs(nc, ctxT, in_proj, conv_w, conv_b, x_proj, dt_proj, dt_bias, u_d, delta_d, du_d, bc_d, ident):
    NX = RANK + 2 * STATES
    TAPS = conv_w.shape[1]
    PAD = TAPS - 1
    with Scope(nc, "ssi") as m:
        ident_sb = m.sb("ident", [P, P])
        in_raw = m.sb("in_raw", [P, ET, CD])
        x_raw = m.sb("x_raw", [NX, DIM])
        dt_raw = m.sb("dt_raw", [P, ET, RANK])
        inT = m.sb("inT", [P, 2, KC, DIM], F32R)
        xT = m.sb("xT", [P, ET, NX])
        dtT = m.sb("dtT", [RANK, DIM])
        taps = m.sb("taps", [P, ET, TAPS])
        cb = m.sb("conv_b", [P, ET])
        db = m.sb("dt_b", [P, ET])
        cx = m.sb("cx", [P, 2, KC, S], F32R)
        xp = [m.sb(f"xp{i}", [P, PAD + S]) for i in range(2)]
        conv = [m.sb(f"conv{i}", [P, S]) for i in range(2)]
        u = m.sb("u", [P, ET, S])
        dbl = m.sb("dbl", [NX, S])
        mag = m.sb("mag", [P, ET, S])
        ex = m.sb("ex", [P, ET, S])
        soft = m.sb("soft", [P, ET, S])
        relu = m.sb("relu", [P, ET, S])
        delta = m.sb("delta", [P, ET, S])
        du = m.sb("du", [P, ET, S])
        ps_t = m.ps("turn", [P, 512])
        ps_x = [m.ps(f"x{i}", [P, S]) for i in range(2)]
        ps_d = m.ps("dbl_ps", [P, S])
        ps_z = [m.ps(f"z{i}", [P, S]) for i in range(ET)]

        s_in = m.sem("weights_in")
        s_t = m.sem("turned")
        s_te = m.sem("turned_out")
        s_tl = m.sem("turned_lo")
        s_cx = m.sem("cx_in")
        s_x, s_xp = m.sem("x"), m.sem("x_padded")
        s_conv, s_u = m.sem("conv"), m.sem("u")
        s_dve = m.sem("dve_steps")
        s_d, s_dbl = m.sem("dbl_made"), m.sem("dbl_copied")
        s_z, s_mag, s_ex, s_soft = m.sem("z"), m.sem("mag_done"), m.sem("exp_done"), m.sem("ln_done")
        s_relu, s_delta, s_du = m.sem("relu_done"), m.sem("delta_done"), m.sem("du_done")
        s_st = [m.sem(f"stored{i}") for i in range(4)]
        with m.block() as block:
            @block.sync
            def _(sp):
                sp.dma_start(ident_sb[:, :], ident).then_inc(s_in, 16)
                sp.dma_start(in_raw[:, :, :], in_proj.rearrange("(t p) d -> p t d", p=P)).then_inc(s_in, 16)
                sp.dma_start(x_raw[:, :], x_proj).then_inc(s_in, 16)
                sp.dma_start(dt_raw[:, :, :], dt_proj.rearrange("(t p) r -> p t r", p=P)).then_inc(s_in, 16)
                sp.dma_start(taps[:, :, :], conv_w.rearrange("(t p) r -> p t r", p=P)).then_inc(s_in, 16)
                sp.dma_start(cb[:, :], conv_b.rearrange("(t p) -> p t", p=P), allow_slow_non_contiguous=True).then_inc(s_in, 16)
                sp.dma_start(db[:, :], dt_bias.rearrange("(t p) -> p t", p=P), allow_slow_non_contiguous=True).then_inc(s_in, 16)
                sp.dma_start(cx[:, :, :, :].bitcast(F32), ctxT[0]).then_inc(s_cx, 16)
                for b in range(B):
                    if b + 1 < B:
                        sp.wait_ge(s_x, ET * (b + 1))
                        sp.dma_start(cx[:, :, :, :].bitcast(F32), ctxT[b + 1]).then_inc(s_cx, 16)
                    sp.wait_ge(s_dbl, b + 1)
                    sp.dma_start(bc_d[b], dbl[RANK:NX, :]).then_inc(s_st[0], 16)
                    sp.wait_ge(s_u, ET * (b + 1))
                    sp.dma_start(u_d[b], u[:, :, :]).then_inc(s_st[1], 16)
                    sp.wait_ge(s_delta, b + 1)
                    sp.dma_start(delta_d[b], delta[:, :, :]).then_inc(s_st[2], 16)
                    sp.wait_ge(s_du, b + 1)
                    sp.dma_start(du_d[b], du[:, :, :]).then_inc(s_st[3], 16)
                for q in s_st:
                    sp.wait_ge(q, 16 * B)

            @block.tensor
            def _(pe):
                pe.wait_ge(s_in, 16 * 7)
                for k in range(KC):
                    if k:
                        pe.wait_ge(s_tl, k)
                    for t in range(ET):
                        tr = pe.transpose(ps_t[:, t * P:(t + 1) * P], in_raw[:, t, k * P:(k + 1) * P], ident_sb[:, :])
                    tr.then_inc(s_t, 1)
                pe.wait_ge(s_tl, KC)
                for t in range(ET):
                    tr = pe.transpose(ps_t[:, t * NX:(t + 1) * NX], x_raw[:, t * P:(t + 1) * P], ident_sb[0:NX, 0:NX])
                tr.then_inc(s_t, 1)
                pe.wait_ge(s_te, KC + 1)
                for t in range(ET):
                    tr = pe.transpose(ps_t[0:RANK, t * P:(t + 1) * P], dt_raw[:, t, :], ident_sb[:, :])
                tr.then_inc(s_t, 1)
                pe.wait_ge(s_te, KC + 2)
                for b in range(B):
                    pe.wait_ge(s_cx, 16 * (b + 1))
                    for t in range(ET):
                        n = b * ET + t
                        if n >= 2:
                            pe.wait_ge(s_xp, n - 1)
                        cols = slice(t * P, (t + 1) * P)
                        for k in range(KC):
                            mm = split_product(pe, ps_x[n % 2][:, :], (inT[:, 0, k, cols], inT[:, 1, k, cols]),
                                               (cx[:, 0, k, :], cx[:, 1, k, :]), k == 0, k == KC - 1)
                        mm.then_inc(s_x, 1)
                    if b:
                        pe.wait_ge(s_dbl, b)
                    for t in range(ET):
                        pe.wait_ge(s_u, b * ET + t + 1)
                        mm = pe.matmul(ps_d[0:NX, :], xT[:, t, :], u[:, t, :], start=(t == 0), stop=(t == ET - 1))
                    mm.then_inc(s_d, 1)
                    pe.wait_ge(s_dbl, b + 1)
                    for t in range(ET):
                        if b:
                            pe.wait_ge(s_relu, b)
                            pe.wait_ge(s_mag, ET * b)
                        pe.matmul(ps_z[t][:, :], dtT[:, t * P:(t + 1) * P], dbl[0:RANK, :], start=True,
                                  stop=True).then_inc(s_z, 1)

            @block.scalar
            def _(act):
                for k in range(KC):
                    act.wait_ge(s_t, k + 1)
                    act.copy(inT[:, 0, k, :], ps_t[:, :]).then_inc(s_te, 1)
                act.wait_ge(s_t, KC + 1)
                act.copy(xT[:, :, :], ps_t[:, 0:ET * NX].rearrange("p (t n) -> p t n", t=ET)).then_inc(s_te, 1)
                act.wait_ge(s_t, KC + 2)
                act.copy(dtT[:, :], ps_t[0:RANK, :]).then_inc(s_te, 1)
                act.wait_ge(s_dve, 2)
                for b in range(B):
                    for t in range(ET + 1):
                        n = b * ET + t
                        if t < ET:
                            act.wait_ge(s_x, n + 1)
                            if n >= 2:
                                act.wait_ge(s_conv, n - 1)
                            act.copy(xp[n % 2][:, PAD:], ps_x[n % 2][:, :]).then_inc(s_xp, 1)
                        if t > 0:
                            act.wait_ge(s_conv, n)
                            if b:
                                act.wait_ge(s_st[1], 16 * b)
                                act.wait_ge(s_du, b)
                            act.activation(u[:, t - 1, :], conv[(n - 1) % 2][:, :], ACT.Silu,
                                           bias=cb[:, t - 1:t]).then_inc(s_u, 1)
                    act.wait_ge(s_d, b + 1)
                    if b:
                        act.wait_ge(s_st[0], 16 * b)
                        act.wait_ge(s_z, ET * b)
                    act.copy(dbl[:, :], ps_d[0:NX, :]).then_inc(s_dbl, 1)
                    for t in range(ET):
                        act.wait_ge(s_z, ET * b + t + 1)
                        act.activation(mag[:, t, :], ps_z[t][:, :], ACT.Abs, bias=db[:, t:t + 1]).then_inc(s_mag, 1)
                    act.wait_ge(s_mag, ET * (b + 1))
                    act.activation(ex[:, :, :], mag[:, :, :], ACT.Exp, scale=-1.0).then_inc(s_ex, 1)
                    act.wait_ge(s_ex, b + 1)
                    if b:
                        act.wait_ge(s_delta, b)
                    act.activation(soft[:, :, :], ex[:, :, :], ACT.Ln, bias=1.0).then_inc(s_soft, 1)

            @block.vector
            def _(dve):
                own = Steps(dve, s_dve)
                for i in range(2):
                    own.mark(dve.memset(xp[i][:, 0:PAD], 0.0))
                for k in range(KC):
                    dve.wait_ge(s_te, k + 1)
                    dve.tensor_tensor(inT[:, 1, k, :], ps_t[:, :], inT[:, 0, k, :].bitcast(F32), ALU.subtract).then_inc(s_tl, 1)
                for b in range(B):
                    for t in range(ET):
                        n = b * ET + t
                        dve.wait_ge(s_xp, n + 1)
                        if n >= 2:
                            dve.wait_ge(s_u, n - 1)
                        c, x = conv[n % 2], xp[n % 2]
                        own.after(dve.tensor_scalar(c[:, :], x[:, 0:S], taps[:, t, 0:1], None, ALU.mult))
                        for j in range(1, TAPS):
                            ins = dve.scalar_tensor_tensor(c[:, :], x[:, j:j + S], taps[:, t, j:j + 1], c[:, :],
                                                           ALU.mult, ALU.add)
                            if j < TAPS - 1:
                                own.after(ins)
                        ins.then_inc(s_conv, 1)
                    dve.wait_ge(s_mag, ET * (b + 1))
                    if b:
                        dve.wait_ge(s_delta, b)
                    for t in range(ET):
                        ins = dve.tensor_scalar(relu[:, t, :], ps_z[t][:, :], db[:, t:t + 1], 0.0, ALU.add, ALU.max)
                    ins.then_inc(s_relu, 1)
                    dve.wait_ge(s_relu, b + 1)
                    dve.wait_ge(s_soft, b + 1)
                    if b:
                        dve.wait_ge(s_st[2], 16 * b)
                        dve.wait_ge(s_st[3], 16 * b)
                    dve.tensor_tensor(delta[:, :, :], relu[:, :, :], soft[:, :, :], ALU.add).then_inc(s_delta, 1)
                    dve.wait_ge(s_delta, b + 1)
                    dve.tensor_tensor(du[:, :, :], delta[:, :, :], u[:, :, :], ALU.mult).then_inc(s_du, 1)


def stage_ssm_gate(nc, xs, u_d, y_d, skip, ident):
    with Scope(nc, "gate") as m:
        ident_sb = m.sb("ident", [P, P])
        d = m.sb("skip", [P, ET])
        rows = [xs[:, b * TB:(b + 1) * TB, :] for b in range(B)]
        u = [m.sb(f"u{i}", [P, ET, S]) for i in range(2)]
        y = [m.sb(f"y{i}", [P, ET, S]) for i in range(2)]
        silu = m.sb("silu", [P, TB, DIM])
        gated = m.sb("gated", [P, ET, S])
        stats = m.sb("stats", [P, TB, 6])
        meanvar = m.sb("meanvar", [P, TB, 2])
        var_eps = m.sb("var_eps", [P, TB])
        rstd = m.sb("rstd", [P, TB])
        shift = m.sb("shift", [P, TB])
        guess = m.sb("guess", [P, TB])
        work = m.sb("work", [P, TB])
        banks = [m.ps(f"bank{t}", [P, ET, P]) for t in range(TB)]
        s_in = m.sem("in")
        s_ld = [m.sem(f"batch_in{i}") for i in range(2)]
        s_dve, s_shift, s_silu = m.sem("dve_steps"), m.sem("shift_done"), m.sem("silu_done")
        s_g, s_t, s_res, s_st = m.sem("gated_done"), m.sem("turned"), m.sem("res_done"), m.sem("stored")
        with m.block() as block:
            @block.sync
            def _(sp):
                sp.dma_start(ident_sb[:, :], ident).then_inc(s_in, 16)
                sp.dma_start(d[:, :], skip.rearrange("(t p) -> p t", p=P), allow_slow_non_contiguous=True).then_inc(s_in, 16)
                for b in range(B):
                    if b >= 2:
                        sp.wait_ge(s_res, TB * (b - 1))
                    sp.dma_start(u[b % 2][:, :, :], u_d[b]).then_inc(s_ld[b % 2], 16)
                    sp.dma_start(y[b % 2][:, :, :], y_d[b]).then_inc(s_ld[b % 2], 16)

            @block.vector
            def _(dve):
                own = Steps(dve, s_dve)
                dve.wait_ge(s_in, 32)
                for b in range(B):
                    for t in range(TB):
                        own.mark(dve.bn_stats(stats[:, t, :], rows[b][:, t, :]))
                    own.wait()
                    for t in range(TB):
                        own.mark(dve.bn_aggr(meanvar[:, t, :], stats[:, t, :]))
                    own.wait()
                    own.after(dve.tensor_scalar(var_eps[:, :], meanvar[:, :, 1], LN_EPS, None, ALU.add))
                    newton_rsqrt(dve, own, rstd[:, :], var_eps[:, :], guess[:, :], work[:, :])
                    dve.scalar_tensor_tensor(shift[:, :], meanvar[:, :, 0], -1.0, rstd[:, :], ALU.mult,
                                             ALU.mult).then_inc(s_shift, 1)
                    dve.wait_ge(s_ld[b % 2], 32 * (b // 2 + 1))
                    for t in range(ET):
                        own.mark(dve.scalar_tensor_tensor(y[b % 2][:, t, :], u[b % 2][:, t, :], d[:, t:t + 1],
                                                          y[b % 2][:, t, :], ALU.mult, ALU.add))
                    own.wait()
                    if b:
                        dve.wait_ge(s_t, TB * b)
                    for t in range(ET):
                        dve.wait_ge(s_silu, TB * b + t + 1)
                        dve.tensor_tensor(gated[:, t, :], y[b % 2][:, t, :], silu[:, t, :], ALU.mult).then_inc(s_g, 1)
                    for t in range(TB):
                        dve.wait_ge(s_t, TB * b + t + 1)
                        dve.tensor_tensor(rows[b][:, t, :], banks[t][:, :, :].rearrange("p e n -> p (e n)"),
                                          rows[b][:, t, :], ALU.add).then_inc(s_res, 1)

            @block.scalar
            def _(act):
                for b in range(B):
                    act.wait_ge(s_shift, b + 1)
                    if b:
                        act.wait_ge(s_g, ET * b)
                    for t in range(TB):
                        act.activation(silu[:, t, :], rows[b][:, t, :], ACT.Silu, bias=shift[:, t:t + 1],
                                       scale=rstd[:, t:t + 1]).then_inc(s_silu, 1)

            @block.tensor
            def _(pe):
                pe.wait_ge(s_in, 32)
                for b in range(B):
                    pe.wait_ge(s_g, ET * (b + 1))
                    for t in range(TB):
                        if b:
                            pe.wait_ge(s_res, TB * (b - 1) + t + 1)
                        for e in range(ET):
                            tr = pe.transpose(banks[t][:, e, :], gated[:, e, t * P:(t + 1) * P], ident_sb[:, :])
                        tr.then_inc(s_t, 1)


EXPERTS = 16


def stage_ffn_scan(nc, xs, uT, wT, A_log, delta_d, du_d, bc_d, y_d):
    INNER, IC = 256, 2
    UNITS = wT.shape[0] * 2
    RING = 4
    PER_STEP = 2 * ET
    PER_BATCH = STATES * ET
    STEPS = 2 * B
    assert UNITS == 2 * B and STEPS * 2 == STATES
    A_v = A_log.rearrange("(t p) n -> p t n", p=P)
    wsrc = wT.rearrange("c p s (w k n) -> c p s w k n", w=3, k=KD)
    with Scope(nc, "ffn") as m:
        xin = [m.sb(f"xT{b}", [P, 2, KD, S], F32R) for b in range(B)]
        w = [m.sb(f"w{i}", [P, 2, 2, KD, INNER], F32R) for i in range(2)]
        wd = m.sb("w_down", [P, 2, IC, DIM], F32R)
        hid = [m.sb(f"hid{i}", [P, S]) for i in range(IC)]
        hT = [m.sb(f"hT{i}", [P, 2, IC, S], F32R) for i in range(2)]
        a_log = m.sb("a_log", [P, ET, STATES])
        a = m.sb("a", [P, ET, STATES])
        delta = m.sb("delta", [P, ET, S])
        du = m.sb("du", [P, ET, S])
        rows = [m.sb(f"rows{i}", [P, 2, S]) for i in range(2)]
        decay = [m.sb(f"decay{i}", [P, S]) for i in range(RING)]
        drive = [m.sb(f"drive{i}", [P, S]) for i in range(RING)]
        y = [m.sb(f"y{t}", [P, S]) for t in range(ET)]
        ps_u = [m.ps(f"up{i}", [P, S]) for i in range(IC)]
        ps_g = [m.ps(f"gate{i}", [P, S]) for i in range(IC)]
        ps_y = [m.ps(f"y{i}_ps", [P, DIM]) for i in range(TB)]

        s_w, s_wd = [m.sem(f"w_in{i}") for i in range(2)], m.sem("w_down_in")
        s_xT = [m.sem(f"xT_in{b}") for b in range(B)]
        s_ug = m.sem("up_gate")
        s_silu = m.sem("silu_done")
        s_h = m.sem("hidden")
        s_hhi = m.sem("hidden_hi")
        s_hlo = m.sem("hidden_lo")
        s_y = m.sem("y_made")
        s_yadd = m.sem("y_added")
        s_a, s_aexp, s_neg = m.sem("a_in"), m.sem("a_exp_done"), m.sem("a_done")
        s_delta, s_du = m.sem("delta_in"), m.sem("du_in")
        s_rows = [m.sem(f"rows_in{i}") for i in range(2)]
        s_decay, s_drive = m.sem("decay_done"), m.sem("drive_done")
        s_scan = m.sem("scanned")
        s_term = m.sem("term_done")
        s_add = m.sem("term_added")
        s_st = [m.sem(f"y_stored{t}") for t in range(ET)]
        s_pace = m.sem("pace")

        def every(eng, step):
            with eng.Fori(0, UNITS // 2 - 1) as p:
                for s in range(STEPS):
                    step(p, s, False)
            for s in range(STEPS):
                step(UNITS // 2 - 1, s, s == STEPS - 1)

        def scans(s, part):
            ms = (range(0, 3), range(3, 6), range(6, PER_STEP))[part]
            return [(s * PER_STEP + k, 2 * s + k // ET, k % ET) for k in ms]

        with m.block() as block:
            @block.sync
            def _(sp):
                def load_w(chunk, half, sem):
                    cols = slice(half * INNER, (half + 1) * INNER)
                    for which in range(2):
                        for hl in range(2):
                            sp.dma_start(w[half][:, hl, which].bitcast(F32), wsrc[chunk, :, hl, which, :, cols]).then_inc(sem, 16)

                def load_down(chunk, half):
                    sp.dma_start(wd[:, :, :, :].bitcast(F32), wsrc[chunk, :, :, 2, half * IC:(half + 1) * IC, :]).then_inc(s_wd, 16)

                def load_rows(b, n):
                    for j in range(2):
                        src = bc_d[b, j * STATES + n:j * STATES + n + 1, :]
                        sp.dma_start(rows[n % 2][:, j, :], src.to_broadcast([P, S])).then_inc(s_rows[n % 2], 16)

                for t in range(ET):
                    sp.sem_inc(s_st[t], 16)
                sp.dma_start(a_log[:, :, :], A_v).then_inc(s_a, 16)
                sp.dma_start(delta[:, :, :], delta_d[0]).then_inc(s_delta, 16)
                load_rows(0, 0)
                load_w(0, 0, s_w[0])
                sp.dma_start(xin[0][:, :, :, :].bitcast(F32), uT[0]).then_inc(s_xT[0], 16)
                sp.dma_start(du[:, :, :], du_d[0]).then_inc(s_du, 16)
                load_rows(0, 1)
                for b in range(1, B):
                    sp.dma_start(xin[b][:, :, :, :].bitcast(F32), uT[b]).then_inc(s_xT[b], 16)
                load_down(0, 0)

                def step(p, s, last):
                    half, b = divmod(s, B)
                    u = p * 2 + half
                    tail = isinstance(p, int)
                    if b == 0 and not (tail and half == 1):
                        wait_apart(sp, s_ug, 1 + IC * B * u, s_pace)
                        load_w(p + half, 1 - half, s_w[1 - half])
                    done = p * PER_BATCH + (s + 1) * PER_STEP
                    if s < STEPS - 1:
                        for k in range(2):
                            wait_apart(sp, s_term, done - PER_STEP + (k + 1) * ET, s_pace)
                            load_rows(p, 2 * s + 2 + k)
                    else:
                        if not tail:
                            wait_apart(sp, s_term, done - ET, s_pace)
                            load_rows(p + 1, 0)
                            wait_apart(sp, s_decay, done, s_pace)
                            sp.dma_start(delta[:, :, :], delta_d[p + 1]).then_inc(s_delta, 16)
                            wait_apart(sp, s_drive, done, s_pace)
                            sp.dma_start(du[:, :, :], du_d[p + 1]).then_inc(s_du, 16)
                        for t in range(ET):
                            wait_apart(sp, s_add, RING + done - ET + t + 1, s_pace)
                            sp.dma_start(y_d[p, :, t, :], y[t][:, :]).then_inc(s_st[t], 16)
                        if not tail:
                            load_rows(p + 1, 1)
                    if b == B - 1 and not last:
                        wait_apart(sp, s_y, TB * B * (u + 1), s_pace)
                        load_down(p + half, 1 - half)

                every(sp, step)
                for t in range(ET):
                    sp.wait_ge(s_st[t], 16 * (B + 1))

            @block.tensor
            def _(pe):
                def up_gate(p, half, b):
                    j = (p * 2 + half) * B + b
                    if b == 0:
                        pe.wait_ge(s_w[half], 64 * (p + 1))
                    pe.wait_ge(s_xT[b], 16)
                    for ic in range(IC):
                        pe.wait_ge(s_h, IC * j + ic + 1)
                        cols = slice(ic * P, (ic + 1) * P)
                        for which, bank in ((0, ps_g), (1, ps_u)):
                            for k in range(KD):
                                mm = split_product(pe, bank[ic][:, :], (w[half][:, 0, which, k, cols], w[half][:, 1, which, k, cols]),
                                                   (xin[b][:, 0, k, :], xin[b][:, 1, k, :]), k == 0, k == KD - 1)
                        mm.then_inc(s_ug, 1)

                def down(p, half, b):
                    u = p * 2 + half
                    i = u * B + b
                    if b == 0:
                        pe.wait_ge(s_wd, 16 * (u + 1))
                    pe.wait_ge(s_hlo, IC + IC * (i + 1))
                    for t in range(TB):
                        pe.wait_ge(s_yadd, TB * i + t + 1)
                        rows = slice(t * P, (t + 1) * P)
                        for ic in range(IC):
                            mm = split_product(pe, ps_y[t][:, :], (hT[b % 2][:, 0, ic, rows], hT[b % 2][:, 1, ic, rows]),
                                               (wd[:, 0, ic, :], wd[:, 1, ic, :]), ic == 0, ic == IC - 1)
                        mm.then_inc(s_y, 1)

                pe.sem_inc(s_ug, 1)
                up_gate(0, 0, 0)

                def step(p, s, last):
                    if not last:
                        up_gate(p + (s + 1) // STEPS, (s + 1) // B % 2, (s + 1) % B)
                    down(p, s // B, s % B)

                every(pe, step)

            @block.scalar
            def _(act):
                def decays(p, s, part):
                    for k, n, t in scans(s, part):
                        wait_apart(act, s_scan, p * PER_BATCH + k + 1, s_pace)
                        act.activation(decay[k % RING][:, :], delta[:, t, :], ACT.Exp,
                                       scale=a[:, t, n:n + 1]).then_inc(s_decay, 1)

                def silu(j, ic):
                    act.wait_ge(s_ug, 1 + IC * j + ic + 1)
                    act.wait_ge(s_hlo, IC * j + ic + 1)
                    act.activation(hid[ic][:, :], ps_g[ic][:, :], ACT.Silu).then_inc(s_silu, 1)

                def hi(j, par, ic):
                    act.wait_ge(s_h, IC + IC * j + ic + 1)
                    act.copy(hT[par][:, 0, ic, :], hid[ic][:, :]).then_inc(s_hhi, 1)

                act.wait_ge(s_a, 16)
                act.activation(a[:, :, :], a_log[:, :, :], ACT.Exp).then_inc(s_aexp, 1)
                act.wait_ge(s_aexp, 1)
                act.mul(a[:, :, :], a[:, :, :], -1.0).then_inc(s_neg, 1)
                act.wait_ge(s_neg, 1)
                for ic in range(IC):
                    silu(0, ic)
                for ic in range(IC):
                    hi(0, 0, ic)

                def step(p, s, last):
                    j = p * STEPS + s + 1
                    if s == 0:
                        act.wait_ge(s_delta, 16 * (p + 1))
                    decays(p, s, 0)
                    if not last:
                        silu(j, 0)
                        silu(j, 1)
                    decays(p, s, 1)
                    if not last:
                        hi(j, (s + 1) % 2, 0)
                    decays(p, s, 2)
                    if not last:
                        hi(j, (s + 1) % 2, 1)

                every(act, step)

            @block.gpsimd
            def _(pool):
                def drives(p, s, part):
                    for k, n, t in scans(s, part):
                        if k % ET == 0:
                            pool.wait_ge(s_rows[n % 2], 32 * (p * STEPS + n // 2 + 1))
                        wait_apart(pool, s_add, p * PER_BATCH + k + 1, s_pace)
                        pool.tensor_tensor(drive[k % RING][:, :], du[:, t, :], rows[n % 2][:, 0, :],
                                           ALU.mult).then_inc(s_drive, 1)

                def lo(j, par, ic):
                    pool.wait_ge(s_hhi, IC * j + ic + 1)
                    pool.tensor_tensor(hT[par][:, 1, ic, :], hid[ic][:, :], hT[par][:, 0, ic, :].bitcast(F32),
                                       ALU.subtract).then_inc(s_hlo, 1)

                pool.sem_inc(s_hlo, IC)
                for ic in range(IC):
                    lo(0, 0, ic)

                def step(p, s, last):
                    j = p * STEPS + s + 1
                    if s == 0:
                        wait_apart(pool, s_du, 16 * (p + 1), s_pace)
                    drives(p, s, 0)
                    drives(p, s, 1)
                    if not last:
                        lo(j, (s + 1) % 2, 0)
                    drives(p, s, 2)
                    if not last:
                        lo(j, (s + 1) % 2, 1)

                every(pool, step)

            @block.vector
            def _(dve):
                def add(p, k, n, t):
                    q = p * PER_BATCH + k
                    dve.wait_ge(s_term, q + 1)
                    if n == 0:
                        dve.sem_inc(s_add, 1)
                    else:
                        dve.wait_ge(s_add, RING + q - ET + 1)
                        dve.tensor_tensor(y[t][:, :], y[t][:, :], drive[k % RING][:, :], ALU.add).then_inc(s_add, 1)

                def scan(p, s, part):
                    for k, n, t in scans(s, part):
                        q = p * PER_BATCH + k
                        d = drive[k % RING]
                        dve.wait_ge(s_decay, q + 1)
                        dve.wait_ge(s_drive, q + 1)
                        dve.tensor_tensor_scan(d[:, :], decay[k % RING][:, :], d[:, :], 0.0, ALU.mult,
                                               ALU.add).then_inc(s_scan, 1)
                        if k:
                            add(p, k - 1, (k - 1) // ET, (k - 1) % ET)
                        dve.wait_ge(s_scan, RING + q + 1)
                        if k % ET == 0:
                            dve.wait_ge(s_rows[n % 2], 32 * (p * STEPS + n // 2 + 1))
                        if n == 0:
                            dve.wait_ge(s_st[t], 16 * (p + 1))
                        dve.tensor_tensor((y[t] if n == 0 else d)[:, :], d[:, :], rows[n % 2][:, 1, :],
                                          ALU.mult).then_inc(s_term, 1)
                        if k == PER_BATCH - 1:
                            add(p, k, n, t)

                def hidden(j, ic):
                    dve.wait_ge(s_silu, IC * j + ic + 1)
                    dve.tensor_tensor(hid[ic][:, :], ps_u[ic][:, :], hid[ic][:, :], ALU.mult).then_inc(s_h, 1)

                def add_y(p, s, t):
                    dve.wait_ge(s_y, TB * (p * STEPS + s) + t + 1)
                    row = xs[:, s % B * TB + t, :]
                    dve.tensor_tensor(row, ps_y[t][:, :], row, ALU.add).then_inc(s_yadd, 1)

                dve.sem_inc(s_h, IC)
                dve.sem_inc(s_yadd, TB)
                dve.sem_inc(s_scan, RING)
                dve.sem_inc(s_add, RING)
                for ic in range(IC):
                    hidden(0, ic)

                def step(p, s, last):
                    j = p * STEPS + s + 1
                    scan(p, s, 0)
                    if not last:
                        hidden(j, 0)
                    scan(p, s, 1)
                    if not last:
                        hidden(j, 1)
                    add_y(p, s, 0)
                    scan(p, s, 2)
                    for t in range(1, TB):
                        add_y(p, s, t)

                every(dve, step)
TILES = 47
WRING = 3


def stage_router(nc, xs, x, xT, Wr, bias, ident, iota, before, token, plan):
    N = B * TB
    EVEN = TILES + TILES % 2
    I32 = mybir.dt.int32
    with Scope(nc, "rou") as m:
        ident_sb = m.sb("ident", [P, P])
        iota_sb = m.sb("iota", [P, P])
        before_sb = m.sb("before", [P, P])
        ones = m.sb("ones", [P, P])
        token_sb = m.sb("token", [P, N])
        bias_sb = m.sb("bias", [P, EXPERTS])
        wr = m.sb("wr", [EXPERTS, DIM])
        wrT = m.sb("wrT", [P, 2, KD, EXPERTS], F32R)
        xin = [m.sb(f"x{b}", [P, 2, KD, S], F32R) for b in range(B)]
        logits = m.sb("logits", [P, N, EXPERTS])
        top = m.sb("top", [P, N])
        ex = m.sb("ex", [P, N, EXPERTS])
        total = m.sb("total", [P, N])
        best = m.sb("best", [P, N, 8])
        where = m.sb("where", [P, N, 8], mybir.dt.uint32)
        wheref = m.sb("wheref", [P, N, 2])
        pick = m.sb("pick", [P, N])
        hot = [m.sb(f"hot{i}", [P, N, EXPERTS]) for i in range(2)]
        chosen = m.sb("chosen", [P, N, EXPERTS])
        pre = m.sb("pre", [P, N + 1, EXPERTS])
        count = m.sb("count", [P, EXPERTS], I32)
        tiles = m.sb("tiles", [P, EXPERTS])
        ends = m.sb("ends", [P, EXPERTS])
        first = m.sb("first", [P, EXPERTS])
        place = m.sb("place", [P, N, EXPERTS])
        mine = m.sb("mine", [P, N, EXPERTS])
        slotf = m.sb("slotf", [P, N, 2])
        part_i = m.sb("part_i", [P, 2, N, 2], I32)
        partf = m.sb("partf", [P, 2, N, 2])
        place_hot = [m.sb(f"place_hot{i}", [P, P], F32R) for i in range(4)]
        tile_hot = [m.sb(f"tile_hot{i}", [P, EVEN], F32R) for i in range(4)]
        over = m.sb("over", [P, TILES, EXPERTS])
        expertf = m.sb("expertf", [P, TILES])
        ps_t = m.ps("turn", [P, KD, EXPERTS])
        ps_l = m.ps("logits_ps", [P, N, EXPERTS])
        ps_c = m.ps("counts_ps", [P, N, EXPERTS])
        ps_r = m.ps("ranks_ps", [P, N, EXPERTS])
        ps_s = m.ps("source_ps", [P, EVEN])
        s_in, s_x = m.sem("in"), [m.sem(f"x_in{b}") for b in range(B)]
        s_t, s_whi, s_wlo, s_l = m.sem("turned"), m.sem("w_hi"), m.sem("w_lo"), m.sem("logits_done")
        s_st = m.sem("stored")
        s_sub, s_ex, s_dve = m.sem("shifted"), m.sem("exp_done"), m.sem("dve_steps")
        s_chosen, s_counts, s_hots, s_source = m.sem("chosen_done"), m.sem("counted"), m.sem("hots"), m.sem("sourced")

        def spread(a, k=EXPERTS):
            return a.rearrange("p (n a) -> p n a", a=1).to_broadcast([P, a.shape[1], k])

        def repeat(a, n=N):
            return a.rearrange("p (a n) -> p a n", a=1).to_broadcast([P, n, a.shape[1]])

        with m.block() as block:
            @block.sync
            def _(sp):
                sp.dma_start(ident_sb[:, :], ident).then_inc(s_in, 16)
                sp.dma_start(wr[:, :], Wr).then_inc(s_in, 16)
                sp.dma_start(bias_sb[:, :], bias.rearrange("(a n) -> a n", a=1).to_broadcast([P, EXPERTS])).then_inc(s_in, 16)
                sp.dma_start(iota_sb[:, :], iota).then_inc(s_in, 16)
                sp.dma_start(before_sb[:, :], before).then_inc(s_in, 16)
                sp.dma_start(token_sb[:, :], token).then_inc(s_in, 16)
                for b in range(B):
                    sp.dma_start(xin[b][:, :, :, :].bitcast(F32), xT[b]).then_inc(s_x[b], 16)
                sp.dma_start(x.rearrange("(n p) d -> p n d", p=P), xs[:, :, :]).then_inc(s_st, 16)
                sp.wait_ge(s_st, 16)

            @block.tensor
            def _(pe):
                pe.wait_ge(s_in, 16 * 6)
                for k in range(KD):
                    tr = pe.transpose(ps_t[:, k, :], wr[:, k * P:(k + 1) * P], ident_sb[0:EXPERTS, 0:EXPERTS])
                tr.then_inc(s_t, 1)
                pe.wait_ge(s_wlo, 1)
                for b in range(B):
                    pe.wait_ge(s_x[b], 16)
                    for t in range(TB):
                        rows = slice(t * P, (t + 1) * P)
                        for k in range(KD):
                            mm = split_product(pe, ps_l[:, b * TB + t, :], (xin[b][:, 0, k, rows], xin[b][:, 1, k, rows]),
                                               (wrT[:, 0, k, :], wrT[:, 1, k, :]), k == 0, k == KD - 1)
                mm.then_inc(s_l, 1)
                pe.wait_ge(s_chosen, 1)
                pe.matmul(ps_c[:, :, :], ones[:, :], chosen[:, :, :], start=True, stop=True)
                pe.matmul(ps_r[:, :, :], before_sb[:, :], chosen[:, :, :], start=True, stop=True).then_inc(s_counts, 1)
                for n in range(2 * N):
                    pe.wait_ge(s_hots, n + 1)
                    pe.matmul(ps_s[:, :], place_hot[n % 4][:, :], tile_hot[n % 4][:, :], start=(n == 0),
                              stop=(n == 2 * N - 1)).then_inc(s_source, 1)

            @block.scalar
            def _(act):
                act.wait_ge(s_t, 1)
                act.copy(wrT[:, 0, :, :], ps_t[:, :, :]).then_inc(s_whi, 1)
                act.wait_ge(s_sub, 1)
                act.activation(ex[:, :, :], logits[:, :, :], ACT.Exp).then_inc(s_ex, 1)

            @block.vector
            def _(dve):
                own = Steps(dve, s_dve)
                dve.wait_ge(s_whi, 1)
                dve.tensor_tensor(wrT[:, 1, :, :], ps_t[:, :, :], wrT[:, 0, :, :].bitcast(F32), ALU.subtract).then_inc(s_wlo, 1)
                own.mark(dve.memset(ones[:, :], 1.0))
                own.mark(dve.memset(pre[:, 0, :], 0.0))
                dve.wait_ge(s_l, 1)
                own.after(dve.tensor_tensor(logits[:, :, :], ps_l[:, :, :], repeat(bias_sb[:, :]), ALU.add))
                own.after(dve.tensor_reduce(top[:, :], logits[:, :, :], AX_X, ALU.max))
                dve.tensor_tensor(logits[:, :, :], logits[:, :, :], spread(top[:, :]), ALU.subtract).then_inc(s_sub, 1)
                dve.wait_ge(s_ex, 1)
                own.after(dve.tensor_reduce(total[:, :], ex[:, :, :], AX_X, ALU.add))
                own.after(dve.reciprocal(total[:, :], total[:, :]))
                own.after(dve.tensor_tensor(ex[:, :, :], ex[:, :, :], spread(total[:, :]), ALU.mult))
                for n in range(N):
                    own.mark(dve.max(best[:, n, :], ex[:, n, :]))
                own.wait()
                for n in range(N):
                    own.mark(dve.max_index(where[:, n, :], best[:, n, :], ex[:, n, :]))
                own.wait()
                own.mark(dve.tensor_copy(wheref[:, :, :], where[:, :, 0:2]))
                own.after(dve.tensor_tensor(pick[:, :], best[:, :, 0], best[:, :, 1], ALU.add))
                own.after(dve.tensor_scalar(pick[:, :], pick[:, :], 1e-9, None, ALU.add))
                own.after(dve.reciprocal(pick[:, :], pick[:, :]))
                for j in range(2):
                    own.mark(dve.tensor_tensor(plan.weight[:, j, :], best[:, :, j], pick[:, :], ALU.mult))
                    own.mark(dve.tensor_tensor(hot[j][:, :, :], repeat(iota_sb[:, 0:EXPERTS]), spread(wheref[:, :, j]),
                                               ALU.is_equal))
                own.wait()
                dve.tensor_tensor(chosen[:, :, :], hot[0][:, :, :], hot[1][:, :, :], ALU.add).then_inc(s_chosen, 1)
                dve.wait_ge(s_counts, 1)
                for n in range(N):
                    own.after(dve.tensor_tensor(pre[:, n + 1, :], pre[:, n, :], ps_c[:, n, :], ALU.add))
                own.after(dve.tensor_scalar(count[:, :], pre[:, N, :], float(P - 1), None, ALU.add))
                own.after(dve.tensor_scalar(count[:, :], count[:, :], 7, None, ALU.logical_shift_right))
                own.after(dve.tensor_copy(tiles[:, :], count[:, :]))
                own.after(dve.tensor_copy(ends[:, 0:1], tiles[:, 0:1]))
                for e in range(1, EXPERTS):
                    own.after(dve.tensor_tensor(ends[:, e:e + 1], ends[:, e - 1:e], tiles[:, e:e + 1], ALU.add))
                own.mark(dve.tensor_copy(plan.ends[:, :], ends[0:1, :]))
                own.after(dve.tensor_tensor(first[:, :], ends[:, :], tiles[:, :], ALU.subtract))
                own.after(dve.tensor_scalar(first[:, :], first[:, :], float(P), None, ALU.mult))
                own.after(dve.tensor_tensor(place[:, :, :], pre[:, 0:N, :], ps_r[:, :, :], ALU.add))
                own.after(dve.tensor_tensor(place[:, :, :], place[:, :, :], repeat(first[:, :]), ALU.add))
                for j in range(2):
                    own.after(dve.tensor_tensor(mine[:, :, :], place[:, :, :], hot[j][:, :, :], ALU.mult))
                    own.after(dve.tensor_reduce(slotf[:, :, j], mine[:, :, :], AX_X, ALU.add))
                own.after(dve.tensor_copy(plan.slot[:, :, :], slotf[:, :, :]))
                own.mark(dve.tensor_scalar(part_i[:, 0, :, :], plan.slot[:, :, :].bitcast(I32), 7, None,
                                           ALU.logical_shift_right))
                own.after(dve.tensor_scalar(part_i[:, 1, :, :], plan.slot[:, :, :].bitcast(I32), P - 1, None,
                                            ALU.bitwise_and))
                own.after(dve.tensor_copy(partf[:, :, :, :], part_i[:, :, :, :]))
                for i in range(2 * N):
                    n, j = divmod(i, 2)
                    if i >= 4:
                        dve.wait_ge(s_source, i - 3)
                    own.mark(dve.tensor_scalar(place_hot[i % 4][:, :], iota_sb[:, :], partf[:, 1, n, j:j + 1], None,
                                               ALU.is_equal))
                    dve.tensor_scalar(tile_hot[i % 4][:, :], iota_sb[:, 0:EVEN], partf[:, 0, n, j:j + 1],
                                      token_sb[:, n:n + 1], ALU.is_equal, ALU.mult).then_inc(s_hots, 1)
                own.after(dve.tensor_tensor(over[:, :, :], repeat(ends[:, :], TILES), spread(iota_sb[:, 0:TILES]),
                                            ALU.is_le))
                own.after(dve.tensor_reduce(expertf[:, :], over[:, :, :], AX_X, ALU.add))
                own.after(dve.tensor_scalar(plan.expert[:, :], expertf[0:1, :], float(EXPERTS - 1), None, ALU.min))
                dve.wait_ge(s_source, 2 * N)
                own.after(dve.tensor_copy(plan.source[:, :], ps_s[:, 0:TILES]))


class Plan:

    def __init__(self, m):
        self.weight = m.sb("weight", [P, 2, B * TB])
        self.slot = m.sb("slot", [P, B * TB, 2], mybir.dt.uint32)
        self.source = m.sb("source", [P, TILES], mybir.dt.uint32)
        self.expert = m.sb("expert", [1, TILES], mybir.dt.int32)
        self.ends = m.sb("ends", [1, EXPERTS], mybir.dt.int32)


def stage_experts(nc, xn, y, Wg, Wu, Wd, ident, plan):
    INNER = Wg.shape[2]
    IC = INNER // P
    N_IN = KD * 2 * INNER
    N_ALL = N_IN + IC * DIM
    GROUPS = [4, 4] + [8] * 4 + [3, 4]
    HELD = 43
    assert sum(GROUPS) == TILES
    with Scope(nc, "exp") as m:
        ident_sb = m.sb("ident", [P, P])
        rows = m.sb("rows", [P, HELD, DIM])
        raw = [m.sb(f"raw{i}", [P, N_ALL]) for i in range(2)]
        w = m.sb("w", [P, WRING, 2, N_ALL], F32R)
        row = [m.sb(f"row{i}", [P, DIM]) for i in range(2)]
        xT = [m.sb(f"xT{i}", [P, 2, KD, P], F32R) for i in range(2)]
        gated = [m.sb(f"gated{i}", [P, INNER]) for i in range(2)]
        hid = [m.sb(f"hid{i}", [P, INNER]) for i in range(2)]
        hT = [m.sb(f"hT{i}", [P, 2, IC, P], F32R) for i in range(2)]
        yout = [m.sb(f"y{i}", [P, DIM]) for i in range(2)]
        ps_x = [m.ps(f"x{i}", [P, KD, P]) for i in range(2)]
        ps_g = [m.ps(f"g{i}", [P, 2, INNER]) for i in range(2)]
        ps_h = [m.ps(f"h{i}", [P, IC, P]) for i in range(2)]
        ps_y = [m.ps(f"y_ps{i}", [P, DIM]) for i in range(2)]
        s_id = m.sem("ident_in")
        s_raw = [m.sem(f"raw_in{i}") for i in range(2)]
        s_gather = [m.sem(f"gathered{g}") for g in range(len(GROUPS))]
        s_rows = m.sem("rows_in")
        s_hi = m.sem("w_hi")
        s_split = m.sem("first_w_hi")
        s_w = m.sem("w_split")
        s_row = m.sem("row_copied")
        s_xt, s_xhi, s_xlo = m.sem("x_turned"), m.sem("x_hi"), m.sem("x_lo")
        s_g, s_silu, s_h = m.sem("gate_up"), m.sem("silu_done"), m.sem("hidden")
        s_ht, s_hhi, s_hlo = m.sem("h_turned"), m.sem("h_hi"), m.sem("h_lo")
        s_y, s_yout = m.sem("y_made"), m.sem("y_copied")
        s_st = [m.sem(f"stored{i}") for i in range(2)]
        s_pace = m.sem("pace")

        def part(par, hl, at, n):
            return w[:, par, hl, at:at + n]

        def tiles(eng, step):
            step(0, 0)
            pairs = (HELD - 3) // 2
            with eng.Fori(0, pairs) as pair:
                step(pair * 2 + 1, 1)
                step(pair * 2 + 2, 0)
            for k in range(2 * pairs + 1, TILES + 1):
                step(k, k % 2)

        def known(k, test):
            return test(k) if isinstance(k, int) else True

        with m.block() as block:
            @block.sync
            def _(sp):
                sp.dma_start(ident_sb[:, :], ident).then_inc(s_id, 16)
                for e in range(EXPERTS):
                    if e >= 2:
                        sp.wait_ge(s_w, e - 1)
                    wi = raw[e % 2][:, 0:N_IN].rearrange("p (k g n) -> p k g n", k=KD, g=2)
                    for g, src in enumerate((Wg, Wu)):
                        sp.dma_start(wi[:, :, g, :], src[e].rearrange("(k p) n -> p k n", p=P)).then_inc(s_raw[e % 2], 16)
                    sp.dma_start(raw[e % 2][:, N_IN:].rearrange("p (k n) -> p k n", k=IC),
                                 Wd[e].rearrange("(k p) n -> p k n", p=P)).then_inc(s_raw[e % 2], 16)

            @block.gpsimd
            def _(pool):
                k = 0
                for g, size in enumerate(GROUPS):
                    for _ in range(size):
                        if k >= HELD:
                            pool.wait_ge(s_row, k - HELD + 1)
                        pool.indirect_dma_start(rows[:, k % HELD, :], None, xn,
                                                bass.IndirectOffsetOnAxis(plan.source[:, k:k + 1], 0)
                                                ).then_inc(s_gather[g], 16)
                        k += 1
                    if g:
                        pool.wait_ge(s_gather[g - 1], 16 * GROUPS[g - 1])
                        pool.sem_inc(s_rows, GROUPS[g - 1])
                pool.wait_ge(s_gather[-1], 16 * GROUPS[-1])
                pool.sem_inc(s_rows, GROUPS[-1])
                for e in range(WRING, EXPERTS):
                    pool.wait_ge(s_raw[e % 2], 48 * (e // 2 + 1))
                    end = pool.value_load(plan.ends[0:1, e - WRING:e - WRING + 1], min_val=0, max_val=TILES)
                    wait_apart(pool, s_y, end + 2, s_pace)
                    pool.tensor_scalar(w[:, e % WRING, 0, :], raw[e % 2][:, :], 1.0, 1.0, ALU.mult, ALU.mult).then_inc(s_hi, 1)
                    pool.wait_ge(s_hi, e - WRING + 1)
                    pool.wait_ge(s_w, e)
                    pool.tensor_tensor(w[:, e % WRING, 1, :], raw[e % 2][:, :], w[:, e % WRING, 0, :].bitcast(F32),
                                       ALU.subtract).then_inc(s_w, 1)

            @block.scalar
            def _(act):
                act.sem_inc(s_st[0], 16)
                act.sem_inc(s_st[1], 16)
                act.sem_inc(s_yout, 2)

                def fetch(k, i):
                    act.wait_ge(s_rows, k + 1)
                    wait_apart(act, s_xt, k + 1, s_pace)
                    act.copy(row[i][:, :], rows[:, k % HELD if isinstance(k, int) else k, :]).then_inc(s_row, 1)

                def x_hi(k, i):
                    act.wait_ge(s_xt, k + 3)
                    act.wait_ge(s_g, k + 1)
                    act.copy(xT[i][:, 0, :, :], ps_x[i][:, :, :]).then_inc(s_xhi, 1)

                fetch(0, 0)
                fetch(1, 1)
                x_hi(0, 0)

                def step(k, i):
                    if known(k, lambda k: k >= 1):
                        act.wait_ge(s_ht, k + 2)
                        act.wait_ge(s_y, k)
                        act.copy(hT[1 - i][:, 0, :, :], ps_h[1 - i][:, :, :]).then_inc(s_hhi, 1)
                    if known(k, lambda k: k + 1 < TILES):
                        x_hi(k + 1, 1 - i)
                    if known(k, lambda k: k + 2 < TILES):
                        fetch(k + 2, i)
                    if known(k, lambda k: k < TILES):
                        act.wait_ge(s_g, k + 3)
                        act.wait_ge(s_h, k + 1)
                        act.activation(gated[i][:, :], ps_g[i][:, 0, :], ACT.Silu).then_inc(s_silu, 1)
                    if known(k, lambda k: k >= 1):
                        act.wait_ge(s_y, k + 2)
                        act.wait_ge(s_st[1 - i], 16 * ((k - 1) // 2 + 1))
                        act.copy(yout[1 - i][:, :], ps_y[1 - i][:, :]).then_inc(s_yout, 1)
                        act.wait_ge(s_yout, k + 2)
                        act.dma_start(y[bass.ds((k - 1) * P, P), :], yout[1 - i][:, :]).then_inc(s_st[1 - i], 16)

                tiles(act, step)
                for i in range(2):
                    act.wait_ge(s_st[i], 16 * ((TILES + 1 - i) // 2 + 1))

            @block.vector
            def _(dve):
                dve.sem_inc(s_xlo, 2)
                dve.sem_inc(s_h, 2)
                dve.sem_inc(s_hlo, 2)
                for e in range(WRING):
                    dve.wait_ge(s_raw[e % 2], 48 * (e // 2 + 1))
                    dve.tensor_copy(w[:, e, 0, :], raw[e % 2][:, :]).then_inc(s_split, 1)
                    dve.wait_ge(s_split, e + 1)
                    dve.tensor_tensor(w[:, e, 1, :], raw[e % 2][:, :], w[:, e, 0, :].bitcast(F32), ALU.subtract).then_inc(s_w, 1)

                def x_lo(k, i):
                    dve.wait_ge(s_xhi, k + 1)
                    dve.tensor_tensor(xT[i][:, 1, :, :], ps_x[i][:, :, :], xT[i][:, 0, :, :].bitcast(F32),
                                      ALU.subtract).then_inc(s_xlo, 1)

                x_lo(0, 0)

                def step(k, i):
                    if known(k, lambda k: k >= 1):
                        dve.wait_ge(s_hhi, k)
                        dve.tensor_tensor(hT[1 - i][:, 1, :, :], ps_h[1 - i][:, :, :], hT[1 - i][:, 0, :, :].bitcast(F32),
                                          ALU.subtract).then_inc(s_hlo, 1)
                    if known(k, lambda k: k + 1 < TILES):
                        x_lo(k + 1, 1 - i)
                    if known(k, lambda k: k < TILES):
                        dve.wait_ge(s_silu, k + 1)
                        dve.wait_ge(s_ht, k + 1)
                        dve.tensor_tensor(hid[i][:, :], ps_g[i][:, 1, :], gated[i][:, :], ALU.mult).then_inc(s_h, 1)

                tiles(dve, step)

            @block.tensor
            def _(pe):
                for sem in (s_xt, s_g, s_ht, s_y):
                    pe.sem_inc(sem, 2)
                pe.wait_ge(s_id, 16)

                def turn_x(k, i):
                    pe.wait_ge(s_row, k + 1)
                    pe.wait_ge(s_xlo, k + 1)
                    for c in range(KD):
                        tr = pe.transpose(ps_x[i][:, c, :], row[i][:, c * P:(c + 1) * P], ident_sb[:, :])
                    tr.then_inc(s_xt, 1)

                def expert(k):
                    return pe.value_load(plan.expert[0:1, bass.ds(k, 1)], min_val=0, max_val=EXPERTS - 1)

                turn_x(0, 0)

                def step(k, i):
                    if known(k, lambda k: k < TILES):
                        now = expert(k)
                        wn = now % WRING
                    if known(k, lambda k: k >= 1):
                        wt = expert(k - 1) % WRING
                        pe.wait_ge(s_h, k + 2)
                        pe.wait_ge(s_hlo, k)
                        for c in range(IC):
                            tr = pe.transpose(ps_h[1 - i][:, c, :], hid[1 - i][:, c * P:(c + 1) * P], ident_sb[:, :])
                        tr.then_inc(s_ht, 1)
                    if known(k, lambda k: k + 1 < TILES):
                        turn_x(k + 1, 1 - i)
                    if known(k, lambda k: k < TILES):
                        pe.wait_ge(s_w, now + 1)
                        pe.wait_ge(s_xlo, k + 3)
                        pe.wait_ge(s_h, k + 1)
                        for c in range(KD):
                            at = c * 2 * INNER
                            mm = split_product(pe, ps_g[i][:, :, :], (xT[i][:, 0, c, :], xT[i][:, 1, c, :]),
                                               (part(wn, 0, at, 2 * INNER), part(wn, 1, at, 2 * INNER)),
                                               c == 0, c == KD - 1)
                        mm.then_inc(s_g, 1)
                    if known(k, lambda k: k >= 1):
                        pe.wait_ge(s_hlo, k + 2)
                        pe.wait_ge(s_yout, k)
                        for c in range(IC):
                            at = N_IN + c * DIM
                            mm = split_product(pe, ps_y[1 - i][:, :], (hT[1 - i][:, 0, c, :], hT[1 - i][:, 1, c, :]),
                                               (part(wt, 0, at, DIM), part(wt, 1, at, DIM)),
                                               c == 0, c == IC - 1)
                        mm.then_inc(s_y, 1)

                tiles(pe, step)


def stage_combine(nc, x, y, out, plan):
    outr = out.rearrange("(b t p) d -> b p t d", b=B, t=TB)
    with Scope(nc, "com") as m:
        acc = [m.sb(f"acc{b}", [P, TB, DIM]) for b in range(B)]
        picked = m.sb("picked", [P, B * TB, 2, DIM])
        s_acc = [m.sem(f"acc_in{b}") for b in range(B)]
        s_picked = [m.sem(f"picked{b}") for b in range(B)]
        s_first, s_sum, s_st = m.sem("first_added"), m.sem("summed"), m.sem("stored")
        with m.block() as block:
            @block.sync
            def _(sp):
                for b in range(B):
                    sp.dma_start(acc[b][:, :, :], x[b * S:(b + 1) * S, :].rearrange("(t p) d -> p t d", p=P)).then_inc(s_acc[b], 16)
                for b in range(B):
                    sp.wait_ge(s_sum, TB * (b + 1))
                    sp.dma_start(outr[b], acc[b][:, :, :]).then_inc(s_st, 16)
                sp.wait_ge(s_st, 16 * B)

            @block.gpsimd
            def _(pool):
                for b in range(B):
                    for n in range(b * TB, (b + 1) * TB):
                        for j in range(2):
                            pool.indirect_dma_start(picked[:, n, j, :], None, y,
                                                    bass.IndirectOffsetOnAxis(plan.slot[:, n, j:j + 1], 0)
                                                    ).then_inc(s_picked[b], 16)

            @block.vector
            def _(dve):
                for b in range(B):
                    dve.wait_ge(s_acc[b], 16)
                    dve.wait_ge(s_picked[b], 16 * 2 * TB)
                    for j, sem in enumerate((s_first, s_sum)):
                        if j:
                            dve.wait_ge(s_first, TB * (b + 1))
                        for t in range(TB):
                            n = b * TB + t
                            dve.scalar_tensor_tensor(acc[b][:, t, :], picked[:, n, j, :], plan.weight[:, j, n:n + 1],
                                                     acc[b][:, t, :], ALU.mult, ALU.add).then_inc(sem, 1)


def build(nc, x, ctx_1024, L0_xattn_Wq, L0_xattn_Wk, L0_xattn_Wv, L0_xattn_Wo, L0_xattn_gq, L0_xattn_gk,
          L0_ffn_SU_ug, L0_ffn_SU_dp, L0_ffn_Wscale_ug, L0_ffn_Wscale_dp, L0_ffn_W_up, L0_ffn_W_gate, L0_ffn_W_down,
          L1_xattn_in_proj_w, L1_xattn_conv_w, L1_xattn_conv_b, L1_xattn_x_proj_w, L1_xattn_dt_proj_w,
          L1_xattn_dt_proj_b, L1_xattn_A_log, L1_xattn_D, L1_ffn_Wr, L1_ffn_bias, L1_ffn_Wg, L1_ffn_Wu, L1_ffn_Wd,
          L1_ffn_sWg, L1_ffn_sWu, L1_ffn_sWd, ident, had, iota, before, token, out):
    def scratch(name, shape):
        return nc.dram_tensor(name, shape, F32).ap()

    x0 = x.rearrange("b s d -> (b s) d")
    result = out.rearrange("b s d -> (b s) d")
    normT = scratch("normT", (B, P, 2, KD, S))
    rotT = scratch("rotT", (B, P, 2, KD, S))
    ctxT = scratch("ctxT", (B, P, 2, KC, S))
    ffnT = scratch("ffnT", (4, P, 2, 3 * KD * 512))
    u_d, delta_d, du_d, y_d = (scratch(n, (B, P, ET, S)) for n in ("u_d", "delta_d", "du_d", "y_d"))
    bc_d = scratch("bc_d", (B, 2 * STATES, S))
    xrows, mixed = scratch("xrows", (B * S, DIM)), scratch("mixed", (B * S, DIM))
    slots = scratch("slots", (TILES * P, DIM))

    decided = ExitStack()
    plan = Plan(decided.enter_context(Memory(nc, "plan")))
    with Memory(nc, "residual") as r:
        xs = r.sb("x", [P, B * TB, DIM])
        stage_norm(nc, "nrm0", xs, normT, ident, x0, ctx_1024, ctxT)
        stage_attention(nc, xs, normT, ctxT, L0_xattn_Wq, L0_xattn_Wk, L0_xattn_Wv, L0_xattn_Wo, L0_xattn_gq,
                        L0_xattn_gk, ident)

        stage_ssm_inputs(nc, ctxT, L1_xattn_in_proj_w, L1_xattn_conv_w, L1_xattn_conv_b, L1_xattn_x_proj_w,
                         L1_xattn_dt_proj_w, L1_xattn_dt_proj_b, u_d, delta_d, du_d, bc_d, ident)
        stage_ffn_weights(nc, ffnT, L0_ffn_W_gate, L0_ffn_W_up, L0_ffn_W_down, L0_ffn_Wscale_ug, L0_ffn_Wscale_dp,
                          L0_ffn_SU_dp, ident, had)
        stage_norm(nc, "nrm1", xs, normT, ident)
        stage_rotate(nc, normT, rotT, L0_ffn_SU_ug, had)

        stage_ffn_scan(nc, xs, rotT, ffnT, L1_xattn_A_log, delta_d, du_d, bc_d, y_d)
        stage_ssm_gate(nc, xs, u_d, y_d, L1_xattn_D, ident)

        stage_norm(nc, "nrm2", xs, normT, ident, rowsout=xrows)

        def shared_weights(sp, u, dst, sem):
            at = 0
            for src in (L1_ffn_sWg, L1_ffn_sWu, L1_ffn_sWd):
                n = src.shape[0] // P * src.shape[1]
                sp.dma_start(dst[:, at:at + n].rearrange("p (k n) -> p k n", k=src.shape[0] // P),
                             src.rearrange("(k p) n -> p k n", p=P)).then_inc(sem, 16)
                at += n

        stage_mlp(nc, "shared", xs, normT, 1, L1_ffn_sWg.shape[1], shared_weights, True, True)
        stage_router(nc, xs, mixed, normT, L1_ffn_Wr, L1_ffn_bias, ident, iota, before, token, plan)

    stage_experts(nc, xrows, slots, L1_ffn_Wg, L1_ffn_Wu, L1_ffn_Wd, ident, plan)
    stage_combine(nc, mixed, slots, result, plan)
    decided.close()


def kernel(**inputs):
    import numpy as _np
    import concourse.bacc as _bacc
    from concourse import mybir as _mybir
    from concourse.bass_utils import run_bass_kernel_spmd as _run

    nc = _bacc.Bacc("TRN2", target_bir_lowering=False, num_devices=1)
    sylvester = _np.ones((1, 1), _np.float32)
    while len(sylvester) < P:
        sylvester = _np.block([[sylvester, sylvester], [sylvester, -sylvester]])
    constants = {
        "ident": _np.eye(P, dtype=_np.float32),
        "had": sylvester,
        "iota": _np.tile(_np.arange(P, dtype=_np.float32), (P, 1)),
        "before": _np.triu(_np.ones((P, P), _np.float32), 1),
        "token": _np.ascontiguousarray(_np.arange(B * S, dtype=_np.float32).reshape(B * TB, P).T),
    }
    arrays, args = {}, {}
    for name, a in {**inputs, **constants}.items():
        a = _np.ascontiguousarray(a)
        arrays[f"in_{name}"] = a
        args[name] = nc.dram_tensor(f"in_{name}", a.shape, _mybir.dt.from_np(a.dtype), kind="ExternalInput").ap()
    args["out"] = nc.dram_tensor("out_0", (B, S, DIM), F32, kind="ExternalOutput").ap()
    build(nc, **args)
    r = _run(nc, [arrays], core_ids=[0])
    return r.results[0]["out_0"]
```

```python
from contextlib import ExitStack

import concourse.bass as bass
from concourse import mybir

F32 = mybir.dt.float32
F32R = mybir.dt.float32r
ALU = mybir.AluOpType
ACT = mybir.ActivationFunctionType
AX_X = mybir.AxisListType.X

P = 128
B = 4
S = 512
TB = S // P
DIM = 512
KD = DIM // P
CD = 256
KC = CD // P
HEADS = 16
LN_EPS = 1e-5


class Steps:

    def __init__(self, eng, sem, base=0):
        self.eng, self.sem, self.base, self.n = eng, sem, base, 0

    def mark(self, ins):
        self.n += 1
        ins.then_inc(self.sem, 1)

    def wait(self):
        self.eng.wait_ge(self.sem, self.base + self.n)

    def wait_apart(self, pace):
        wait_apart(self.eng, self.sem, self.base + self.n, pace)

    def after(self, ins):
        self.mark(ins)
        self.wait()


class Memory:

    def __init__(self, nc, stage):
        self.nc, self.stage, self.stack, self.sems = nc, stage, ExitStack(), []

    def __enter__(self):
        self.stack.__enter__()
        return self

    def __exit__(self, *a):
        return self.stack.__exit__(*a)

    def sb(self, name, shape, dt=F32):
        return self.stack.enter_context(self.nc.sbuf_tensor(f"{self.stage}_{name}", shape, dt))


class Scope(Memory):

    def __exit__(self, *a):
        self.nc.clear_and_free_semaphores(self.sems)
        self.nc.all_engine_barrier()
        return self.stack.__exit__(*a)

    def ps(self, name, shape, dt=F32):
        return self.stack.enter_context(self.nc.psum_tensor(f"{self.stage}_{name}", shape, dt))

    def sem(self, name):
        self.sems.append(self.nc.alloc_semaphore(f"{self.stage}_{name}"))
        return self.sems[-1]

    def block(self):
        return self.nc.Block()


def wait_apart(eng, sem, value, pace):
    eng.wait_ge(sem, value)
    eng.sem_inc(pace, 1)


def split_product(pe, out, lhs, rhs, start, stop):
    (lh, ll), (rh, rl) = lhs, rhs
    pe.matmul(out, lh, rh, start=start, stop=False)
    pe.matmul(out, lh, rl, start=False, stop=False)
    return pe.matmul(out, ll, rh, start=False, stop=stop)


def newton_rsqrt(dve, own, out, value, guess_bits, work):
    own.after(dve.tensor_scalar(guess_bits.bitcast(mybir.dt.int32), value.bitcast(mybir.dt.int32), 1, None,
                                ALU.logical_shift_right))
    own.after(dve.tensor_scalar(out.bitcast(mybir.dt.int32), guess_bits.bitcast(mybir.dt.int32), -1.0,
                                float(0x5F3759DF), ALU.mult, ALU.add))
    for _ in range(3):
        own.after(dve.tensor_tensor(work, out, out, ALU.mult))
        own.after(dve.tensor_tensor(work, work, value, ALU.mult))
        own.after(dve.tensor_scalar(work, work, -0.5, 1.5, ALU.mult, ALU.add))
        last = dve.tensor_tensor(out, out, work, ALU.mult)
        own.after(last)


def stage_norm(nc, stage, xs, xT, ident, x=None, ctx=None, ctxT=None, rowsout=None):
    with Scope(nc, stage) as m:
        ident_sb = m.sb("ident", [P, P])
        normed = [m.sb(f"normed{i}", [P, TB, DIM]) for i in range(2)]
        stats = m.sb("stats", [P, TB, 6])
        meanvar = m.sb("meanvar", [P, TB, 2])
        var_eps = m.sb("var_eps", [P, TB])
        guess = m.sb("guess", [P, TB])
        work = m.sb("work", [P, TB])
        rstd = m.sb("rstd", [P, TB])
        keep = isinstance(xT, list)
        outT = xT if keep else [m.sb(f"outT{i}", [P, 2, KD, S], F32R) for i in range(2)]
        banks = [m.ps(f"bank{t}", [P, KD, P]) for t in range(TB)]
        s_ident = m.sem("ident_in")
        s_x = [m.sem(f"x_in{b}") for b in range(B)]
        s_dve = m.sem("dve_steps")
        s_normed, s_tr, s_hi, s_lo = m.sem("normed"), m.sem("transposed"), m.sem("hi"), m.sem("lo")
        s_out = [m.sem(f"stored{i}") for i in range(2)]
        s_rowsout = [m.sem(f"rows_stored{i}") for i in range(2)]
        if ctx is not None:
            crows = m.sb("crows", [P, B, TB, CD])
            coutT = [m.sb(f"coutT{i}", [P, 2, KC, S], F32R) for i in range(2)]
            cbanks = [m.ps(f"cbank{t}", [P, KD, P]) for t in range(TB)]
            s_crows = [m.sem(f"crows_in{b}") for b in range(B)]
            s_ctr, s_chi, s_clo = m.sem("ctx_transposed"), m.sem("ctx_hi"), m.sem("ctx_lo")
            s_cout = [m.sem(f"ctx_stored{i}") for i in range(2)]

        with m.block() as block:
            @block.sync
            def _(sp):
                sp.dma_start(ident_sb[:, :], ident).then_inc(s_ident, 16)
                for b in range(B):
                    if ctx is not None:
                        sp.dma_start(crows[:, b], ctx[b].rearrange("(t p) d -> p t d", p=P)).then_inc(s_crows[b], 16)
                    if x is not None:
                        rows = x[b * S:(b + 1) * S, :].rearrange("(t p) d -> p t d", p=P)
                        sp.dma_start(xs[:, b * TB:(b + 1) * TB, :], rows).then_inc(s_x[b], 16)
                for b in range(B):
                    if rowsout is not None:
                        sp.wait_ge(s_normed, (b + 1) * TB)
                        rows = rowsout[b * S:(b + 1) * S, :].rearrange("(t p) d -> p t d", p=P)
                        sp.dma_start(rows, normed[b % 2][:, :, :]).then_inc(s_rowsout[b % 2], 16)
                    if ctx is not None:
                        sp.wait_ge(s_clo, (b + 1) * TB)
                        sp.dma_start(ctxT[b], coutT[b % 2][:, :, :, :].bitcast(F32)).then_inc(s_cout[b % 2], 16)
                    if not keep:
                        sp.wait_ge(s_lo, (b + 1) * TB)
                        sp.dma_start(xT[b], outT[b % 2][:, :, :, :].bitcast(F32)).then_inc(s_out[b % 2], 16)
                for i in range(2):
                    if not keep:
                        sp.wait_ge(s_out[i], 16 * B // 2)
                    if rowsout is not None:
                        sp.wait_ge(s_rowsout[i], 16 * B // 2)
                    if ctx is not None:
                        sp.wait_ge(s_cout[i], 16 * B // 2)

            @block.vector
            def _(dve):
                own = Steps(dve, s_dve)

                def normalize(b):
                    if x is not None:
                        dve.wait_ge(s_x[b], 16)
                    for t in range(TB):
                        own.mark(dve.bn_stats(stats[:, t, :], xs[:, b * TB + t, :]))
                    own.wait()
                    for t in range(TB):
                        own.mark(dve.bn_aggr(meanvar[:, t, :], stats[:, t, :]))
                    own.wait()
                    own.after(dve.tensor_scalar(var_eps[:, :], meanvar[:, :, 1], LN_EPS, None, ALU.add))
                    newton_rsqrt(dve, own, rstd[:, :], var_eps[:, :], guess[:, :], work[:, :])
                    if b >= 2:
                        dve.wait_ge(s_tr, (b - 1) * TB)
                        if rowsout is not None:
                            dve.wait_ge(s_rowsout[b % 2], 16)
                    for t in range(TB):
                        dve.tensor_scalar(normed[b % 2][:, t, :], xs[:, b * TB + t, :], meanvar[:, t, 0:1],
                                          rstd[:, t:t + 1], ALU.subtract, ALU.mult).then_inc(s_normed, 1)

                normalize(0)
                for b in range(B):
                    if b + 1 < B:
                        normalize(b + 1)
                    for t in range(TB):
                        part = slice(t * P, (t + 1) * P)
                        if ctx is not None:
                            dve.wait_ge(s_chi, b * TB + t + 1)
                            dve.tensor_tensor(coutT[b % 2][:, 1, :, part], cbanks[t][:, 0:KC, :],
                                              coutT[b % 2][:, 0, :, part].bitcast(F32), ALU.subtract).then_inc(s_clo, 1)
                        dve.wait_ge(s_hi, b * TB + t + 1)
                        o = outT[b % len(outT)]
                        dve.tensor_tensor(o[:, 1, :, part], banks[t][:, :, :], o[:, 0, :, part].bitcast(F32),
                                          ALU.subtract).then_inc(s_lo, 1)

            @block.tensor
            def _(pe):
                pe.wait_ge(s_ident, 16)
                for b in range(B):
                    for t in range(TB):
                        if ctx is not None:
                            pe.wait_ge(s_crows[b], 16)
                            if b:
                                pe.wait_ge(s_clo, (b - 1) * TB + t + 1)
                            for k in range(KC):
                                tr = pe.transpose(cbanks[t][:, k, :], crows[:, b, t, k * P:(k + 1) * P], ident_sb[:, :])
                            tr.then_inc(s_ctr, 1)
                    for t in range(TB):
                        pe.wait_ge(s_normed, b * TB + t + 1)
                        if b:
                            pe.wait_ge(s_lo, (b - 1) * TB + t + 1)
                        for k in range(KD):
                            tr = pe.transpose(banks[t][:, k, :], normed[b % 2][:, t, k * P:(k + 1) * P], ident_sb[:, :])
                        tr.then_inc(s_tr, 1)

            @block.scalar
            def _(act):
                for b in range(B):
                    if b >= 2:
                        if not keep:
                            act.wait_ge(s_out[b % 2], 16)
                        if ctx is not None:
                            act.wait_ge(s_cout[b % 2], 16)
                    for t in range(TB):
                        part = slice(t * P, (t + 1) * P)
                        if ctx is not None:
                            act.wait_ge(s_ctr, b * TB + t + 1)
                            act.copy(coutT[b % 2][:, 0, :, part], cbanks[t][:, 0:KC, :]).then_inc(s_chi, 1)
                        act.wait_ge(s_tr, b * TB + t + 1)
                        act.copy(outT[b % len(outT)][:, 0, :, part], banks[t][:, :, :]).then_inc(s_hi, 1)


def stage_attention(nc, xs, xT, ctxT, Wq, Wk, Wv, Wo, gq, gk, ident):
    D = P
    HP = 2
    PAIRS = HEADS // HP
    W2 = HP * D
    RMS_EPS = 1e-5
    NEWTON = 3
    scale = D ** -0.5
    wq_d = Wq.rearrange("(k p) n -> p k n", p=P)
    wk_d = Wk.rearrange("(k p) n -> p k n", p=P)
    wv_d = Wv.rearrange("(k p) n -> p k n", p=P)
    wo_d = Wo.rearrange("(h p) n -> p h n", p=P)
    NQ, NKV = KD * W2, KC * W2
    with Scope(nc, "att") as m:
        ident_sb = m.sb("ident", [P, P])
        ones = m.sb("ones", [P, 1])
        gains = m.sb("gains", [P, 2])
        gain = m.sb("gain", [P, 1])
        raw = m.sb("raw_qkv", [P, NQ + 2 * NKV])
        raw_o = m.sb("raw_o", [P, HP, DIM])
        w = m.sb("w_qkv", [P, 2, NQ + 2 * NKV], F32R)
        wo = m.sb("wo", [P, 2, 2, HP, DIM], F32R)
        xn = m.sb("xn", [P, 2, KD, S], F32R)
        cxs = [m.sb(f"cx{b}", [P, 2, KC, S], F32R) for b in range(B)]
        kn = m.sb("kn", [P, TB, HP, D])
        ksq = m.sb("ksq", [P, TB, HP, D])
        qsq = m.sb("qsq", [P, HP, S])
        qT = m.sb("qT", [P, 2, HP, S], F32R)
        kT = m.sb("kT", [P, 2, HP, S], F32R)
        v = m.sb("v", [P, 2, TB, W2], F32R)
        probs = m.sb("probs", [P, HP * TB, S])
        pT = m.sb("pT", [P, 2, TB, S], F32R)
        oT = m.sb("oT", [P, 2, HP, S], F32R)
        kss = m.sb("kss", [P, TB * HP])
        qss = m.sb("qss", [P, TB * HP])
        rk = m.sb("rk", [P, TB * HP])
        rq = m.sb("rq", [P, TB * HP])
        kguess = m.sb("kguess", [P, TB * HP])
        qguess = m.sb("qguess", [P, TB * HP])
        work = m.sb("work", [P, TB * HP])
        nmax = m.sb("nmax", [P, TB * HP])
        bias = m.sb("bias", [P, TB * HP])
        sums = m.sb("sums", [P, TB * HP])
        recip = m.sb("recip", [P, TB * HP])
        ps_s = [m.ps(f"s{i}", [P, S]) for i in range(2)]
        ps_pt = [m.ps(f"pt{i}", [P, TB, P]) for i in range(2)]
        ps_w = [m.ps(f"w{i}", [P, 512]) for i in range(3)]
        ps_o = m.ps("o", [P, S])

        s_const = m.sem("const_in")
        s_gain = m.sem("gain")
        s_raw, s_rawo = m.sem("raw_in"), m.sem("raw_o_in")
        s_w, s_wo = m.sem("w_split"), m.sem("wo_split")
        s_xn, s_cx = m.sem("xn_in"), [m.sem(f"cx_in{b}") for b in range(B)]
        s_s = m.sem("scores")
        s_max = m.sem("max")
        s_exp = m.sem("exp")
        s_rec = m.sem("recip")
        s_pn = m.sem("probs_normed")
        s_k, s_kc, s_ksq, s_kn = m.sem("k"), m.sem("k_copied"), m.sem("k_squared"), m.sem("k_normed")
        s_kt, s_kthi, s_ktlo = m.sem("kT"), m.sem("kT_hi"), m.sem("kT_lo")
        s_q, s_qhi, s_qsq, s_qlo = m.sem("q"), m.sem("q_hi"), m.sem("q_squared"), m.sem("q_lo")
        s_kss, s_rk, s_qss, s_pool = m.sem("k_sums"), m.sem("rk"), m.sem("q_squares"), m.sem("pool_steps")
        s_ss, s_ssread, s_rq = m.sem("q_sums"), m.sem("q_sums_read"), m.sem("rq")
        s_v, s_vhi, s_vlo = m.sem("v"), m.sem("v_hi"), m.sem("v_lo")
        s_pt, s_pthi = m.sem("pT"), m.sem("pT_hi")
        s_ptlo = m.sem("pT_lo")
        s_pv, s_ohi = m.sem("pv"), m.sem("o_hi")
        s_olo = m.sem("o_lo")
        s_y = m.sem("y")
        s_yadd = m.sem("y_added")
        s_dve = m.sem("dve_steps")
        s_pace = m.sem("pace")

        def pairs(eng, iteration):
            with eng.Fori(0, PAIRS - 1) as hp:
                for b in range(B):
                    iteration(hp, b, False)
            for b in range(B):
                iteration(PAIRS - 1, b, b == B - 1)

        def wpart(part, which, k):
            at = {"q": 0, "k": NQ, "v": NQ + NKV}[which] + k * W2
            return w[:, part, at:at + W2]

        with m.block() as block:
            @block.sync
            def _(sp):
                def load_weights(hp):
                    sp.dma_start(raw[:, 0:NQ].rearrange("p (k n) -> p k n", k=KD), wq_d[:, :, bass.ds(hp * W2, W2)]).then_inc(s_raw, 16)
                    for at, src in ((NQ, wk_d), (NQ + NKV, wv_d)):
                        sp.dma_start(raw[:, at:at + NKV].rearrange("p (k n) -> p k n", k=KC),
                                     src[:, :, bass.ds(hp * W2, W2)]).then_inc(s_raw, 16)

                def load_wo(hp):
                    sp.dma_start(raw_o[:, :, :], wo_d[:, bass.ds(hp * HP, HP), :]).then_inc(s_rawo, 16)

                sp.dma_start(ident_sb[:, :], ident).then_inc(s_const, 16)
                sp.dma_start(gains[:, 0:1], gq.rearrange("(p a) -> p a", a=1)).then_inc(s_const, 16)
                sp.dma_start(gains[:, 1:2], gk.rearrange("(p a) -> p a", a=1)).then_inc(s_const, 16)
                load_weights(0)
                sp.dma_start(cxs[0][:, :, :, :].bitcast(F32), ctxT[0]).then_inc(s_cx[0], 16)
                sp.dma_start(xn[:, :, :, :].bitcast(F32), xT[0]).then_inc(s_xn, 16)
                load_wo(0)
                for b in range(1, B):
                    sp.dma_start(cxs[b][:, :, :, :].bitcast(F32), ctxT[b]).then_inc(s_cx[b], 16)

                def iteration(hp, b, last):
                    i = hp * B + b
                    if not last:
                        sp.wait_ge(s_q, 2 * i + 2)
                        sp.dma_start(xn[:, :, :, :].bitcast(F32), xT[(b + 1) % B]).then_inc(s_xn, 16)
                    if b == 0 and not (isinstance(hp, int) and hp == PAIRS - 1):
                        sp.wait_ge(s_w, 2 * hp + 2)
                        load_weights(hp + 1)
                        sp.wait_ge(s_wo, hp + 1)
                        load_wo(hp + 1)

                pairs(sp, iteration)

            @block.tensor
            def _(pe):
                def score(i, n):
                    h, t = divmod(n, TB)
                    if n == 0:
                        pe.wait_ge(s_ktlo, 2 * i + 2)
                        pe.wait_ge(s_qlo, 2 * i + 2)
                    pe.wait_ge(s_exp, 8 * i + n + 1)
                    q = slice(t * P, (t + 1) * P)
                    split_product(pe, ps_s[n % 2][:, :], (qT[:, 0, h, q], qT[:, 1, h, q]),
                                  (kT[:, 0, h, :], kT[:, 1, h, :]), True, True).then_inc(s_s, 1)

                def kv(cx, which, half, bank, sem):
                    for a in range(2):
                        t = 2 * half + a
                        rows = slice(t * P, (t + 1) * P)
                        for k in range(KC):
                            mm = split_product(pe, ps_w[bank][:, a * W2:(a + 1) * W2],
                                               (cx[:, 0, k, rows], cx[:, 1, k, rows]),
                                               (wpart(0, which, k), wpart(1, which, k)), k == 0, k == KC - 1)
                    mm.then_inc(sem, 1)

                def queries(h, bank):
                    d = slice(h * D, (h + 1) * D)
                    for k in range(KD):
                        mm = split_product(pe, ps_w[bank][:, :], (wpart(0, "q", k)[:, d], wpart(1, "q", k)[:, d]),
                                           (xn[:, 0, k, :], xn[:, 1, k, :]), k == 0, k == KD - 1)
                    mm.then_inc(s_q, 1)

                def turn_k(h, bank):
                    for t in range(TB):
                        tr = pe.transpose(ps_w[bank][:, t * P:(t + 1) * P], kn[:, t, h, :], ident_sb[:, :])
                    tr.then_inc(s_kt, 1)

                def sums_q():
                    for n in range(HP * TB):
                        h, t = divmod(n, TB)
                        mm = pe.matmul(ps_o[:, n:n + 1], qsq[:, h, t * P:(t + 1) * P], ones[:, :], start=True, stop=True)
                    mm.then_inc(s_ss, 1)

                def turn_p(i, h, k):
                    n = 8 * i + 4 * h + k
                    if k == 0:
                        pe.wait_ge(s_pn, 8 * i + 4 * h + 4)
                    pe.wait_ge(s_ptlo, n + 1)
                    for t in range(TB):
                        tr = pe.transpose(ps_pt[k % 2][:, t, :], probs[:, h * TB + t, k * P:(k + 1) * P], ident_sb[:, :])
                    tr.then_inc(s_pt, 1)

                def pv(i, h):
                    pe.wait_ge(s_ptlo, 8 * i + 4 * h + 4 + 2)
                    d = slice(h * D, (h + 1) * D)
                    for k in range(TB):
                        mm = split_product(pe, ps_o[:, :], (v[:, 0, k, d], v[:, 1, k, d]),
                                           (pT[:, 0, k, :], pT[:, 1, k, :]), k == 0, k == TB - 1)
                    mm.then_inc(s_pv, 1)

                def project(hp, t, bank):
                    rows = slice(t * P, (t + 1) * P)
                    for h in range(HP):
                        mm = split_product(pe, ps_w[bank][:, :], (oT[:, 0, h, rows], oT[:, 1, h, rows]),
                                           (wo[:, hp % 2, 0, h, :], wo[:, hp % 2, 1, h, :]), h == 0, h == HP - 1)
                    mm.then_inc(s_y, 1)

                pe.wait_ge(s_const, 48)
                pe.wait_ge(s_gain, 1)
                pe.wait_ge(s_w, 2)
                pe.wait_ge(s_cx[0], 16)
                kv(cxs[0], "k", 0, 0, s_k)
                kv(cxs[0], "k", 1, 1, s_k)
                pe.wait_ge(s_xn, 16)
                queries(0, 2)
                pe.wait_ge(s_kc, 1)
                queries(1, 0)
                pe.wait_ge(s_kn, 1)
                turn_k(0, 1)
                pe.wait_ge(s_qlo, 1)
                turn_k(1, 2)
                pe.wait_ge(s_qsq, 2)
                sums_q()
                pe.wait_ge(s_qlo, 2)
                kv(cxs[0], "v", 0, 0, s_v)
                pe.wait_ge(s_ktlo, 1)
                kv(cxs[0], "v", 1, 1, s_v)
                score(0, 0)
                score(0, 1)

                def iteration(hp, b, last):
                    i = hp * B + b
                    j = i + 1
                    cx = cxs[(b + 1) % B]
                    score(i, 2)
                    score(i, 3)
                    if not last:
                        pe.wait_ge(s_w, (2 * hp + 3) if b == B - 1 else (2 * hp + 2))
                        pe.wait_ge(s_cx[(b + 1) % B], 16)
                        pe.wait_ge(s_yadd, 4 * i + 2)
                        kv(cx, "k", 0, 0, s_k)
                    score(i, 4)
                    if not last:
                        pe.wait_ge(s_yadd, 4 * i + 3)
                        kv(cx, "k", 1, 1, s_k)
                    score(i, 5)
                    if not last:
                        pe.wait_ge(s_xn, 16 * j + 16)
                        if b == B - 1:
                            pe.wait_ge(s_w, 2 * hp + 4)
                        pe.wait_ge(s_yadd, 4 * i + 4)
                        queries(0, 2)
                    turn_p(i, 0, 0)
                    turn_p(i, 0, 1)
                    score(i, 6)
                    score(i, 7)
                    turn_p(i, 0, 2)
                    turn_p(i, 0, 3)
                    if not last:
                        pe.wait_ge(s_kc, 2 * j + 1)
                        queries(1, 0)
                    pe.wait_ge(s_vlo, 2 * i + 2)
                    pe.wait_ge(s_olo, 2 * i + 2)
                    pv(i, 0)
                    if not last:
                        pe.wait_ge(s_kn, j + 1)
                        turn_k(0, 1)
                        pe.wait_ge(s_qlo, 2 * j + 1)
                        turn_k(1, 2)
                    turn_p(i, 1, 0)
                    turn_p(i, 1, 1)
                    if not last:
                        pe.wait_ge(s_qlo, 2 * j + 2)
                        kv(cx, "v", 0, 0, s_v)
                    turn_p(i, 1, 2)
                    pe.wait_ge(s_olo, 2 * i + 3)
                    if not last:
                        pe.wait_ge(s_qsq, 2 * j + 2)
                        sums_q()
                    turn_p(i, 1, 3)
                    if not last:
                        pe.wait_ge(s_ktlo, 2 * j + 1)
                        kv(cx, "v", 1, 1, s_v)
                        pe.wait_ge(s_ssread, j + 1)
                    pv(i, 1)
                    if not last:
                        score(j, 0)
                        score(j, 1)
                    pe.wait_ge(s_olo, 2 * i + 4)
                    pe.wait_ge(s_wo, hp + 1)
                    project(hp, 0, 2)
                    if not last:
                        pe.wait_ge(s_vlo, 2 * j + 1)
                    project(hp, 1, 0)
                    if not last:
                        pe.wait_ge(s_vlo, 2 * j + 2)
                    project(hp, 2, 1)
                    pe.wait_ge(s_yadd, 4 + 4 * i + 1)
                    project(hp, 3, 2)

                pairs(pe, iteration)

            @block.scalar
            def _(act):
                def copy_k(j, half):
                    act.wait_ge(s_k, 2 * j + half + 1)
                    act.copy(kn[:, 2 * half:2 * half + 2, :, :], ps_w[half][:, :]).then_inc(s_kc, 1)

                def q_parts(j, h):
                    bank = ps_w[(2, 0)[h]]
                    act.wait_ge(s_q, 2 * j + h + 1)
                    act.copy(qT[:, 0, h, :], bank[:, :]).then_inc(s_qhi, 1)
                    act.activation(qsq[:, h, :], bank[:, :], ACT.Square).then_inc(s_qsq, 1)

                def kt_hi(j, h):
                    act.wait_ge(s_kt, 2 * j + h + 1)
                    act.activation(kT[:, 0, h, :], ps_w[1 + h][:, :], ACT.Copy, scale=gain[:, 0:1]).then_inc(s_kthi, 1)

                def v_hi(j, half):
                    act.wait_ge(s_v, 2 * j + half + 1)
                    act.copy(v[:, 0, 2 * half:2 * half + 2, :], ps_w[half][:, :]).then_inc(s_vhi, 1)

                def exp(i, n):
                    act.wait_ge(s_max, 8 * i + n + 1)
                    act.activation(probs[:, n, :], ps_s[n % 2][:, :], ACT.Exp, bias=bias[:, n:n + 1],
                                   scale=rq[:, n:n + 1], accum_out=sums[:, n:n + 1]).then_inc(s_exp, 1)

                def pt_hi(i, h, k):
                    act.wait_ge(s_pt, 8 * i + 4 * h + k + 1)
                    act.copy(pT[:, 0, k, :], ps_pt[k % 2][:, :, :]).then_inc(s_pthi, 1)

                def o_hi(i, h):
                    act.wait_ge(s_pv, 2 * i + h + 1)
                    act.copy(oT[:, 0, h, :], ps_o[:, :]).then_inc(s_ohi, 1)

                act.sem_inc(s_exp, 2)
                act.wait_ge(s_gain, 1)
                copy_k(0, 0)
                copy_k(0, 1)
                q_parts(0, 0)
                q_parts(0, 1)
                kt_hi(0, 0)
                kt_hi(0, 1)
                v_hi(0, 0)
                v_hi(0, 1)
                act.wait_ge(s_rq, 1)
                exp(0, 0)
                exp(0, 1)

                def iteration(hp, b, last):
                    i = hp * B + b
                    j = i + 1
                    exp(i, 2)
                    exp(i, 3)
                    if not last:
                        copy_k(j, 0)
                    exp(i, 4)
                    if not last:
                        copy_k(j, 1)
                    exp(i, 5)
                    pt_hi(i, 0, 0)
                    pt_hi(i, 0, 1)
                    pt_hi(i, 0, 2)
                    exp(i, 6)
                    pt_hi(i, 0, 3)
                    if not last:
                        q_parts(j, 0)
                    exp(i, 7)
                    if not last:
                        q_parts(j, 1)
                    o_hi(i, 0)
                    if not last:
                        kt_hi(j, 0)
                        kt_hi(j, 1)
                    for k in range(TB):
                        pt_hi(i, 1, k)
                    o_hi(i, 1)
                    if not last:
                        v_hi(j, 0)
                        v_hi(j, 1)
                        act.wait_ge(s_rq, j + 1)
                        exp(j, 0)
                        exp(j, 1)

                pairs(act, iteration)

            @block.gpsimd
            def _(pool):
                def square_k(j):
                    pool.wait_ge(s_kc, 2 * j + 2)
                    pool.tensor_tensor(ksq[:, :, :, :], kn[:, :, :, :], kn[:, :, :, :], ALU.mult).then_inc(s_ksq, 1)

                def norm_p(i, n):
                    wait_apart(pool, s_rec, 8 * i + n + 1, s_pace)
                    pool.tensor_scalar(probs[:, n, :], probs[:, n, :], recip[:, n:n + 1], 1.0, ALU.mult,
                                       ALU.mult).then_inc(s_pn, 1)

                def newton(own, out, value, guess, work):
                    cur = guess
                    for _ in range(NEWTON):
                        own.mark(pool.tensor_tensor(work, cur, cur, ALU.mult))
                        own.wait_apart(s_pace)
                        own.mark(pool.tensor_tensor(work, work, value, ALU.mult))
                        own.wait_apart(s_pace)
                        own.mark(pool.tensor_scalar(work, work, -0.5, 1.5, ALU.mult, ALU.add))
                        own.wait_apart(s_pace)
                        own.mark(pool.tensor_tensor(out, cur, work, ALU.mult))
                        own.wait_apart(s_pace)
                        cur = out

                def norm_k(own, j):
                    wait_apart(pool, s_kss, j + 1, s_pace)
                    newton(own, rk[:, :], kss[:, :], kguess[:, :], work[:, :])
                    pool.sem_inc(s_rk, 1)

                def norm_q(own, j):
                    wait_apart(pool, s_qss, j + 1, s_pace)
                    newton(own, rq[:, :], qss[:, :], qguess[:, :], work[:, :])
                    pool.sem_inc(s_rq, 1)

                own = Steps(pool, s_pool)
                square_k(0)
                norm_k(own, 0)
                norm_q(own, 0)
                base = own.n
                per_pair = B * base

                def iteration(own, hp, b, last):
                    i = hp * B + b
                    j = i + 1
                    for n in range(4):
                        norm_p(i, n)
                    if not last:
                        square_k(j)
                    norm_p(i, 4)
                    norm_p(i, 5)
                    if not last:
                        norm_k(own, j)
                    norm_p(i, 6)
                    norm_p(i, 7)
                    if not last:
                        norm_q(own, j)

                with pool.Fori(0, PAIRS - 1) as hp:
                    own = Steps(pool, s_pool, hp * per_pair + base)
                    for b in range(B):
                        iteration(own, hp, b, False)
                own = Steps(pool, s_pool, (PAIRS - 1) * per_pair + base)
                for b in range(B):
                    iteration(own, PAIRS - 1, b, b == B - 1)

            @block.vector
            def _(dve):
                def split_w(own, hp, cols):
                    dve.wait_ge(s_raw, 48 * (hp + 1))
                    own.after(dve.tensor_copy(w[:, 0, cols], raw[:, cols]))
                    dve.tensor_tensor(w[:, 1, cols], raw[:, cols], w[:, 0, cols].bitcast(F32),
                                      ALU.subtract).then_inc(s_w, 1)

                KV, Q = slice(NQ, NQ + 2 * NKV), slice(0, NQ)

                def split_wo(own, hp):
                    dve.wait_ge(s_rawo, 16 * (hp + 1))
                    own.after(dve.tensor_copy(wo[:, hp % 2, 0, :, :], raw_o[:, :, :]))
                    dve.tensor_tensor(wo[:, hp % 2, 1, :, :], raw_o[:, :, :], wo[:, hp % 2, 0, :, :].bitcast(F32),
                                      ALU.subtract).then_inc(s_wo, 1)

                def row_max(own, i, n):
                    dve.wait_ge(s_s, 8 * i + n + 1)
                    own.after(dve.tensor_reduce(nmax[:, n:n + 1], ps_s[n % 2][:, :], AX_X, ALU.max, negate=True))
                    dve.tensor_tensor(bias[:, n:n + 1], nmax[:, n:n + 1], rq[:, n:n + 1], ALU.mult).then_inc(s_max, 1)

                def row_recip(i, n):
                    dve.wait_ge(s_exp, 8 * i + n + 1 + 2)
                    dve.reciprocal(recip[:, n:n + 1], sums[:, n:n + 1]).then_inc(s_rec, 1)

                def guess(own, out, value):
                    I32 = mybir.dt.int32
                    own.after(dve.tensor_scalar(out.bitcast(I32), value.bitcast(I32), 1, None, ALU.logical_shift_right))
                    return dve.tensor_scalar(out.bitcast(I32), out.bitcast(I32), -1.0, float(0x5F3759DF), ALU.mult, ALU.add)

                def sum_k(own, j):
                    dve.wait_ge(s_ksq, j + 1)
                    own.after(dve.tensor_reduce(kss[:, :], ksq[:, :, :, :], AX_X, ALU.add))
                    own.after(dve.tensor_scalar(kss[:, :], kss[:, :], 1.0 / D, RMS_EPS, ALU.mult, ALU.add))
                    guess(own, kguess[:, :], kss[:, :]).then_inc(s_kss, 1)

                def scale_k(j):
                    dve.wait_ge(s_rk, j + 1)
                    for n in range(TB * HP):
                        t, h = divmod(n, HP)
                        ins = dve.tensor_scalar(kn[:, t, h, :], kn[:, t, h, :], rk[:, n:n + 1], None, ALU.mult)
                    ins.then_inc(s_kn, 1)

                def q_lo(j, h):
                    dve.wait_ge(s_qsq, 2 * j + h + 1)
                    dve.tensor_tensor(qT[:, 1, h, :], ps_w[(2, 0)[h]][:, :], qT[:, 0, h, :].bitcast(F32),
                                      ALU.subtract).then_inc(s_qlo, 1)

                def kt_lo(j, h):
                    dve.wait_ge(s_kthi, 2 * j + h + 1)
                    dve.scalar_tensor_tensor(kT[:, 1, h, :], ps_w[1 + h][:, :], gain[:, 0:1],
                                             kT[:, 0, h, :].bitcast(F32), ALU.mult, ALU.subtract).then_inc(s_ktlo, 1)

                def v_lo(j, half):
                    dve.wait_ge(s_vhi, 2 * j + half + 1)
                    rows = slice(2 * half, 2 * half + 2)
                    dve.tensor_tensor(v[:, 1, rows, :], ps_w[half][:, :].rearrange("p (a n) -> p a n", a=2),
                                      v[:, 0, rows, :].bitcast(F32), ALU.subtract).then_inc(s_vlo, 1)

                def sum_q(own, j):
                    dve.wait_ge(s_ss, j + 1)
                    ins = dve.tensor_scalar(qss[:, :], ps_o[:, 0:TB * HP], 1.0 / D, RMS_EPS, ALU.mult, ALU.add)
                    ins.then_inc(s_ssread, 1)
                    dve.wait_ge(s_ssread, j + 1)
                    guess(own, qguess[:, :], qss[:, :]).then_inc(s_qss, 1)

                def pt_lo(i, h, k):
                    dve.wait_ge(s_pthi, 8 * i + 4 * h + k + 1)
                    dve.tensor_tensor(pT[:, 1, k, :], ps_pt[k % 2][:, :, :].rearrange("p t n -> p (t n)"),
                                      pT[:, 0, k, :].bitcast(F32), ALU.subtract).then_inc(s_ptlo, 1)

                def o_lo(i, h):
                    dve.wait_ge(s_ohi, 2 * i + h + 1)
                    dve.tensor_tensor(oT[:, 1, h, :], ps_o[:, :], oT[:, 0, h, :].bitcast(F32),
                                      ALU.subtract).then_inc(s_olo, 1)

                def add_y(i, b, t):
                    dve.wait_ge(s_y, 4 * i + t + 1)
                    row = xs[:, b * TB + t, :]
                    dve.tensor_tensor(row, ps_w[(2, 0, 1, 2)[t]][:, :], row, ALU.add).then_inc(s_yadd, 1)

                dve.sem_inc(s_ptlo, 2)
                dve.sem_inc(s_olo, 2)
                dve.sem_inc(s_yadd, 4)
                own = Steps(dve, s_dve)
                own.mark(dve.memset(ones[:, :], 1.0))
                own.wait()
                dve.wait_ge(s_const, 48)
                dve.scalar_tensor_tensor(gain[:, :], gains[:, 0:1], scale, gains[:, 1:2], ALU.mult,
                                         ALU.mult).then_inc(s_gain, 1)
                dve.wait_ge(s_gain, 1)
                split_w(own, 0, KV)
                split_w(own, 0, Q)
                sum_k(own, 0)
                scale_k(0)
                q_lo(0, 0)
                q_lo(0, 1)
                kt_lo(0, 0)
                kt_lo(0, 1)
                sum_q(own, 0)
                v_lo(0, 0)
                v_lo(0, 1)
                split_wo(own, 0)
                dve.wait_ge(s_rq, 1)
                row_max(own, 0, 0)
                row_max(own, 0, 1)
                base = own.n
                per_pair = B * (8 + 3 + 1) + 3

                def iteration(own, hp, b, last):
                    i = hp * B + b
                    j = i + 1
                    more = not isinstance(hp, int)
                    row_recip(i, 0)
                    row_recip(i, 1)
                    row_max(own, i, 2)
                    row_max(own, i, 3)
                    row_recip(i, 2)
                    row_max(own, i, 4)
                    row_recip(i, 3)
                    row_max(own, i, 5)
                    row_recip(i, 4)
                    if not last:
                        sum_k(own, j)
                    row_recip(i, 5)
                    pt_lo(i, 0, 0)
                    pt_lo(i, 0, 1)
                    row_max(own, i, 6)
                    pt_lo(i, 0, 2)
                    row_max(own, i, 7)
                    row_recip(i, 6)
                    pt_lo(i, 0, 3)
                    if not last:
                        q_lo(j, 0)
                    row_recip(i, 7)
                    if not last:
                        scale_k(j)
                        q_lo(j, 1)
                    o_lo(i, 0)
                    if not last:
                        kt_lo(j, 0)
                        kt_lo(j, 1)
                    pt_lo(i, 1, 0)
                    pt_lo(i, 1, 1)
                    pt_lo(i, 1, 2)
                    if not last:
                        sum_q(own, j)
                    pt_lo(i, 1, 3)
                    if b == B - 3 and more:
                        split_wo(own, hp + 1)
                    if b == B - 2 and more:
                        dve.wait_ge(s_v, 2 * j + 2)
                        split_w(own, hp + 1, KV)
                        split_w(own, hp + 1, Q)
                    o_lo(i, 1)
                    if not last:
                        v_lo(j, 0)
                        v_lo(j, 1)
                        dve.wait_ge(s_rq, j + 1)
                        row_max(own, j, 0)
                        row_max(own, j, 1)
                    for t in range(TB):
                        add_y(i, b, t)

                with dve.Fori(0, PAIRS - 1) as hp:
                    own = Steps(dve, s_dve, hp * per_pair + base)
                    for b in range(B):
                        iteration(own, hp, b, False)
                    assert own.n == per_pair, own.n
                own = Steps(dve, s_dve, (PAIRS - 1) * per_pair + base)
                for b in range(B):
                    iteration(own, PAIRS - 1, b, b == B - 1)


def stage_shared(nc, xs, xT, gate_w, up_w, down_w):
    INNER = gate_w.shape[1]
    IC = INNER // P
    N_IN = KD * INNER
    N_ALL = 2 * N_IN + IC * DIM
    with Scope(nc, "shared") as m:
        raw = m.sb("raw", [P, N_ALL])
        w = m.sb("w", [P, 2, N_ALL], F32R)
        gated = [m.sb(f"gated{i}", [P, S]) for i in range(2)]
        hid = [m.sb(f"hid{i}", [P, S]) for i in range(2)]
        hT = [m.sb(f"hT{i}", [P, 2, IC, S], F32R) for i in range(2)]
        ps_u = [m.ps(f"up{i}", [P, S]) for i in range(2)]
        ps_g = [m.ps(f"gate{i}", [P, S]) for i in range(2)]
        ps_y = [m.ps(f"y{i}", [P, DIM]) for i in range(TB)]
        s_raw = [m.sem(f"{n}_in") for n in ("gate", "up", "down")]
        s_whi, s_w = m.sem("w_hi"), m.sem("w_split")
        s_ug, s_silu, s_h = m.sem("up_gate"), m.sem("silu_done"), m.sem("hidden")
        s_hhi, s_hlo = m.sem("hidden_hi"), m.sem("hidden_lo")
        s_y, s_yadd = m.sem("y_made"), m.sem("y_added")
        PARTS = (slice(0, N_IN), slice(N_IN, 2 * N_IN), slice(2 * N_IN, N_ALL))

        def part(hl, which, k):
            width = DIM if which == 2 else INNER
            at = PARTS[which].start + k * width
            return w[:, hl, at:at + width]

        with m.block() as block:
            @block.sync
            def _(sp):
                for n, src in enumerate((gate_w, up_w, down_w)):
                    sp.dma_start(raw[:, PARTS[n]].rearrange("p (k n) -> p k n", k=src.shape[0] // P),
                                 src.rearrange("(k p) n -> p k n", p=P)).then_inc(s_raw[n], 16)

            @block.tensor
            def _(pe):
                def up_gate(b):
                    for ic in range(IC):
                        j = b * IC + ic
                        if j >= 2:
                            pe.wait_ge(s_h, j - 1)
                        cols = slice(ic * P, (ic + 1) * P)
                        for which, bank in ((0, ps_g), (1, ps_u)):
                            if b == 0 and ic == 0:
                                pe.wait_ge(s_w, which + 1)
                            for k in range(KD):
                                mm = split_product(pe, bank[j % 2][:, :], (part(0, which, k)[:, cols], part(1, which, k)[:, cols]),
                                                   (xT[b][:, 0, k, :], xT[b][:, 1, k, :]), k == 0, k == KD - 1)
                        mm.then_inc(s_ug, 1)

                def down(b):
                    pe.wait_ge(s_w, 3)
                    pe.wait_ge(s_hlo, IC * (b + 1))
                    for t in range(TB):
                        if b:
                            pe.wait_ge(s_yadd, TB * (b - 1) + t + 1)
                        rows = slice(t * P, (t + 1) * P)
                        for ic in range(IC):
                            mm = split_product(pe, ps_y[t][:, :], (hT[b % 2][:, 0, ic, rows], hT[b % 2][:, 1, ic, rows]),
                                               (part(0, 2, ic), part(1, 2, ic)), ic == 0, ic == IC - 1)
                        mm.then_inc(s_y, 1)

                up_gate(0)
                for b in range(B):
                    if b + 1 < B:
                        up_gate(b + 1)
                    down(b)

            @block.scalar
            def _(act):
                for j in range(B * IC + 1):
                    if j < B * IC:
                        act.wait_ge(s_ug, j + 1)
                        if j >= 2:
                            act.wait_ge(s_h, j - 1)
                        act.activation(gated[j % 2][:, :], ps_g[j % 2][:, :], ACT.Silu).then_inc(s_silu, 1)
                    if j > 0:
                        b, ic = divmod(j - 1, IC)
                        act.wait_ge(s_h, j)
                        if b >= 2:
                            act.wait_ge(s_y, TB * (b - 1))
                        act.copy(hT[b % 2][:, 0, ic, :], hid[(j - 1) % 2][:, :]).then_inc(s_hhi, 1)

            @block.gpsimd
            def _(pool):
                for j in range(B * IC):
                    b, ic = divmod(j, IC)
                    pool.wait_ge(s_hhi, j + 1)
                    pool.tensor_tensor(hT[b % 2][:, 1, ic, :], hid[j % 2][:, :], hT[b % 2][:, 0, ic, :].bitcast(F32),
                                       ALU.subtract).then_inc(s_hlo, 1)

            @block.vector
            def _(dve):
                def hidden(b):
                    for ic in range(IC):
                        j = b * IC + ic
                        dve.wait_ge(s_silu, j + 1)
                        if j >= 2:
                            dve.wait_ge(s_hlo, j - 1)
                        dve.tensor_tensor(hid[j % 2][:, :], ps_u[j % 2][:, :], gated[j % 2][:, :], ALU.mult).then_inc(s_h, 1)

                for n, cols in enumerate(PARTS):
                    dve.wait_ge(s_raw[n], 16)
                    dve.tensor_copy(w[:, 0, cols], raw[:, cols]).then_inc(s_whi, 1)
                    dve.wait_ge(s_whi, n + 1)
                    dve.tensor_tensor(w[:, 1, cols], raw[:, cols], w[:, 0, cols].bitcast(F32), ALU.subtract).then_inc(s_w, 1)
                hidden(0)
                for b in range(B):
                    if b + 1 < B:
                        hidden(b + 1)
                    for t in range(TB):
                        dve.wait_ge(s_y, TB * b + t + 1)
                        row = xs[:, b * TB + t, :]
                        dve.tensor_tensor(row, ps_y[t][:, :], row, ALU.add).then_inc(s_yadd, 1)


def hadamard_sign(i, j):
    return -1 if bin(i & j).count("1") % 2 else 1


def stage_ffn_weights(nc, wT, W_gate, W_up, W_down, Wscale_ug, Wscale_dp, SU_dp, ident, had):
    INTER = W_gate.shape[0]
    CH, NB = 512, INTER // P
    CHUNKS = INTER // CH
    PART = KD * CH
    srcs = [(W_gate, INTER), (W_up, 0)]
    with Scope(nc, "ffw") as m:
        ident_sb = m.sb("ident", [P, P])
        had_f = m.sb("had_f", [P, P])
        had_r = m.sb("had", [P, P], F32R)
        scales = m.sb("scales", [P, 2 * NB])
        dscale = m.sb("dscale", [P, KD])
        su = m.sb("su", [P, NB])
        raw = [m.sb(f"raw{t}", [P, DIM]) for t in range(TB)]
        scaled = [m.sb(f"scaled{t}", [P, DIM]) for t in range(TB)]
        outT = [m.sb(f"outT{i}", [P, 2, KD, CH], F32R) for i in range(2)]
        dn = [m.sb(f"down{i}", [P, KD, INTER]) for i in range(2)]
        dT = [m.sb(f"downT{i}", [P, 2, DIM], F32R) for i in range(2)]
        dout = [m.sb(f"dout{i}", [P, 2, 4, DIM], F32R) for i in range(2)]
        banks = [m.ps(f"bank{t}", [P, KD, P]) for t in range(TB)]
        tb = [m.ps(f"turn{i}", [P, DIM]) for i in range(2)]
        hb = [m.ps(f"rot{i}", [P, DIM]) for i in range(2)]

        s_const = m.sem("const_in")
        s_raw = [m.sem(f"raw_in{t}") for t in range(TB)]
        s_scaled, s_tr, s_hi, s_lo = m.sem("scaled"), m.sem("transposed"), m.sem("hi"), m.sem("lo")
        s_out = [m.sem(f"stored{i}") for i in range(2)]
        s_dn, s_bf = m.sem("down_in"), m.sem("butterflies")
        s_had = m.sem("had_rounded")
        s_dt, s_dthi, s_dtlo = m.sem("downT"), m.sem("downT_hi"), m.sem("downT_lo")
        s_dr, s_drhi, s_drlo = m.sem("rotated"), m.sem("rotated_hi"), m.sem("rotated_lo")
        s_dout = [m.sem(f"down_stored{i}") for i in range(2)]

        with m.block() as block:
            @block.sync
            def _(sp):
                sp.dma_start(dn[0][:, :, :], W_down.rearrange("(k p) n -> p k n", p=P)).then_inc(s_dn, 16)
                sp.dma_start(dscale[:, :], Wscale_dp.rearrange("(k p) -> p k", p=P), allow_slow_non_contiguous=True).then_inc(s_dn, 16)
                sp.dma_start(ident_sb[:, :], ident).then_inc(s_const, 16)
                sp.dma_start(had_f[:, :], had).then_inc(s_const, 16)
                sp.dma_start(scales[:, :], Wscale_ug.rearrange("(n p) -> p n", p=P), allow_slow_non_contiguous=True).then_inc(s_const, 16)
                sp.dma_start(su[:, :], SU_dp.rearrange("(n p) -> p n", p=P), allow_slow_non_contiguous=True).then_inc(s_const, 16)

                def load(i):
                    n, c = divmod(i, CHUNKS)
                    rows = srcs[n][0].rearrange("(c t p) d -> c t p d", c=CHUNKS, t=TB)
                    for t in range(TB):
                        if i:
                            sp.wait_ge(s_scaled, (i - 1) * TB + t + 1)
                        sp.dma_start(raw[t][:, :], rows[c, t]).then_inc(s_raw[t], 16)

                load(0)
                for i in range(2 * CHUNKS):
                    n, c = divmod(i, CHUNKS)
                    if i + 1 < 2 * CHUNKS:
                        load(i + 1)
                    sp.wait_ge(s_lo, (i + 1) * TB)
                    sp.dma_start(wT[c, :, :, n * PART:(n + 1) * PART],
                                 outT[i % 2][:, :, :, :].bitcast(F32).rearrange("p s k n -> p s (k n)")).then_inc(s_out[i % 2], 16)
                for c in range(CHUNKS):
                    sp.wait_ge(s_drlo, 4 * (c + 1))
                    sp.dma_start(wT[c, :, :, 2 * PART:3 * PART],
                                 dout[c % 2][:, :, :, :].bitcast(F32).rearrange("p s k n -> p s (k n)")).then_inc(s_dout[c % 2], 16)
                for i in range(2):
                    sp.wait_ge(s_out[i], 16 * CHUNKS)
                    sp.wait_ge(s_dout[i], 16 * CHUNKS // 2)

            @block.gpsimd
            def _(pool):
                pool.wait_ge(s_dn, 32)
                for k in range(KD):
                    pool.tensor_scalar(dn[0][:, k, :], dn[0][:, k, :], dscale[:, k:k + 1], INTER ** -0.5,
                                       ALU.mult, ALU.mult).then_inc(s_bf, 1)
                done = KD
                for stage in range(NB.bit_length() - 1):
                    src, dst = dn[stage % 2], dn[1 - stage % 2]
                    width = P << stage
                    s_v, d_v = (x[:, :, :].rearrange("p k (g two w) -> p (k g) two w", two=2, w=width) for x in (src, dst))
                    pool.wait_ge(s_bf, done)
                    for two, op in ((0, ALU.add), (1, ALU.subtract)):
                        pool.tensor_tensor(d_v[:, :, two, :], s_v[:, :, 0, :], s_v[:, :, 1, :], op).then_inc(s_bf, 1)
                    done += 2

            @block.vector
            def _(dve):
                dve.wait_ge(s_const, 64)
                dve.tensor_copy(had_r[:, :], had_f[:, :]).then_inc(s_had, 1)

                def scale(i):
                    n, c = divmod(i, CHUNKS)
                    at = srcs[n][1] // P + c * TB
                    for t in range(TB):
                        dve.wait_ge(s_raw[t], (i + 1) * 16)
                        if i:
                            dve.wait_ge(s_tr, (i - 1) * TB + t + 1)
                        dve.tensor_scalar(scaled[t][:, :], raw[t][:, :], scales[:, at + t:at + t + 1], None,
                                          ALU.mult).then_inc(s_scaled, 1)

                scale(0)
                for i in range(2 * CHUNKS):
                    if i + 1 < 2 * CHUNKS:
                        scale(i + 1)
                    for t in range(TB):
                        cols = slice(t * P, (t + 1) * P)
                        dve.wait_ge(s_hi, i * TB + t + 1)
                        dve.tensor_tensor(outT[i % 2][:, 1, :, cols], banks[t][:, :, :],
                                          outT[i % 2][:, 0, :, cols].bitcast(F32), ALU.subtract).then_inc(s_lo, 1)

                def turned_lo(a):
                    dve.wait_ge(s_dthi, a + 1)
                    dve.tensor_tensor(dT[a % 2][:, 1, :], tb[a % 2][:, :], dT[a % 2][:, 0, :].bitcast(F32),
                                      ALU.subtract).then_inc(s_dtlo, 1)

                def rotated_lo(a):
                    dve.wait_ge(s_drhi, a + 1)
                    o = dout[a // 4 % 2]
                    dve.scalar_tensor_tensor(o[:, 1, a % 4, :], hb[a % 2][:, :], su[:, a:a + 1],
                                             o[:, 0, a % 4, :].bitcast(F32), ALU.mult, ALU.subtract).then_inc(s_drlo, 1)

                turned_lo(0)
                for a in range(NB):
                    if a + 1 < NB:
                        turned_lo(a + 1)
                    rotated_lo(a)

            @block.tensor
            def _(pe):
                pe.wait_ge(s_const, 64)
                for i in range(2 * CHUNKS):
                    for t in range(TB):
                        pe.wait_ge(s_scaled, i * TB + t + 1)
                        if i:
                            pe.wait_ge(s_lo, (i - 1) * TB + t + 1)
                        for k in range(KD):
                            tr = pe.transpose(banks[t][:, k, :], scaled[t][:, k * P:(k + 1) * P], ident_sb[:, :])
                        tr.then_inc(s_tr, 1)
                dsrc = dn[(NB.bit_length() - 1) % 2]
                pe.wait_ge(s_bf, KD + 2 * (NB.bit_length() - 1))
                pe.wait_ge(s_had, 1)

                def turn(a):
                    if a >= 2:
                        pe.wait_ge(s_dtlo, a - 1)
                    for k in range(KD):
                        tr = pe.transpose(tb[a % 2][:, k * P:(k + 1) * P], dsrc[:, k, a * P:(a + 1) * P], ident_sb[:, :])
                    tr.then_inc(s_dt, 1)

                turn(0)
                for a in range(NB):
                    if a + 1 < NB:
                        turn(a + 1)
                    pe.wait_ge(s_dtlo, a + 1)
                    if a >= 2:
                        pe.wait_ge(s_drlo, a - 1)
                    pe.matmul(hb[a % 2][:, :], had_r[:, :], dT[a % 2][:, 0, :], start=True, stop=False)
                    pe.matmul(hb[a % 2][:, :], had_r[:, :], dT[a % 2][:, 1, :], start=False, stop=True).then_inc(s_dr, 1)

            @block.scalar
            def _(act):
                for i in range(2 * CHUNKS):
                    if i >= 2:
                        act.wait_ge(s_out[i % 2], 16 * (i // 2))
                    for t in range(TB):
                        act.wait_ge(s_tr, i * TB + t + 1)
                        act.copy(outT[i % 2][:, 0, :, t * P:(t + 1) * P], banks[t][:, :, :]).then_inc(s_hi, 1)

                def turned_hi(a):
                    act.wait_ge(s_dt, a + 1)
                    if a >= 2:
                        act.wait_ge(s_dr, a - 1)
                    act.copy(dT[a % 2][:, 0, :], tb[a % 2][:, :]).then_inc(s_dthi, 1)

                def rotated_hi(a):
                    act.wait_ge(s_dr, a + 1)
                    if a >= 8 and a % 4 == 0:
                        act.wait_ge(s_dout[a // 4 % 2], 16 * (a // 8))
                    act.activation(dout[a // 4 % 2][:, 0, a % 4, :], hb[a % 2][:, :], ACT.Copy,
                                   scale=su[:, a:a + 1]).then_inc(s_drhi, 1)

                turned_hi(0)
                for a in range(NB):
                    if a + 1 < NB:
                        turned_hi(a + 1)
                    rotated_hi(a)


def stage_rotate(nc, xT, uT, SU, had):
    with Scope(nc, "rot") as m:
        had_f = m.sb("had_f", [P, P])
        su = m.sb("su", [P, KD])
        hs_f = m.sb("hs_f", [P, 2, KD, P])
        hs = m.sb("hs", [P, 2, 2, KD, P], F32R)
        banks = [m.ps(f"bank{k}", [P, S]) for k in range(KD)]
        s_const = m.sem("const_in")
        s_dve = m.sem("dve_steps")
        s_r, s_hi, s_lo = m.sem("rotated"), m.sem("hi"), m.sem("lo")
        SC = DIM ** -0.5
        with m.block() as block:
            @block.sync
            def _(sp):
                sp.dma_start(had_f[:, :], had).then_inc(s_const, 16)
                sp.dma_start(su[:, :], SU.rearrange("(k p) -> p k", p=P), allow_slow_non_contiguous=True).then_inc(s_const, 16)

            @block.vector
            def _(dve):
                own = Steps(dve, s_dve)
                dve.wait_ge(s_const, 32)
                for k in range(KD):
                    own.mark(dve.tensor_scalar(hs_f[:, 0, k, :], had_f[:, :], su[:, k:k + 1], None, ALU.mult))
                    own.mark(dve.tensor_scalar(hs_f[:, 1, k, :], had_f[:, :], su[:, k:k + 1], -1.0, ALU.mult, ALU.mult))
                own.wait()
                own.after(dve.tensor_copy(hs[:, 0, :, :, :], hs_f[:, :, :, :]))
                own.after(dve.tensor_tensor(hs[:, 1, :, :, :], hs_f[:, :, :, :], hs[:, 0, :, :, :].bitcast(F32), ALU.subtract))
                for b in range(B):
                    for k in range(KD):
                        dve.wait_ge(s_hi, KD * b + k + 1)
                        dve.scalar_tensor_tensor(uT[b][:, 1, k, :], banks[k][:, :], SC,
                                                 uT[b][:, 0, k, :].bitcast(F32), ALU.mult, ALU.subtract).then_inc(s_lo, 1)

            @block.tensor
            def _(pe):
                pe.wait_ge(s_dve, 2 * KD + 2)
                for b in range(B):
                    for ko in range(KD):
                        if b > 0:
                            pe.wait_ge(s_lo, KD * (b - 1) + ko + 1)
                        for k in range(KD):
                            g = 0 if hadamard_sign(k, ko) > 0 else 1
                            mm = split_product(pe, banks[ko][:, :], (hs[:, 0, g, k, :], hs[:, 1, g, k, :]),
                                               (xT[b][:, 0, k, :], xT[b][:, 1, k, :]), k == 0, k == KD - 1)
                        mm.then_inc(s_r, 1)

            @block.scalar
            def _(act):
                for b in range(B):
                    for k in range(KD):
                        act.wait_ge(s_r, KD * b + k + 1)
                        act.activation(uT[b][:, 0, k, :], banks[k][:, :], ACT.Copy, scale=SC).then_inc(s_hi, 1)


STATES = 16
RANK = 16
ET = DIM // P


def stage_ssm_inputs(nc, ctxT, in_proj, conv_w, conv_b, x_proj, dt_proj, dt_bias, u_d, delta_d, du_d, bc_d, ident):
    NX = RANK + 2 * STATES
    TAPS = conv_w.shape[1]
    PAD = TAPS - 1
    with Scope(nc, "ssi") as m:
        ident_sb = m.sb("ident", [P, P])
        in_raw = m.sb("in_raw", [P, ET, CD])
        x_raw = m.sb("x_raw", [NX, DIM])
        dt_raw = m.sb("dt_raw", [P, ET, RANK])
        inT = m.sb("inT", [P, 2, KC, DIM], F32R)
        xT = m.sb("xT", [P, ET, NX])
        dtT = m.sb("dtT", [RANK, DIM])
        taps = m.sb("taps", [P, ET, TAPS])
        cb = m.sb("conv_b", [P, ET])
        db = m.sb("dt_b", [P, ET])
        cx = m.sb("cx", [P, 2, KC, S], F32R)
        xp = [m.sb(f"xp{i}", [P, PAD + S]) for i in range(2)]
        conv = [m.sb(f"conv{i}", [P, S]) for i in range(2)]
        us = [m.sb(f"u{i}", [P, ET, S]) for i in range(2)]
        dbl = m.sb("dbl", [NX, S])
        mag = m.sb("mag", [P, ET, S])
        ex = m.sb("ex", [P, ET, S])
        soft = m.sb("soft", [P, ET, S])
        relu = m.sb("relu", [P, ET, S])
        delta = m.sb("delta", [P, ET, S])
        du = m.sb("du", [P, ET, S])
        ps_t = m.ps("turn", [P, 512])
        ps_x = [m.ps(f"x{i}", [P, S]) for i in range(2)]
        ps_d = m.ps("dbl_ps", [P, S])
        ps_z = [m.ps(f"z{i}", [P, S]) for i in range(ET)]

        s_in = m.sem("weights_in")
        s_t = m.sem("turned")
        s_te = m.sem("turned_out")
        s_tl = m.sem("turned_lo")
        s_cx = m.sem("cx_in")
        s_x, s_xp = m.sem("x"), m.sem("x_padded")
        s_conv, s_u = m.sem("conv"), m.sem("u")
        s_dve = m.sem("dve_steps")
        s_d, s_dbl = m.sem("dbl_made"), m.sem("dbl_copied")
        s_z, s_mag, s_ex, s_soft = m.sem("z"), m.sem("mag_done"), m.sem("exp_done"), m.sem("ln_done")
        s_relu, s_delta, s_du = m.sem("relu_done"), m.sem("delta_done"), m.sem("du_done")
        s_st = [m.sem(f"stored_{n}") for n in ("bc", "delta", "du")]
        s_ust = [m.sem(f"stored_u{i}") for i in range(2)]
        with m.block() as block:
            @block.sync
            def _(sp):
                sp.dma_start(ident_sb[:, :], ident).then_inc(s_in, 16)
                sp.dma_start(in_raw[:, :, :], in_proj.rearrange("(t p) d -> p t d", p=P)).then_inc(s_in, 16)
                sp.dma_start(x_raw[:, :], x_proj).then_inc(s_in, 16)
                sp.dma_start(dt_raw[:, :, :], dt_proj.rearrange("(t p) r -> p t r", p=P)).then_inc(s_in, 16)
                sp.dma_start(taps[:, :, :], conv_w.rearrange("(t p) r -> p t r", p=P)).then_inc(s_in, 16)
                sp.dma_start(cb[:, :], conv_b.rearrange("(t p) -> p t", p=P), allow_slow_non_contiguous=True).then_inc(s_in, 16)
                sp.dma_start(db[:, :], dt_bias.rearrange("(t p) -> p t", p=P), allow_slow_non_contiguous=True).then_inc(s_in, 16)
                sp.dma_start(cx[:, :, :, :].bitcast(F32), ctxT[0]).then_inc(s_cx, 16)

                def finish(b):
                    for made, dst, src, sem in ((s_dbl, bc_d[b], dbl[RANK:NX, :], s_st[0]),
                                                (s_delta, delta_d[b], delta[:, :, :], s_st[1]),
                                                (s_du, du_d[b], du[:, :, :], s_st[2])):
                        sp.wait_ge(made, b + 1)
                        sp.dma_start(dst, src).then_inc(sem, 16)

                for b in range(B):
                    if b + 1 < B:
                        sp.wait_ge(s_x, ET * (b + 1))
                        sp.dma_start(cx[:, :, :, :].bitcast(F32), ctxT[b + 1]).then_inc(s_cx, 16)
                    sp.wait_ge(s_u, ET * (b + 1))
                    sp.dma_start(u_d[b], us[b % 2][:, :, :]).then_inc(s_ust[b % 2], 16)
                    if b:
                        finish(b - 1)
                finish(B - 1)
                for q in s_st:
                    sp.wait_ge(q, 16 * B)
                for i in range(2):
                    sp.wait_ge(s_ust[i], 16 * B // 2)

            @block.tensor
            def _(pe):
                pe.wait_ge(s_in, 16 * 7)
                for k in range(KC):
                    if k:
                        pe.wait_ge(s_tl, k)
                    for t in range(ET):
                        tr = pe.transpose(ps_t[:, t * P:(t + 1) * P], in_raw[:, t, k * P:(k + 1) * P], ident_sb[:, :])
                    tr.then_inc(s_t, 1)
                pe.wait_ge(s_tl, KC)
                for t in range(ET):
                    tr = pe.transpose(ps_t[:, t * NX:(t + 1) * NX], x_raw[:, t * P:(t + 1) * P], ident_sb[0:NX, 0:NX])
                tr.then_inc(s_t, 1)
                pe.wait_ge(s_te, KC + 1)
                for t in range(ET):
                    tr = pe.transpose(ps_t[0:RANK, t * P:(t + 1) * P], dt_raw[:, t, :], ident_sb[:, :])
                tr.then_inc(s_t, 1)
                pe.wait_ge(s_te, KC + 2)

                def channels(b):
                    pe.wait_ge(s_cx, 16 * (b + 1))
                    for t in range(ET):
                        n = b * ET + t
                        if n >= 2:
                            pe.wait_ge(s_xp, n - 1)
                        cols = slice(t * P, (t + 1) * P)
                        for k in range(KC):
                            mm = split_product(pe, ps_x[n % 2][:, :], (inT[:, 0, k, cols], inT[:, 1, k, cols]),
                                               (cx[:, 0, k, :], cx[:, 1, k, :]), k == 0, k == KC - 1)
                        mm.then_inc(s_x, 1)

                channels(0)
                for b in range(B):
                    if b + 1 < B:
                        channels(b + 1)
                    if b:
                        pe.wait_ge(s_dbl, b)
                    for t in range(ET):
                        pe.wait_ge(s_u, b * ET + t + 1)
                        mm = pe.matmul(ps_d[0:NX, :], xT[:, t, :], us[b % 2][:, t, :], start=(t == 0), stop=(t == ET - 1))
                    mm.then_inc(s_d, 1)
                    pe.wait_ge(s_dbl, b + 1)
                    for t in range(ET):
                        if b:
                            pe.wait_ge(s_relu, b)
                            pe.wait_ge(s_mag, ET * b)
                        pe.matmul(ps_z[t][:, :], dtT[:, t * P:(t + 1) * P], dbl[0:RANK, :], start=True,
                                  stop=True).then_inc(s_z, 1)

            @block.scalar
            def _(act):
                for k in range(KC):
                    act.wait_ge(s_t, k + 1)
                    act.copy(inT[:, 0, k, :], ps_t[:, :]).then_inc(s_te, 1)
                act.wait_ge(s_t, KC + 1)
                act.copy(xT[:, :, :], ps_t[:, 0:ET * NX].rearrange("p (t n) -> p t n", t=ET)).then_inc(s_te, 1)
                act.wait_ge(s_t, KC + 2)
                act.copy(dtT[:, :], ps_t[0:RANK, :]).then_inc(s_te, 1)
                act.wait_ge(s_dve, 2)

                def channels(b):
                    for t in range(ET + 1):
                        n = b * ET + t
                        if t < ET:
                            act.wait_ge(s_x, n + 1)
                            if n >= 2:
                                act.wait_ge(s_conv, n - 1)
                            act.copy(xp[n % 2][:, PAD:], ps_x[n % 2][:, :]).then_inc(s_xp, 1)
                        if t > 0:
                            act.wait_ge(s_conv, n)
                            if b >= 2:
                                act.wait_ge(s_ust[b % 2], 16 * (b // 2))
                                act.wait_ge(s_du, b - 1)
                            act.activation(us[b % 2][:, t - 1, :], conv[(n - 1) % 2][:, :], ACT.Silu,
                                           bias=cb[:, t - 1:t]).then_inc(s_u, 1)

                channels(0)
                for b in range(B):
                    if b + 1 < B:
                        channels(b + 1)
                    act.wait_ge(s_d, b + 1)
                    if b:
                        act.wait_ge(s_st[0], 16 * b)
                        act.wait_ge(s_z, ET * b)
                    act.copy(dbl[:, :], ps_d[0:NX, :]).then_inc(s_dbl, 1)
                    for t in range(ET):
                        act.wait_ge(s_z, ET * b + t + 1)
                        act.activation(mag[:, t, :], ps_z[t][:, :], ACT.Abs, bias=db[:, t:t + 1]).then_inc(s_mag, 1)
                    act.wait_ge(s_mag, ET * (b + 1))
                    act.activation(ex[:, :, :], mag[:, :, :], ACT.Exp, scale=-1.0).then_inc(s_ex, 1)
                    act.wait_ge(s_ex, b + 1)
                    if b:
                        act.wait_ge(s_delta, b)
                    act.activation(soft[:, :, :], ex[:, :, :], ACT.Ln, bias=1.0).then_inc(s_soft, 1)

            @block.vector
            def _(dve):
                own = Steps(dve, s_dve)
                for i in range(2):
                    own.mark(dve.memset(xp[i][:, 0:PAD], 0.0))
                for k in range(KC):
                    dve.wait_ge(s_te, k + 1)
                    dve.tensor_tensor(inT[:, 1, k, :], ps_t[:, :], inT[:, 0, k, :].bitcast(F32), ALU.subtract).then_inc(s_tl, 1)

                def channels(b):
                    for t in range(ET):
                        n = b * ET + t
                        dve.wait_ge(s_xp, n + 1)
                        if n >= 2:
                            dve.wait_ge(s_u, n - 1)
                        c, x = conv[n % 2], xp[n % 2]
                        own.after(dve.tensor_scalar(c[:, :], x[:, 0:S], taps[:, t, 0:1], None, ALU.mult))
                        for j in range(1, TAPS):
                            ins = dve.scalar_tensor_tensor(c[:, :], x[:, j:j + S], taps[:, t, j:j + 1], c[:, :],
                                                           ALU.mult, ALU.add)
                            if j < TAPS - 1:
                                own.after(ins)
                        ins.then_inc(s_conv, 1)

                channels(0)
                for b in range(B):
                    if b + 1 < B:
                        channels(b + 1)
                    dve.wait_ge(s_mag, ET * (b + 1))
                    if b:
                        dve.wait_ge(s_delta, b)
                    for t in range(ET):
                        ins = dve.tensor_scalar(relu[:, t, :], ps_z[t][:, :], db[:, t:t + 1], 0.0, ALU.add, ALU.max)
                    ins.then_inc(s_relu, 1)
                    dve.wait_ge(s_relu, b + 1)
                    dve.wait_ge(s_soft, b + 1)
                    if b:
                        dve.wait_ge(s_st[1], 16 * b)
                        dve.wait_ge(s_st[2], 16 * b)
                    dve.tensor_tensor(delta[:, :, :], relu[:, :, :], soft[:, :, :], ALU.add).then_inc(s_delta, 1)
                    dve.wait_ge(s_delta, b + 1)
                    dve.tensor_tensor(du[:, :, :], delta[:, :, :], us[b % 2][:, :, :], ALU.mult).then_inc(s_du, 1)


def stage_ssm_gate(nc, xs, u_d, y_d, skip, ident):
    with Scope(nc, "gate") as m:
        ident_sb = m.sb("ident", [P, P])
        d = m.sb("skip", [P, ET])
        rows = [xs[:, b * TB:(b + 1) * TB, :] for b in range(B)]
        u = [m.sb(f"u{i}", [P, ET, S]) for i in range(2)]
        y = [m.sb(f"y{i}", [P, ET, S]) for i in range(2)]
        silu = m.sb("silu", [P, TB, DIM])
        gated = m.sb("gated", [P, ET, S])
        stats = m.sb("stats", [P, TB, 6])
        meanvar = m.sb("meanvar", [P, TB, 2])
        var_eps = m.sb("var_eps", [P, TB])
        rstd = m.sb("rstd", [P, TB])
        shift = m.sb("shift", [P, TB])
        guess = m.sb("guess", [P, TB])
        work = m.sb("work", [P, TB])
        banks = [m.ps(f"bank{t}", [P, ET, P]) for t in range(TB)]
        s_in = m.sem("in")
        s_ld = [m.sem(f"batch_in{i}") for i in range(2)]
        s_dve, s_shift, s_silu = m.sem("dve_steps"), m.sem("shift_done"), m.sem("silu_done")
        s_g, s_t, s_res = m.sem("gated_done"), m.sem("turned"), m.sem("res_done")
        with m.block() as block:
            @block.sync
            def _(sp):
                sp.dma_start(ident_sb[:, :], ident).then_inc(s_in, 16)
                sp.dma_start(d[:, :], skip.rearrange("(t p) -> p t", p=P), allow_slow_non_contiguous=True).then_inc(s_in, 16)
                for b in range(B):
                    if b >= 2:
                        sp.wait_ge(s_res, TB * (b - 1))
                    sp.dma_start(u[b % 2][:, :, :], u_d[b]).then_inc(s_ld[b % 2], 16)
                    sp.dma_start(y[b % 2][:, :, :], y_d[b]).then_inc(s_ld[b % 2], 16)

            @block.vector
            def _(dve):
                own = Steps(dve, s_dve)
                dve.wait_ge(s_in, 32)
                for b in range(B):
                    for t in range(TB):
                        own.mark(dve.bn_stats(stats[:, t, :], rows[b][:, t, :]))
                    own.wait()
                    for t in range(TB):
                        own.mark(dve.bn_aggr(meanvar[:, t, :], stats[:, t, :]))
                    own.wait()
                    own.after(dve.tensor_scalar(var_eps[:, :], meanvar[:, :, 1], LN_EPS, None, ALU.add))
                    newton_rsqrt(dve, own, rstd[:, :], var_eps[:, :], guess[:, :], work[:, :])
                    dve.scalar_tensor_tensor(shift[:, :], meanvar[:, :, 0], -1.0, rstd[:, :], ALU.mult,
                                             ALU.mult).then_inc(s_shift, 1)
                    dve.wait_ge(s_ld[b % 2], 32 * (b // 2 + 1))
                    for t in range(ET):
                        own.mark(dve.scalar_tensor_tensor(y[b % 2][:, t, :], u[b % 2][:, t, :], d[:, t:t + 1],
                                                          y[b % 2][:, t, :], ALU.mult, ALU.add))
                    own.wait()
                    if b:
                        dve.wait_ge(s_t, TB * b)
                    for t in range(ET):
                        dve.wait_ge(s_silu, TB * b + t + 1)
                        dve.tensor_tensor(gated[:, t, :], y[b % 2][:, t, :], silu[:, t, :], ALU.mult).then_inc(s_g, 1)
                    for t in range(TB):
                        dve.wait_ge(s_t, TB * b + t + 1)
                        dve.tensor_tensor(rows[b][:, t, :], banks[t][:, :, :].rearrange("p e n -> p (e n)"),
                                          rows[b][:, t, :], ALU.add).then_inc(s_res, 1)

            @block.scalar
            def _(act):
                for b in range(B):
                    act.wait_ge(s_shift, b + 1)
                    if b:
                        act.wait_ge(s_g, ET * b)
                    for t in range(TB):
                        act.activation(silu[:, t, :], rows[b][:, t, :], ACT.Silu, bias=shift[:, t:t + 1],
                                       scale=rstd[:, t:t + 1]).then_inc(s_silu, 1)

            @block.tensor
            def _(pe):
                pe.wait_ge(s_in, 32)
                for b in range(B):
                    pe.wait_ge(s_g, ET * (b + 1))
                    for t in range(TB):
                        if b:
                            pe.wait_ge(s_res, TB * (b - 1) + t + 1)
                        for e in range(ET):
                            tr = pe.transpose(banks[t][:, e, :], gated[:, e, t * P:(t + 1) * P], ident_sb[:, :])
                        tr.then_inc(s_t, 1)


EXPERTS = 16


def stage_ffn_scan(nc, xs, uT, wT, A_log, delta_d, du_d, bc_d, y_d):
    INNER, IC = 256, 2
    UNITS = wT.shape[0] * 2
    RING = ET
    OWN = ET - 1
    PER_STEP = 2 * ET
    PER_BATCH = STATES * ET
    STEPS = 2 * B
    assert UNITS == 2 * B and STEPS * 2 == STATES
    A_v = A_log.rearrange("(t p) n -> p t n", p=P)
    wsrc = wT.rearrange("c p s (w k n) -> c p s w k n", w=3, k=KD)
    with Scope(nc, "ffn") as m:
        w = [m.sb(f"w{i}", [P, 2, 2, KD, INNER], F32R) for i in range(2)]
        wd = m.sb("w_down", [P, 2, IC, DIM], F32R)
        hid = [m.sb(f"hid{i}", [P, S]) for i in range(IC)]
        hT = [m.sb(f"hT{i}", [P, 2, IC, S], F32R) for i in range(2)]
        a_log = m.sb("a_log", [P, ET, STATES])
        a = m.sb("a", [P, ET, STATES])
        delta = m.sb("delta", [P, ET, S])
        du = m.sb("du", [P, ET, S])
        rows = [m.sb(f"rows{i}", [P, 2, S]) for i in range(2)]
        decay = [m.sb(f"decay{i}", [P, S]) for i in range(RING)]
        drive = [m.sb(f"drive{i}", [P, S]) for i in range(RING)]
        y = [m.sb(f"y{t}", [P, S]) for t in range(ET)]
        ps_u = [m.ps(f"up{i}", [P, S]) for i in range(IC)]
        ps_g = [m.ps(f"gate{i}", [P, S]) for i in range(IC)]
        ps_y = [m.ps(f"y{i}_ps", [P, DIM]) for i in range(TB)]

        s_w, s_wd = [m.sem(f"w_in{i}") for i in range(2)], m.sem("w_down_in")
        s_ug = m.sem("up_gate")
        s_silu = m.sem("silu_done")
        s_h = m.sem("hidden")
        s_hhi = m.sem("hidden_hi")
        s_hlo = m.sem("hidden_lo")
        s_y = m.sem("y_made")
        s_yadd = m.sem("y_added")
        s_a, s_aexp, s_neg = m.sem("a_in"), m.sem("a_exp_done"), m.sem("a_done")
        s_delta, s_du = m.sem("delta_in"), m.sem("du_in")
        s_rows = [m.sem(f"rows_in{i}") for i in range(2)]
        s_decay, s_drive = m.sem("decay_done"), m.sem("drive_done")
        s_scan = m.sem("scanned")
        s_term = m.sem("term_done")
        s_add = m.sem("term_added")
        s_padd = m.sem("term_added_pool")
        s_st = [m.sem(f"y_stored{t}") for t in range(ET)]
        s_pace = m.sem("pace")

        def every(eng, step):
            with eng.Fori(0, UNITS // 2 - 1) as p:
                for s in range(STEPS):
                    step(p, s, False)
            for s in range(STEPS):
                step(UNITS // 2 - 1, s, s == STEPS - 1)

        def scans(s, part):
            ms = (range(0, 3), range(3, 6), range(6, PER_STEP))[part]
            return [(s * PER_STEP + k, 2 * s + k // ET, k % ET) for k in ms]

        with m.block() as block:
            @block.sync
            def _(sp):
                def load_w(chunk, half, sem):
                    cols = slice(half * INNER, (half + 1) * INNER)
                    for which in range(2):
                        for hl in range(2):
                            sp.dma_start(w[half][:, hl, which].bitcast(F32), wsrc[chunk, :, hl, which, :, cols]).then_inc(sem, 16)

                def load_down(chunk, half):
                    sp.dma_start(wd[:, :, :, :].bitcast(F32), wsrc[chunk, :, :, 2, half * IC:(half + 1) * IC, :]).then_inc(s_wd, 16)

                def load_rows(b, n):
                    for j in range(2):
                        src = bc_d[b, j * STATES + n:j * STATES + n + 1, :]
                        sp.dma_start(rows[n % 2][:, j, :], src.to_broadcast([P, S])).then_inc(s_rows[n % 2], 16)

                for t in range(ET):
                    sp.sem_inc(s_st[t], 16)
                sp.dma_start(a_log[:, :, :], A_v).then_inc(s_a, 16)
                sp.dma_start(delta[:, :, :], delta_d[0]).then_inc(s_delta, 16)
                load_rows(0, 0)
                load_w(0, 0, s_w[0])
                sp.dma_start(du[:, :, :], du_d[0]).then_inc(s_du, 16)
                load_rows(0, 1)
                load_down(0, 0)

                def step(p, s, last):
                    half, b = divmod(s, B)
                    u = p * 2 + half
                    tail = isinstance(p, int)
                    if b == 0 and not (tail and half == 1):
                        wait_apart(sp, s_ug, 1 + IC * B * u, s_pace)
                        load_w(p + half, 1 - half, s_w[1 - half])
                    done = p * PER_BATCH + (s + 1) * PER_STEP
                    if s < STEPS - 1:
                        for k in range(2):
                            wait_apart(sp, s_term, done - PER_STEP + (k + 1) * ET, s_pace)
                            load_rows(p, 2 * s + 2 + k)
                    else:
                        if not tail:
                            wait_apart(sp, s_term, done - ET, s_pace)
                            load_rows(p + 1, 0)
                            wait_apart(sp, s_decay, done, s_pace)
                            sp.dma_start(delta[:, :, :], delta_d[p + 1]).then_inc(s_delta, 16)
                            wait_apart(sp, s_drive, done, s_pace)
                            sp.dma_start(du[:, :, :], du_d[p + 1]).then_inc(s_du, 16)
                        for t in range(ET):
                            if t < OWN:
                                wait_apart(sp, s_add, OWN * (p * STATES + STATES) + t + 1, s_pace)
                            else:
                                wait_apart(sp, s_padd, 1 + (p + 1) * (STATES - 1), s_pace)
                            sp.dma_start(y_d[p, :, t, :], y[t][:, :]).then_inc(s_st[t], 16)
                        if not tail:
                            load_rows(p + 1, 1)
                    if b == B - 1 and not last:
                        wait_apart(sp, s_y, TB * B * (u + 1), s_pace)
                        load_down(p + half, 1 - half)

                every(sp, step)
                for t in range(ET):
                    sp.wait_ge(s_st[t], 16 * (B + 1))

            @block.tensor
            def _(pe):
                def up_gate(p, half, b):
                    j = (p * 2 + half) * B + b
                    if b == 0:
                        pe.wait_ge(s_w[half], 64 * (p + 1))
                    for ic in range(IC):
                        pe.wait_ge(s_h, IC * j + ic + 1)
                        cols = slice(ic * P, (ic + 1) * P)
                        for which, bank in ((0, ps_g), (1, ps_u)):
                            for k in range(KD):
                                mm = split_product(pe, bank[ic][:, :], (w[half][:, 0, which, k, cols], w[half][:, 1, which, k, cols]),
                                                   (uT[b][:, 0, k, :], uT[b][:, 1, k, :]), k == 0, k == KD - 1)
                        mm.then_inc(s_ug, 1)

                def down(p, half, b):
                    u = p * 2 + half
                    i = u * B + b
                    if b == 0:
                        pe.wait_ge(s_wd, 16 * (u + 1))
                    pe.wait_ge(s_hlo, IC + IC * (i + 1))
                    for t in range(TB):
                        pe.wait_ge(s_yadd, TB * i + t + 1)
                        rows = slice(t * P, (t + 1) * P)
                        for ic in range(IC):
                            mm = split_product(pe, ps_y[t][:, :], (hT[b % 2][:, 0, ic, rows], hT[b % 2][:, 1, ic, rows]),
                                               (wd[:, 0, ic, :], wd[:, 1, ic, :]), ic == 0, ic == IC - 1)
                        mm.then_inc(s_y, 1)

                pe.sem_inc(s_ug, 1)
                up_gate(0, 0, 0)

                def step(p, s, last):
                    if not last:
                        up_gate(p + (s + 1) // STEPS, (s + 1) // B % 2, (s + 1) % B)
                    down(p, s // B, s % B)

                every(pe, step)

            @block.scalar
            def _(act):
                def decays(p, s, part):
                    for k, n, t in scans(s, part):
                        wait_apart(act, s_scan, p * PER_BATCH + k + 1, s_pace)
                        act.activation(decay[k % RING][:, :], delta[:, t, :], ACT.Exp,
                                       scale=a[:, t, n:n + 1]).then_inc(s_decay, 1)

                def silu(j, ic):
                    act.wait_ge(s_ug, 1 + IC * j + ic + 1)
                    act.wait_ge(s_hlo, IC * j + ic + 1)
                    act.activation(hid[ic][:, :], ps_g[ic][:, :], ACT.Silu).then_inc(s_silu, 1)

                def hi(j, par, ic):
                    act.wait_ge(s_h, IC + IC * j + ic + 1)
                    act.copy(hT[par][:, 0, ic, :], hid[ic][:, :]).then_inc(s_hhi, 1)

                act.wait_ge(s_a, 16)
                act.activation(a[:, :, :], a_log[:, :, :], ACT.Exp).then_inc(s_aexp, 1)
                act.wait_ge(s_aexp, 1)
                act.mul(a[:, :, :], a[:, :, :], -1.0).then_inc(s_neg, 1)
                act.wait_ge(s_neg, 1)
                for ic in range(IC):
                    silu(0, ic)
                for ic in range(IC):
                    hi(0, 0, ic)

                def step(p, s, last):
                    j = p * STEPS + s + 1
                    if s == 0:
                        act.wait_ge(s_delta, 16 * (p + 1))
                    decays(p, s, 0)
                    if not last:
                        silu(j, 0)
                    decays(p, s, 1)
                    if not last:
                        hi(j, (s + 1) % 2, 0)
                        silu(j, 1)
                    decays(p, s, 2)
                    if not last:
                        hi(j, (s + 1) % 2, 1)

                every(act, step)

            @block.gpsimd
            def _(pool):
                def add(p, n):
                    wait_apart(pool, s_term, p * PER_BATCH + (n + 1) * ET, s_pace)
                    if n:
                        wait_apart(pool, s_padd, p * (STATES - 1) + n, s_pace)
                        pool.tensor_tensor(y[ET - 1][:, :], y[ET - 1][:, :], drive[ET - 1][:, :], ALU.add).then_inc(s_padd, 1)

                def drives(p, s, part):
                    for k, n, t in scans(s, part):
                        if k % ET == 0:
                            pool.wait_ge(s_rows[n % 2], 32 * (p * STEPS + n // 2 + 1))
                        if t < OWN:
                            wait_apart(pool, s_add, OWN * (p * STATES + n) + t + 1, s_pace)
                        else:
                            if n:
                                add(p, n - 1)
                            wait_apart(pool, s_padd, 1 + p * (STATES - 1) + max(n - 1, 0), s_pace)
                        pool.tensor_tensor(drive[k % RING][:, :], du[:, t, :], rows[n % 2][:, 0, :],
                                           ALU.mult).then_inc(s_drive, 1)

                def lo(j, par, ic):
                    pool.wait_ge(s_hhi, IC * j + ic + 1)
                    pool.tensor_tensor(hT[par][:, 1, ic, :], hid[ic][:, :], hT[par][:, 0, ic, :].bitcast(F32),
                                       ALU.subtract).then_inc(s_hlo, 1)

                pool.sem_inc(s_hlo, IC)
                pool.sem_inc(s_padd, 1)
                for ic in range(IC):
                    lo(0, 0, ic)

                def step(p, s, last):
                    j = p * STEPS + s + 1
                    if s == 0:
                        wait_apart(pool, s_du, 16 * (p + 1), s_pace)
                    drives(p, s, 0)
                    drives(p, s, 1)
                    if not last:
                        lo(j, (s + 1) % 2, 0)
                    drives(p, s, 2)
                    if not last:
                        lo(j, (s + 1) % 2, 1)
                    if s == STEPS - 1:
                        add(p, STATES - 1)

                every(pool, step)

            @block.vector
            def _(dve):
                def add(p, k, n, t):
                    q = p * PER_BATCH + k
                    if t == OWN:
                        return
                    dve.wait_ge(s_term, q + 1)
                    if n == 0:
                        dve.sem_inc(s_add, 1)
                    else:
                        dve.wait_ge(s_add, OWN * (p * STATES + n) + t + 1)
                        dve.tensor_tensor(y[t][:, :], y[t][:, :], drive[k % RING][:, :], ALU.add).then_inc(s_add, 1)

                def scan(p, s, part):
                    for k, n, t in scans(s, part):
                        q = p * PER_BATCH + k
                        d = drive[k % RING]
                        dve.wait_ge(s_decay, q + 1)
                        dve.wait_ge(s_drive, q + 1)
                        dve.tensor_tensor_scan(d[:, :], decay[k % RING][:, :], d[:, :], 0.0, ALU.mult,
                                               ALU.add).then_inc(s_scan, 1)
                        if k:
                            add(p, k - 1, (k - 1) // ET, (k - 1) % ET)
                        dve.wait_ge(s_scan, RING + q + 1)
                        if k % ET == 0:
                            dve.wait_ge(s_rows[n % 2], 32 * (p * STEPS + n // 2 + 1))
                        if n == 0:
                            dve.wait_ge(s_st[t], 16 * (p + 1))
                        dve.tensor_tensor((y[t] if n == 0 else d)[:, :], d[:, :], rows[n % 2][:, 1, :],
                                          ALU.mult).then_inc(s_term, 1)

                def hidden(j, ic):
                    dve.wait_ge(s_silu, IC * j + ic + 1)
                    dve.tensor_tensor(hid[ic][:, :], ps_u[ic][:, :], hid[ic][:, :], ALU.mult).then_inc(s_h, 1)

                def add_y(p, s, t):
                    dve.wait_ge(s_y, TB * (p * STEPS + s) + t + 1)
                    row = xs[:, s % B * TB + t, :]
                    dve.tensor_tensor(row, ps_y[t][:, :], row, ALU.add).then_inc(s_yadd, 1)

                dve.sem_inc(s_h, IC)
                dve.sem_inc(s_yadd, TB)
                dve.sem_inc(s_scan, RING)
                dve.sem_inc(s_add, OWN)
                for ic in range(IC):
                    hidden(0, ic)

                def step(p, s, last):
                    j = p * STEPS + s + 1
                    scan(p, s, 0)
                    if not last:
                        hidden(j, 0)
                    scan(p, s, 1)
                    if not last:
                        hidden(j, 1)
                    add_y(p, s, 0)
                    scan(p, s, 2)
                    for t in range(1, TB):
                        add_y(p, s, t)

                every(dve, step)
TILES = (2 * B * S + 16 * (P - 1) + 14) // P
WRING = 3


def stage_router(nc, xs, x, xT, Wr, bias, ident, iota, before, token, plan):
    N = B * TB
    EVEN = TILES + TILES % 2
    I32 = mybir.dt.int32
    with Scope(nc, "rou") as m:
        ident_sb = m.sb("ident", [P, P])
        iota_sb = m.sb("iota", [P, P])
        before_sb = m.sb("before", [P, P])
        ones = m.sb("ones", [P, P])
        token_sb = m.sb("token", [P, N])
        bias_sb = m.sb("bias", [P, EXPERTS])
        wr = m.sb("wr", [EXPERTS, DIM])
        wrT = m.sb("wrT", [P, 2, KD, EXPERTS], F32R)
        logits = m.sb("logits", [P, N, EXPERTS])
        top = m.sb("top", [P, N])
        ex = m.sb("ex", [P, N, EXPERTS])
        total = m.sb("total", [P, N])
        best = m.sb("best", [P, N, 8])
        where = m.sb("where", [P, N, 8], mybir.dt.uint32)
        wheref = m.sb("wheref", [P, N, 2])
        pick = m.sb("pick", [P, N])
        hot = [m.sb(f"hot{i}", [P, N, EXPERTS]) for i in range(2)]
        chosen = m.sb("chosen", [P, N, EXPERTS])
        pre = m.sb("pre", [P, N + 1, EXPERTS])
        count = m.sb("count", [P, EXPERTS], I32)
        tiles = m.sb("tiles", [P, EXPERTS])
        ends = m.sb("ends", [P, EXPERTS])
        first = m.sb("first", [P, EXPERTS])
        place = m.sb("place", [P, N, EXPERTS])
        mine = m.sb("mine", [P, N, EXPERTS])
        slotf = m.sb("slotf", [P, N, 2])
        part_i = m.sb("part_i", [P, 2, N, 2], I32)
        partf = m.sb("partf", [P, 2, N, 2])
        place_hot = [m.sb(f"place_hot{i}", [P, P], F32R) for i in range(4)]
        tile_hot = [m.sb(f"tile_hot{i}", [P, EVEN], F32R) for i in range(4)]
        over = m.sb("over", [P, TILES, EXPERTS])
        expertf = m.sb("expertf", [P, TILES])
        ps_t = m.ps("turn", [P, KD, EXPERTS])
        ps_l = m.ps("logits_ps", [P, N, EXPERTS])
        ps_c = m.ps("counts_ps", [P, N, EXPERTS])
        ps_r = m.ps("ranks_ps", [P, N, EXPERTS])
        ps_s = m.ps("source_ps", [P, EVEN])
        s_in = m.sem("in")
        s_t, s_whi, s_wlo, s_l = m.sem("turned"), m.sem("w_hi"), m.sem("w_lo"), m.sem("logits_done")
        s_st = m.sem("stored")
        s_sub, s_ex, s_dve = m.sem("shifted"), m.sem("exp_done"), m.sem("dve_steps")
        s_chosen, s_counts, s_hots, s_source = m.sem("chosen_done"), m.sem("counted"), m.sem("hots"), m.sem("sourced")

        def spread(a, k=EXPERTS):
            return a.rearrange("p (n a) -> p n a", a=1).to_broadcast([P, a.shape[1], k])

        def repeat(a, n=N):
            return a.rearrange("p (a n) -> p a n", a=1).to_broadcast([P, n, a.shape[1]])

        with m.block() as block:
            @block.sync
            def _(sp):
                sp.dma_start(ident_sb[:, :], ident).then_inc(s_in, 16)
                sp.dma_start(wr[:, :], Wr).then_inc(s_in, 16)
                sp.dma_start(bias_sb[:, :], bias.rearrange("(a n) -> a n", a=1).to_broadcast([P, EXPERTS])).then_inc(s_in, 16)
                sp.dma_start(iota_sb[:, :], iota).then_inc(s_in, 16)
                sp.dma_start(before_sb[:, :], before).then_inc(s_in, 16)
                sp.dma_start(token_sb[:, :], token).then_inc(s_in, 16)
                sp.dma_start(x.rearrange("(n p) d -> p n d", p=P), xs[:, :, :]).then_inc(s_st, 16)
                sp.wait_ge(s_st, 16)

            @block.tensor
            def _(pe):
                pe.wait_ge(s_in, 16 * 6)
                for k in range(KD):
                    tr = pe.transpose(ps_t[:, k, :], wr[:, k * P:(k + 1) * P], ident_sb[0:EXPERTS, 0:EXPERTS])
                tr.then_inc(s_t, 1)
                pe.wait_ge(s_wlo, 1)
                for b in range(B):
                    for t in range(TB):
                        rows = slice(t * P, (t + 1) * P)
                        for k in range(KD):
                            mm = split_product(pe, ps_l[:, b * TB + t, :], (xT[b][:, 0, k, rows], xT[b][:, 1, k, rows]),
                                               (wrT[:, 0, k, :], wrT[:, 1, k, :]), k == 0, k == KD - 1)
                mm.then_inc(s_l, 1)
                pe.wait_ge(s_chosen, 1)
                pe.matmul(ps_c[:, :, :], ones[:, :], chosen[:, :, :], start=True, stop=True)
                pe.matmul(ps_r[:, :, :], before_sb[:, :], chosen[:, :, :], start=True, stop=True).then_inc(s_counts, 1)
                for n in range(2 * N):
                    pe.wait_ge(s_hots, n + 1)
                    pe.matmul(ps_s[:, :], place_hot[n % 4][:, :], tile_hot[n % 4][:, :], start=(n == 0),
                              stop=(n == 2 * N - 1)).then_inc(s_source, 1)

            @block.scalar
            def _(act):
                act.wait_ge(s_t, 1)
                act.copy(wrT[:, 0, :, :], ps_t[:, :, :]).then_inc(s_whi, 1)
                act.wait_ge(s_sub, 1)
                act.activation(ex[:, :, :], logits[:, :, :], ACT.Exp).then_inc(s_ex, 1)

            @block.vector
            def _(dve):
                own = Steps(dve, s_dve)
                dve.wait_ge(s_whi, 1)
                dve.tensor_tensor(wrT[:, 1, :, :], ps_t[:, :, :], wrT[:, 0, :, :].bitcast(F32), ALU.subtract).then_inc(s_wlo, 1)
                own.mark(dve.memset(ones[:, :], 1.0))
                own.mark(dve.memset(pre[:, 0, :], 0.0))
                dve.wait_ge(s_l, 1)
                own.after(dve.tensor_tensor(logits[:, :, :], ps_l[:, :, :], repeat(bias_sb[:, :]), ALU.add))
                own.after(dve.tensor_reduce(top[:, :], logits[:, :, :], AX_X, ALU.max))
                dve.tensor_tensor(logits[:, :, :], logits[:, :, :], spread(top[:, :]), ALU.subtract).then_inc(s_sub, 1)
                dve.wait_ge(s_ex, 1)
                own.after(dve.tensor_reduce(total[:, :], ex[:, :, :], AX_X, ALU.add))
                own.after(dve.reciprocal(total[:, :], total[:, :]))
                own.after(dve.tensor_tensor(ex[:, :, :], ex[:, :, :], spread(total[:, :]), ALU.mult))
                for n in range(N):
                    own.mark(dve.max(best[:, n, :], ex[:, n, :]))
                own.wait()
                for n in range(N):
                    own.mark(dve.max_index(where[:, n, :], best[:, n, :], ex[:, n, :]))
                own.wait()
                own.mark(dve.tensor_copy(wheref[:, :, :], where[:, :, 0:2]))
                own.after(dve.tensor_tensor(pick[:, :], best[:, :, 0], best[:, :, 1], ALU.add))
                own.after(dve.tensor_scalar(pick[:, :], pick[:, :], 1e-9, None, ALU.add))
                own.after(dve.reciprocal(pick[:, :], pick[:, :]))
                for j in range(2):
                    own.mark(dve.tensor_tensor(plan.weight[:, j, :], best[:, :, j], pick[:, :], ALU.mult))
                    own.mark(dve.tensor_tensor(hot[j][:, :, :], repeat(iota_sb[:, 0:EXPERTS]), spread(wheref[:, :, j]),
                                               ALU.is_equal))
                own.wait()
                dve.tensor_tensor(chosen[:, :, :], hot[0][:, :, :], hot[1][:, :, :], ALU.add).then_inc(s_chosen, 1)
                dve.wait_ge(s_counts, 1)
                for n in range(N):
                    own.after(dve.tensor_tensor(pre[:, n + 1, :], pre[:, n, :], ps_c[:, n, :], ALU.add))
                own.after(dve.tensor_scalar(count[:, :], pre[:, N, :], float(P - 1), None, ALU.add))
                own.after(dve.tensor_scalar(count[:, :], count[:, :], 7, None, ALU.logical_shift_right))
                own.after(dve.tensor_copy(tiles[:, :], count[:, :]))
                own.after(dve.tensor_scalar(tiles[:, :], tiles[:, :], 1.0, None, ALU.max))
                own.after(dve.tensor_copy(ends[:, 0:1], tiles[:, 0:1]))
                for e in range(1, EXPERTS):
                    own.after(dve.tensor_tensor(ends[:, e:e + 1], ends[:, e - 1:e], tiles[:, e:e + 1], ALU.add))
                own.mark(dve.tensor_copy(plan.ends[:, :], ends[0:1, :]))
                own.after(dve.tensor_tensor(first[:, :], ends[:, :], tiles[:, :], ALU.subtract))
                own.after(dve.tensor_scalar(first[:, :], first[:, :], float(P), None, ALU.mult))
                own.after(dve.tensor_tensor(place[:, :, :], pre[:, 0:N, :], ps_r[:, :, :], ALU.add))
                own.after(dve.tensor_tensor(place[:, :, :], place[:, :, :], repeat(first[:, :]), ALU.add))
                for j in range(2):
                    own.after(dve.tensor_tensor(mine[:, :, :], place[:, :, :], hot[j][:, :, :], ALU.mult))
                    own.after(dve.tensor_reduce(slotf[:, :, j], mine[:, :, :], AX_X, ALU.add))
                own.after(dve.tensor_copy(plan.slot[:, :, :], slotf[:, :, :]))
                own.mark(dve.tensor_scalar(part_i[:, 0, :, :], plan.slot[:, :, :].bitcast(I32), 7, None,
                                           ALU.logical_shift_right))
                own.after(dve.tensor_scalar(part_i[:, 1, :, :], plan.slot[:, :, :].bitcast(I32), P - 1, None,
                                            ALU.bitwise_and))
                own.after(dve.tensor_copy(partf[:, :, :, :], part_i[:, :, :, :]))
                for i in range(2 * N):
                    n, j = divmod(i, 2)
                    if i >= 4:
                        dve.wait_ge(s_source, i - 3)
                    own.mark(dve.tensor_scalar(place_hot[i % 4][:, :], iota_sb[:, :], partf[:, 1, n, j:j + 1], None,
                                               ALU.is_equal))
                    dve.tensor_scalar(tile_hot[i % 4][:, :], iota_sb[:, 0:EVEN], partf[:, 0, n, j:j + 1],
                                      token_sb[:, n:n + 1], ALU.is_equal, ALU.mult).then_inc(s_hots, 1)
                own.after(dve.tensor_tensor(over[:, :, :], repeat(ends[:, :], TILES), spread(iota_sb[:, 0:TILES]),
                                            ALU.is_le))
                own.after(dve.tensor_reduce(expertf[:, :], over[:, :, :], AX_X, ALU.add))
                own.after(dve.tensor_scalar(plan.expert[:, :], expertf[0:1, :], float(EXPERTS - 1), None, ALU.min))
                dve.wait_ge(s_source, 2 * N)
                own.after(dve.tensor_copy(plan.source[:, :], ps_s[:, 0:TILES]))


class Plan:

    def __init__(self, m):
        self.weight = m.sb("weight", [P, 2, B * TB])
        self.slot = m.sb("slot", [P, B * TB, 2], mybir.dt.uint32)
        self.source = m.sb("source", [P, TILES], mybir.dt.uint32)
        self.expert = m.sb("expert", [1, TILES], mybir.dt.int32)
        self.ends = m.sb("ends", [1, EXPERTS], mybir.dt.int32)


def stage_experts(nc, xn, y, Wg, Wu, Wd, ident, plan):
    INNER = Wg.shape[2]
    IC = INNER // P
    N_IN = KD * 2 * INNER
    N_ALL = N_IN + IC * DIM
    GROUPS = [4, 4] + [8] * 4 + [7]
    assert sum(GROUPS) == TILES
    with Scope(nc, "exp") as m:
        ident_sb = m.sb("ident", [P, P])
        rows = m.sb("rows", [P, TILES, DIM])
        raw = [m.sb(f"raw{i}", [P, N_IN]) for i in range(2)]
        raw_d = m.sb("raw_down", [P, IC * DIM])
        w = m.sb("w", [P, WRING, 2, N_ALL], F32R)
        row = [m.sb(f"row{i}", [P, DIM]) for i in range(2)]
        xT = [m.sb(f"xT{i}", [P, 2, KD, P], F32R) for i in range(2)]
        hid = [m.sb(f"hid{i}", [P, INNER]) for i in range(2)]
        hT = [m.sb(f"hT{i}", [P, 2, IC, P], F32R) for i in range(2)]
        yout = m.sb("y", [P, DIM])
        ps_x = [m.ps(f"x{i}", [P, KD, P]) for i in range(2)]
        ps_g = [m.ps(f"g{i}", [P, 2, INNER]) for i in range(2)]
        ps_h = [m.ps(f"h{i}", [P, IC, P]) for i in range(2)]
        ps_y = [m.ps(f"y_ps{i}", [P, DIM]) for i in range(2)]
        s_id = m.sem("ident_in")
        s_raw, s_rawd = [m.sem(f"raw_in{i}") for i in range(2)], m.sem("raw_down_in")
        s_gather = [m.sem(f"gathered{g}") for g in range(len(GROUPS))]
        s_rows = m.sem("rows_in")
        s_hi = m.sem("w_hi")
        s_split = m.sem("first_w_hi")
        s_wpart, s_w = m.sem("gate_up_split"), m.sem("w_split")
        s_row = m.sem("row_copied")
        s_xt, s_xhi, s_xlo = m.sem("x_turned"), m.sem("x_hi"), m.sem("x_lo")
        s_g, s_silu, s_h = m.sem("gate_up"), m.sem("silu_done"), m.sem("hidden")
        s_ht, s_hhi, s_hlo = m.sem("h_turned"), m.sem("h_hi"), m.sem("h_lo")
        s_y, s_yout = m.sem("y_made"), m.sem("y_copied")
        s_st = m.sem("stored")
        s_pace = m.sem("pace")

        def pieces(e):
            return ((raw[e % 2], slice(0, N_IN), s_raw[e % 2], 32 * (e // 2 + 1)),
                    (raw_d, slice(N_IN, N_ALL), s_rawd, 16 * (e + 1)))

        def part(par, hl, at, n):
            return w[:, par, hl, at:at + n]

        def tiles(eng, step):
            step(0, 0)
            pairs = (TILES - 3) // 2
            with eng.Fori(0, pairs) as pair:
                step(pair * 2 + 1, 1)
                step(pair * 2 + 2, 0)
            for k in range(2 * pairs + 1, TILES + 1):
                step(k, k % 2)

        def known(k, test):
            return test(k) if isinstance(k, int) else True

        with m.block() as block:
            @block.sync
            def _(sp):
                sp.dma_start(ident_sb[:, :], ident).then_inc(s_id, 16)
                for e in range(EXPERTS):
                    if e >= 2:
                        sp.wait_ge(s_w, e - 1)
                    wi = raw[e % 2][:, 0:N_IN].rearrange("p (k g n) -> p k g n", k=KD, g=2)
                    for g, src in enumerate((Wg, Wu)):
                        sp.dma_start(wi[:, :, g, :], src[e].rearrange("(k p) n -> p k n", p=P)).then_inc(s_raw[e % 2], 16)
                    if e:
                        sp.wait_ge(s_w, e)
                    sp.dma_start(raw_d[:, :].rearrange("p (k n) -> p k n", k=IC),
                                 Wd[e].rearrange("(k p) n -> p k n", p=P)).then_inc(s_rawd, 16)

            @block.gpsimd
            def _(pool):
                k = 0
                for g, size in enumerate(GROUPS):
                    for _ in range(size):
                        pool.indirect_dma_start(rows[:, k, :], None, xn,
                                                bass.IndirectOffsetOnAxis(plan.source[:, k:k + 1], 0)
                                                ).then_inc(s_gather[g], 16)
                        k += 1
                    if g:
                        pool.wait_ge(s_gather[g - 1], 16 * GROUPS[g - 1])
                        pool.sem_inc(s_rows, GROUPS[g - 1])
                pool.wait_ge(s_gather[-1], 16 * GROUPS[-1])
                pool.sem_inc(s_rows, GROUPS[-1])
                for e in range(WRING, EXPERTS):
                    end = pool.value_load(plan.ends[0:1, e - WRING:e - WRING + 1], min_val=0, max_val=TILES)
                    wait_apart(pool, s_y, end + 2, s_pace)
                    pool.wait_ge(s_w, e)
                    for n, (src, cols, sem, value) in enumerate(pieces(e)):
                        pool.wait_ge(sem, value)
                        pool.tensor_scalar(w[:, e % WRING, 0, cols], src[:, :], 1.0, 1.0, ALU.mult,
                                           ALU.mult).then_inc(s_hi, 1)
                        pool.wait_ge(s_hi, 2 * (e - WRING) + n + 1)
                        pool.tensor_tensor(w[:, e % WRING, 1, cols], src[:, :], w[:, e % WRING, 0, cols].bitcast(F32),
                                           ALU.subtract).then_inc(s_w if n else s_wpart, 1)
                    pool.wait_ge(s_wpart, e + 1)

            @block.scalar
            def _(act):
                act.sem_inc(s_st, 16)
                act.sem_inc(s_yout, 2)

                def fetch(k, i):
                    act.wait_ge(s_rows, k + 1)
                    wait_apart(act, s_xt, k + 1, s_pace)
                    act.copy(row[i][:, :], rows[:, k, :]).then_inc(s_row, 1)

                def x_hi(k, i):
                    act.wait_ge(s_xt, k + 3)
                    act.wait_ge(s_g, k + 1)
                    act.copy(xT[i][:, 0, :, :], ps_x[i][:, :, :]).then_inc(s_xhi, 1)

                fetch(0, 0)
                fetch(1, 1)
                x_hi(0, 0)

                def step(k, i):
                    if known(k, lambda k: k >= 1):
                        act.wait_ge(s_ht, k + 2)
                        act.wait_ge(s_y, k)
                        act.copy(hT[1 - i][:, 0, :, :], ps_h[1 - i][:, :, :]).then_inc(s_hhi, 1)
                    if known(k, lambda k: k + 1 < TILES):
                        x_hi(k + 1, 1 - i)
                    if known(k, lambda k: k + 2 < TILES):
                        fetch(k + 2, i)
                    if known(k, lambda k: k < TILES):
                        act.wait_ge(s_g, k + 3)
                        act.wait_ge(s_ht, k + 1)
                        act.activation(hid[i][:, :], ps_g[i][:, 0, :], ACT.Silu).then_inc(s_silu, 1)
                    if known(k, lambda k: k >= 1):
                        act.wait_ge(s_y, k + 2)
                        wait_apart(act, s_st, 16 * k, s_pace)
                        act.copy(yout[:, :], ps_y[1 - i][:, :]).then_inc(s_yout, 1)
                        act.wait_ge(s_yout, k + 2)
                        act.dma_start(y[bass.ds((k - 1) * P, P), :], yout[:, :]).then_inc(s_st, 16)

                tiles(act, step)
                act.wait_ge(s_st, 16 * (TILES + 1))

            @block.vector
            def _(dve):
                dve.sem_inc(s_xlo, 2)
                dve.sem_inc(s_h, 2)
                dve.sem_inc(s_hlo, 2)
                for e in range(WRING):
                    for n, (src, cols, sem, value) in enumerate(pieces(e)):
                        dve.wait_ge(sem, value)
                        dve.tensor_copy(w[:, e, 0, cols], src[:, :]).then_inc(s_split, 1)
                        dve.wait_ge(s_split, 2 * e + n + 1)
                        dve.tensor_tensor(w[:, e, 1, cols], src[:, :], w[:, e, 0, cols].bitcast(F32),
                                          ALU.subtract).then_inc(s_w if n else s_wpart, 1)

                def x_lo(k, i):
                    dve.wait_ge(s_xhi, k + 1)
                    dve.tensor_tensor(xT[i][:, 1, :, :], ps_x[i][:, :, :], xT[i][:, 0, :, :].bitcast(F32),
                                      ALU.subtract).then_inc(s_xlo, 1)

                x_lo(0, 0)

                def step(k, i):
                    if known(k, lambda k: k >= 1):
                        dve.wait_ge(s_hhi, k)
                        dve.tensor_tensor(hT[1 - i][:, 1, :, :], ps_h[1 - i][:, :, :], hT[1 - i][:, 0, :, :].bitcast(F32),
                                          ALU.subtract).then_inc(s_hlo, 1)
                    if known(k, lambda k: k + 1 < TILES):
                        x_lo(k + 1, 1 - i)
                    if known(k, lambda k: k < TILES):
                        dve.wait_ge(s_silu, k + 1)
                        dve.tensor_tensor(hid[i][:, :], ps_g[i][:, 1, :], hid[i][:, :], ALU.mult).then_inc(s_h, 1)

                tiles(dve, step)

            @block.tensor
            def _(pe):
                for sem in (s_xt, s_g, s_ht, s_y):
                    pe.sem_inc(sem, 2)
                pe.wait_ge(s_id, 16)

                def turn_x(k, i):
                    pe.wait_ge(s_row, k + 1)
                    pe.wait_ge(s_xlo, k + 1)
                    for c in range(KD):
                        tr = pe.transpose(ps_x[i][:, c, :], row[i][:, c * P:(c + 1) * P], ident_sb[:, :])
                    tr.then_inc(s_xt, 1)

                def expert(k):
                    return pe.value_load(plan.expert[0:1, bass.ds(k, 1)], min_val=0, max_val=EXPERTS - 1)

                turn_x(0, 0)

                def step(k, i):
                    if known(k, lambda k: k < TILES):
                        now = expert(k)
                        wn = now % WRING
                    if known(k, lambda k: k >= 1):
                        wt = expert(k - 1) % WRING
                        pe.wait_ge(s_h, k + 2)
                        pe.wait_ge(s_hlo, k)
                        for c in range(IC):
                            tr = pe.transpose(ps_h[1 - i][:, c, :], hid[1 - i][:, c * P:(c + 1) * P], ident_sb[:, :])
                        tr.then_inc(s_ht, 1)
                    if known(k, lambda k: k + 1 < TILES):
                        turn_x(k + 1, 1 - i)
                    if known(k, lambda k: k < TILES):
                        pe.wait_ge(s_w, now + 1)
                        pe.wait_ge(s_xlo, k + 3)
                        pe.wait_ge(s_h, k + 1)
                        for c in range(KD):
                            at = c * 2 * INNER
                            mm = split_product(pe, ps_g[i][:, :, :], (xT[i][:, 0, c, :], xT[i][:, 1, c, :]),
                                               (part(wn, 0, at, 2 * INNER), part(wn, 1, at, 2 * INNER)),
                                               c == 0, c == KD - 1)
                        mm.then_inc(s_g, 1)
                    if known(k, lambda k: k >= 1):
                        pe.wait_ge(s_hlo, k + 2)
                        pe.wait_ge(s_yout, k)
                        for c in range(IC):
                            at = N_IN + c * DIM
                            mm = split_product(pe, ps_y[1 - i][:, :], (hT[1 - i][:, 0, c, :], hT[1 - i][:, 1, c, :]),
                                               (part(wt, 0, at, DIM), part(wt, 1, at, DIM)),
                                               c == 0, c == IC - 1)
                        mm.then_inc(s_y, 1)

                tiles(pe, step)


def stage_combine(nc, x, y, out, plan):
    outr = out.rearrange("(b t p) d -> b p t d", b=B, t=TB)
    with Scope(nc, "com") as m:
        acc = [m.sb(f"acc{b}", [P, TB, DIM]) for b in range(B)]
        picked = m.sb("picked", [P, B * TB, 2, DIM])
        s_acc = [m.sem(f"acc_in{b}") for b in range(B)]
        s_picked = [m.sem(f"picked{b}") for b in range(B)]
        s_first, s_sum, s_st = m.sem("first_added"), m.sem("summed"), m.sem("stored")
        with m.block() as block:
            @block.sync
            def _(sp):
                for b in range(B):
                    sp.dma_start(acc[b][:, :, :], x[b * S:(b + 1) * S, :].rearrange("(t p) d -> p t d", p=P)).then_inc(s_acc[b], 16)
                for b in range(B):
                    sp.wait_ge(s_sum, TB * (b + 1))
                    sp.dma_start(outr[b], acc[b][:, :, :]).then_inc(s_st, 16)
                sp.wait_ge(s_st, 16 * B)

            @block.gpsimd
            def _(pool):
                for b in range(B):
                    for n in range(b * TB, (b + 1) * TB):
                        for j in range(2):
                            pool.indirect_dma_start(picked[:, n, j, :], None, y,
                                                    bass.IndirectOffsetOnAxis(plan.slot[:, n, j:j + 1], 0)
                                                    ).then_inc(s_picked[b], 16)

            @block.vector
            def _(dve):
                for b in range(B):
                    dve.wait_ge(s_acc[b], 16)
                    dve.wait_ge(s_picked[b], 16 * 2 * TB)
                    for j, sem in enumerate((s_first, s_sum)):
                        if j:
                            dve.wait_ge(s_first, TB * (b + 1))
                        for t in range(TB):
                            n = b * TB + t
                            dve.scalar_tensor_tensor(acc[b][:, t, :], picked[:, n, j, :], plan.weight[:, j, n:n + 1],
                                                     acc[b][:, t, :], ALU.mult, ALU.add).then_inc(sem, 1)


def build(nc, x, ctx_1024, L0_xattn_Wq, L0_xattn_Wk, L0_xattn_Wv, L0_xattn_Wo, L0_xattn_gq, L0_xattn_gk,
          L0_ffn_SU_ug, L0_ffn_SU_dp, L0_ffn_Wscale_ug, L0_ffn_Wscale_dp, L0_ffn_W_up, L0_ffn_W_gate, L0_ffn_W_down,
          L1_xattn_in_proj_w, L1_xattn_conv_w, L1_xattn_conv_b, L1_xattn_x_proj_w, L1_xattn_dt_proj_w,
          L1_xattn_dt_proj_b, L1_xattn_A_log, L1_xattn_D, L1_ffn_Wr, L1_ffn_bias, L1_ffn_Wg, L1_ffn_Wu, L1_ffn_Wd,
          L1_ffn_sWg, L1_ffn_sWu, L1_ffn_sWd, ident, had, iota, before, token, out):
    def scratch(name, shape):
        return nc.dram_tensor(name, shape, F32).ap()

    x0 = x.rearrange("b s d -> (b s) d")
    result = out.rearrange("b s d -> (b s) d")
    normT = scratch("normT", (B, P, 2, KD, S))
    ctxT = scratch("ctxT", (B, P, 2, KC, S))
    ffnT = scratch("ffnT", (4, P, 2, 3 * KD * 512))
    u_d, delta_d, du_d, y_d = (scratch(n, (B, P, ET, S)) for n in ("u_d", "delta_d", "du_d", "y_d"))
    bc_d = scratch("bc_d", (B, 2 * STATES, S))
    xrows, mixed = scratch("xrows", (B * S, DIM)), scratch("mixed", (B * S, DIM))
    slots = scratch("slots", (TILES * P, DIM))

    decided = ExitStack()
    plan = Plan(decided.enter_context(Memory(nc, "plan")))
    with Memory(nc, "residual") as r:
        xs = r.sb("x", [P, B * TB, DIM])
        stage_norm(nc, "nrm0", xs, normT, ident, x0, ctx_1024, ctxT)
        stage_attention(nc, xs, normT, ctxT, L0_xattn_Wq, L0_xattn_Wk, L0_xattn_Wv, L0_xattn_Wo, L0_xattn_gq,
                        L0_xattn_gk, ident)

        stage_ssm_inputs(nc, ctxT, L1_xattn_in_proj_w, L1_xattn_conv_w, L1_xattn_conv_b, L1_xattn_x_proj_w,
                         L1_xattn_dt_proj_w, L1_xattn_dt_proj_b, u_d, delta_d, du_d, bc_d, ident)
        stage_ffn_weights(nc, ffnT, L0_ffn_W_gate, L0_ffn_W_up, L0_ffn_W_down, L0_ffn_Wscale_ug, L0_ffn_Wscale_dp,
                          L0_ffn_SU_dp, ident, had)
        with Memory(nc, "rotated") as k:
            rotT = [k.sb(f"b{b}", [P, 2, KD, S], F32R) for b in range(B)]
            with Memory(nc, "normed1") as n:
                normT1 = [n.sb(f"b{b}", [P, 2, KD, S], F32R) for b in range(B)]
                stage_norm(nc, "nrm1", xs, normT1, ident)
                stage_rotate(nc, normT1, rotT, L0_ffn_SU_ug, had)
            stage_ffn_scan(nc, xs, rotT, ffnT, L1_xattn_A_log, delta_d, du_d, bc_d, y_d)
        stage_ssm_gate(nc, xs, u_d, y_d, L1_xattn_D, ident)

        with Memory(nc, "normed2") as n:
            normT2 = [n.sb(f"b{b}", [P, 2, KD, S], F32R) for b in range(B)]
            stage_norm(nc, "nrm2", xs, normT2, ident, rowsout=xrows)
            stage_shared(nc, xs, normT2, L1_ffn_sWg, L1_ffn_sWu, L1_ffn_sWd)
            stage_router(nc, xs, mixed, normT2, L1_ffn_Wr, L1_ffn_bias, ident, iota, before, token, plan)

    stage_experts(nc, xrows, slots, L1_ffn_Wg, L1_ffn_Wu, L1_ffn_Wd, ident, plan)
    stage_combine(nc, mixed, slots, result, plan)
    decided.close()


def kernel(**inputs):
    import numpy as _np
    import concourse.bacc as _bacc
    from concourse import mybir as _mybir
    from concourse.bass_utils import run_bass_kernel_spmd as _run

    nc = _bacc.Bacc("TRN2", target_bir_lowering=False, num_devices=1)
    sylvester = _np.ones((1, 1), _np.float32)
    while len(sylvester) < P:
        sylvester = _np.block([[sylvester, sylvester], [sylvester, -sylvester]])
    constants = {
        "ident": _np.eye(P, dtype=_np.float32),
        "had": sylvester,
        "iota": _np.tile(_np.arange(P, dtype=_np.float32), (P, 1)),
        "before": _np.triu(_np.ones((P, P), _np.float32), 1),
        "token": _np.ascontiguousarray(_np.arange(B * S, dtype=_np.float32).reshape(B * TB, P).T),
    }
    arrays, args = {}, {}
    for name, a in {**inputs, **constants}.items():
        a = _np.ascontiguousarray(a)
        arrays[f"in_{name}"] = a
        args[name] = nc.dram_tensor(f"in_{name}", a.shape, _mybir.dt.from_np(a.dtype), kind="ExternalInput").ap()
    args["out"] = nc.dram_tensor("out_0", (B, S, DIM), F32, kind="ExternalOutput").ap()
    build(nc, **args)
    r = _run(nc, [arrays], core_ids=[0])
    return r.results[0]["out_0"]
```
